# Optimizing a Trainium2 kernel written in Bass

```python
import numpy as np
import jax
import jax.numpy as jnp

def _softmax(x, axis=-1):
    return jax.nn.softmax(x, axis=axis)

def _gelu(x):
    return jax.nn.gelu(x, approximate=True)

def _silu(x):
    return jax.nn.silu(x)

def _sigmoid(x):
    return jax.nn.sigmoid(x)

def _layernorm(x, axis=-1, eps=1e-05):
    m = jnp.mean(x, axis=axis, keepdims=True)
    v = jnp.var(x, axis=axis, keepdims=True)
    return (x - m) / jnp.sqrt(v + eps)

def _scatter_add(tgt, idx, src, axis=0):
    return tgt.at[idx].add(src)

def _segment_sum(src, seg, n):
    return jax.ops.segment_sum(src, seg, n)
kernel_name = 'mk_macaron_d1_jaxref_r8_086dac'

def setup_inputs(seed: int=0):
    np.random.seed(seed)
    _w = jnp.asarray

    def _L0_attn_setup():
        import math
        import jax, jax.numpy as jnp
        import numpy as np
        NHEAD = 16
        HEAD_DIM = 64
        D_MODEL = 128
        B, T = (2, 512)

        def _cosformer(x, Wq, bq, Wk, bk, Wv, bv, Wo, bo):
            Bsz, Tlen, _ = x.shape
            H, dh = (NHEAD, HEAD_DIM)
            Q = (x @ Wq + bq).reshape(Bsz, Tlen, H, dh)
            K = (x @ Wk + bk).reshape(Bsz, Tlen, H, dh)
            V = (x @ Wv + bv).reshape(Bsz, Tlen, H, dh)
            Qp = jax.nn.relu(Q)
            Kp = jax.nn.relu(K)
            angles = math.pi / (2.0 * Tlen) * jnp.arange(Tlen, dtype=jnp.float32)
            cosw = jnp.cos(angles)[None, :, None, None]
            sinw = jnp.sin(angles)[None, :, None, None]
            Qc, Qs = (Qp * cosw, Qp * sinw)
            Kc, Ks = (Kp * cosw, Kp * sinw)
            tm = lambda a: jnp.moveaxis(a, 1, 0)
            Qc, Qs, Kc, Ks, Vt = (tm(Qc), tm(Qs), tm(Kc), tm(Ks), tm(V))
            S0 = jnp.zeros((Bsz, H, dh, dh), dtype=x.dtype)
            z0 = jnp.zeros((Bsz, H, dh), dtype=x.dtype)

            def step(carry, inp):
                S_cos, S_sin, z_cos, z_sin = carry
                qc, qs, kc, ks_, v = inp
                S_cos = S_cos + kc[..., :, None] * v[..., None, :]
                S_sin = S_sin + ks_[..., :, None] * v[..., None, :]
                z_cos = z_cos + kc
                z_sin = z_sin + ks_
                num = jnp.einsum('bhi,bhij->bhj', qc, S_cos) + jnp.einsum('bhi,bhij->bhj', qs, S_sin)
                den = jnp.sum(qc * z_cos + qs * z_sin, axis=-1)
                den = jnp.maximum(den, 1e-06)[..., None]
                return ((S_cos, S_sin, z_cos, z_sin), num / den)
            _, out = jax.lax.scan(step, (S0, S0, z0, z0), (Qc, Qs, Kc, Ks, Vt))
            out = jnp.moveaxis(out, 0, 1).reshape(Bsz, Tlen, H * dh)
            return out @ Wo + bo
        key = jax.random.key(seed)
        ks = jax.random.split(key, 9)
        HD = NHEAD * HEAD_DIM
        s_in = 1.0 / math.sqrt(D_MODEL)
        s_out = 1.0 / math.sqrt(HD)
        return {'x': jax.random.normal(ks[0], (B, T, D_MODEL), dtype=jnp.float32), 'Wq': jax.random.normal(ks[1], (D_MODEL, HD), dtype=jnp.float32) * s_in, 'bq': jnp.zeros((HD,), dtype=jnp.float32), 'Wk': jax.random.normal(ks[2], (D_MODEL, HD), dtype=jnp.float32) * s_in, 'bk': jnp.zeros((HD,), dtype=jnp.float32), 'Wv': jax.random.normal(ks[3], (D_MODEL, HD), dtype=jnp.float32) * s_in, 'bv': jnp.zeros((HD,), dtype=jnp.float32), 'Wo': jax.random.normal(ks[4], (HD, D_MODEL), dtype=jnp.float32) * s_out, 'bo': jnp.zeros((D_MODEL,), dtype=jnp.float32)}
    _L0_attn_in = _L0_attn_setup()

    def _L0_ffn_setup():
        import jax, jax.numpy as jnp
        import numpy as np
        B, S, H, E, K, I = (4, 256, 128, 8, 2, 512)
        GATE_EPS = 1e-06
        LN_EPS = 1e-05
        key = jax.random.key(seed)
        k0, k1, k2, k3 = jax.random.split(key, 4)
        x = jax.random.normal(k0, (B, S, H), jnp.float32)
        gate_w = jax.random.normal(k1, (E, H), jnp.float32) * np.float32(np.sqrt(2.0 / (H + E)))
        expert_bias = jnp.zeros((E,), jnp.float32)
        w_up = jax.random.normal(k2, (E, I, H), jnp.float32) * np.float32(np.sqrt(2.0 / (H + I)))
        w_down = jax.random.normal(k3, (E, H, I), jnp.float32) * np.float32(np.sqrt(2.0 / (H + I)))
        return {'x': x, 'gate_w': gate_w, 'expert_bias': expert_bias, 'w_up': w_up, 'w_down': w_down}
    _L0_ffn_in = _L0_ffn_setup()
    _d = {'L0_attn_x': _L0_attn_in['x'], 'L0_attn_Wq': _L0_attn_in['Wq'], 'L0_attn_bq': _L0_attn_in['bq'], 'L0_attn_Wk': _L0_attn_in['Wk'], 'L0_attn_bk': _L0_attn_in['bk'], 'L0_attn_Wv': _L0_attn_in['Wv'], 'L0_attn_bv': _L0_attn_in['bv'], 'L0_attn_Wo': _L0_attn_in['Wo'], 'L0_attn_bo': _L0_attn_in['bo'], 'L0_ffn_gate_w': _L0_ffn_in['gate_w'], 'L0_ffn_expert_bias': _L0_ffn_in['expert_bias'], 'L0_ffn_w_up': _L0_ffn_in['w_up'], 'L0_ffn_w_down': _L0_ffn_in['w_down']}
    _x0 = _d['L0_attn_x']
    _d['L0_attn_x'] = jax.random.normal(jax.random.fold_in(jax.random.key(seed), 1), (4, 1024, 128), dtype=_x0.dtype)
    del _x0
    return _d

def reference(L0_attn_x, L0_attn_Wq, L0_attn_bq, L0_attn_Wk, L0_attn_bk, L0_attn_Wv, L0_attn_bv, L0_attn_Wo, L0_attn_bo, L0_ffn_gate_w, L0_ffn_expert_bias, L0_ffn_w_up, L0_ffn_w_down):

    def _L0_attn_ref(x, Wq, bq, Wk, bk, Wv, bv, Wo, bo):
        import math
        import jax, jax.numpy as jnp
        import numpy as np
        NHEAD = 16
        HEAD_DIM = 64
        D_MODEL = 128
        B, T = (2, 512)

        def _cosformer(x, Wq, bq, Wk, bk, Wv, bv, Wo, bo):
            Bsz, Tlen, _ = x.shape
            H, dh = (NHEAD, HEAD_DIM)
            Q = (x @ Wq + bq).reshape(Bsz, Tlen, H, dh)
            K = (x @ Wk + bk).reshape(Bsz, Tlen, H, dh)
            V = (x @ Wv + bv).reshape(Bsz, Tlen, H, dh)
            Qp = jax.nn.relu(Q)
            Kp = jax.nn.relu(K)
            angles = math.pi / (2.0 * Tlen) * jnp.arange(Tlen, dtype=jnp.float32)
            cosw = jnp.cos(angles)[None, :, None, None]
            sinw = jnp.sin(angles)[None, :, None, None]
            Qc, Qs = (Qp * cosw, Qp * sinw)
            Kc, Ks = (Kp * cosw, Kp * sinw)
            tm = lambda a: jnp.moveaxis(a, 1, 0)
            Qc, Qs, Kc, Ks, Vt = (tm(Qc), tm(Qs), tm(Kc), tm(Ks), tm(V))
            S0 = jnp.zeros((Bsz, H, dh, dh), dtype=x.dtype)
            z0 = jnp.zeros((Bsz, H, dh), dtype=x.dtype)

            def step(carry, inp):
                S_cos, S_sin, z_cos, z_sin = carry
                qc, qs, kc, ks_, v = inp
                S_cos = S_cos + kc[..., :, None] * v[..., None, :]
                S_sin = S_sin + ks_[..., :, None] * v[..., None, :]
                z_cos = z_cos + kc
                z_sin = z_sin + ks_
                num = jnp.einsum('bhi,bhij->bhj', qc, S_cos) + jnp.einsum('bhi,bhij->bhj', qs, S_sin)
                den = jnp.sum(qc * z_cos + qs * z_sin, axis=-1)
                den = jnp.maximum(den, 1e-06)[..., None]
                return ((S_cos, S_sin, z_cos, z_sin), num / den)
            _, out = jax.lax.scan(step, (S0, S0, z0, z0), (Qc, Qs, Kc, Ks, Vt))
            out = jnp.moveaxis(out, 0, 1).reshape(Bsz, Tlen, H * dh)
            return out @ Wo + bo
        return _cosformer(x, Wq, bq, Wk, bk, Wv, bv, Wo, bo)

    def _L0_ffn_ref(x, gate_w, expert_bias, w_up, w_down):
        import jax, jax.numpy as jnp
        import numpy as np
        B, S, H, E, K, I = (4, 256, 128, 8, 2, 512)
        GATE_EPS = 1e-06
        LN_EPS = 1e-05
        logits = jnp.einsum('bsh,eh->bse', x, gate_w) + expert_bias
        weights = jax.nn.softmax(logits, axis=-1)
        top_w, top_i = jax.lax.top_k(weights, K)
        top_w = top_w / (jnp.sum(top_w, axis=-1, keepdims=True) + GATE_EPS)
        sparse_w = jnp.sum(jax.nn.one_hot(top_i, E, dtype=weights.dtype) * top_w[..., None], axis=-2)
        out = jnp.zeros_like(x)
        for e in range(E):
            h = jax.nn.gelu(jnp.einsum('bsh,ih->bsi', x, w_up[e]), approximate=False)
            y = jnp.einsum('bsi,hi->bsh', h, w_down[e])
            out = out + sparse_w[..., e:e + 1] * y
        mu = jnp.mean(out, axis=-1, keepdims=True)
        var = jnp.mean(jnp.square(out - mu), axis=-1, keepdims=True)
        out = (out - mu) * jax.lax.rsqrt(var + LN_EPS)
        return out + x
    x = L0_attn_x
    x = x + 0.5 * _L0_ffn_ref(_layernorm(x, axis=-1), L0_ffn_gate_w, L0_ffn_expert_bias, L0_ffn_w_up, L0_ffn_w_down)
    x = x + _L0_attn_ref(_layernorm(x, axis=-1), L0_attn_Wq, L0_attn_bq, L0_attn_Wk, L0_attn_bk, L0_attn_Wv, L0_attn_bv, L0_attn_Wo, L0_attn_bo)
    x = x + 0.5 * _L0_ffn_ref(_layernorm(x, axis=-1), L0_ffn_gate_w, L0_ffn_expert_bias, L0_ffn_w_up, L0_ffn_w_down)
    return x

_drawn_inputs = setup_inputs


def setup_inputs(seed=0):
    import zlib

    import numpy as np

    out = dict(_drawn_inputs(seed))
    spreads = {'L0_attn_bq': (0.0, 0.1),
     'L0_attn_bk': (0.0, 0.1),
     'L0_attn_bv': (0.0, 0.1),
     'L0_attn_bo': (0.0, 0.1),
     'L0_ffn_expert_bias': (0.0, 0.1)}
    factors = {}
    for name, (base, spread) in spreads.items():
        noise = np.random.default_rng([zlib.crc32(name.encode()), seed]).standard_normal(out[name].shape)
        drawn = base * np.exp(spread * noise) if base else spread * noise
        out[name] = jnp.asarray(drawn.astype(out[name].dtype))
    for name, factor in factors.items():
        out[name] = (out[name] * factor).astype(out[name].dtype)
    return out
```

```python
from contextlib import ExitStack

import numpy as np

import concourse.bass as bass
from concourse import mybir

P = 128
B, T, D = 4, 1024, 128
NTOK = B * T
NTILE = NTOK // P
TPB = 4
BLK = TPB * P
NBLK = NTOK // BLK
E, I, TOPK = 8, 512, 2
CH = I // P
PAIR = 2
NP = CH // PAIR
NPB = E * NP
H, DH = 16, 64
HD = H * DH
NHP = HD // P
VZ = DH + 1
UPB = T // BLK
LN_EPS, GATE_EPS, DEN_EPS = 1e-5, 1e-6, 1e-6
SPLIT3 = 3

F32, F16, BF16 = mybir.dt.float32, mybir.dt.float16, mybir.dt.bfloat16
I32, U32 = mybir.dt.int32, mybir.dt.uint32
ALU = mybir.AluOpType
ACT = mybir.ActivationFunctionType
AX_X = mybir.AxisListType.X
RMAX = bass.bass_isa.ReduceOp.max

XSCALE = 4096.0
W_UP, W_DOWN, W_QKV, W_OUT = range(4)


def constants():
    f = np.float32
    angle = (f(np.pi / (2.0 * T)) * np.arange(T, dtype=f)).astype(f)
    cos, sin = np.cos(angle).astype(f), np.sin(angle).astype(f)
    trig_rows = np.concatenate([np.tile(cos, (DH, 1)), np.tile(sin, (DH, 1))], 0)
    trig_cols = np.stack([cos.reshape(-1, P).T, sin.reshape(-1, P).T], 1).astype(f)
    trig_cols = np.repeat(trig_cols[:, :, :, None], 2, 3)
    i, j = np.arange(P)[None, :], np.arange(P)[:, None]
    decay = np.where(j <= i, np.cos(np.pi / (2.0 * T) * (i - j)), 0.0).astype(f)
    pick = np.zeros((P, E, P), f)
    for e in range(E):
        for part in range(SPLIT3):
            pick[part * E + e, e] = 1.0
    return {
        "c_trig_rows": trig_rows,
        "c_trig_cols": trig_cols,
        "c_decay": decay,
        "c_ident": np.eye(P, dtype=f),
        "c_pick": pick.reshape(P, E * P),
        "c_rank": np.tile(np.arange(E, 0, -1, dtype=f), (P, 1)),
    }


def at_least(eng, sem, value):
    if isinstance(value, int) and value <= 0:
        return
    eng.wait_ge(sem, value)


def build(nc, d):
    with ExitStack() as ctx:
        def sb(name, shape, dt=F32):
            return ctx.enter_context(nc.sbuf_tensor(name, shape, dt))

        def sem(name):
            return ctx.enter_context(nc.semaphore(name))

        x_tok = sb("x_tok", [P, NTILE, D])
        xnh = sb("xnh", [P, NTILE, D])
        xT_hi = sb("xT_hi", [P, NTOK], F16)
        xT_lo = sb("xT_lo", [P, NTOK], F16)
        wup_hi, wup_lo = sb("wup_hi", [P, E * I], F16), sb("wup_lo", [P, E * I], F16)
        wdn_hi, wdn_lo = sb("wdn_hi", [P, E * CH, D], F16), sb("wdn_lo", [P, E * CH, D], F16)
        wq_hi, wq_lo = sb("wq_hi", [P, H, 2, DH], F16), sb("wq_lo", [P, H, 2, DH], F16)
        wk_hi, wk_lo = sb("wk_hi", [P, HD], F16), sb("wk_lo", [P, HD], F16)
        wv_hi, wv_lo = sb("wv_hi", [P, HD], F16), sb("wv_lo", [P, HD], F16)
        wo_hi, wo_lo = sb("wo_hi", [P, NHP, D], F16), sb("wo_lo", [P, NHP, D], F16)
        gate_sb = sb("gate_sb", [P, E])
        gbias = sb("gbias", [P, E])
        bq_sb = sb("bq_sb", [P, H])
        bkT_sb = sb("bkT_sb", [P, NHP])
        bk_row, bv_row, bo_row = sb("bk_row", [P, HD]), sb("bv_row", [P, HD]), sb("bo_row", [P, D])
        trig_rows = sb("trig_rows", [P, T])
        trig_cols = sb("trig_cols", [P, 2, 2 * T // P])
        decay = sb("decay", [P, P])
        ident = sb("ident", [P, P])
        ident_h = sb("ident_h", [P, P], F16)
        ident_b = sb("ident_b", [P, P], BF16)
        pick = sb("pick", [P, E, P], BF16)
        rank = sb("rank", [P, E])
        largest = sb("largest", [P, 5])
        largest_all = sb("largest_all", [P, 5])
        pow2 = sb("pow2", [P, 4])
        rpow2 = sb("rpow2", [P, 4])
        s_w = sb("s_w", [P, 4])
        s_pre = sb("s_pre", [P, 1])
        s_h = sb("s_h", [P, 1])
        s_y = sb("s_y", [P, 1])
        s_qkv = sb("s_qkv", [P, 1])
        s_o = sb("s_o", [P, 1])
        s_att = sb("s_att", [P, 1])
        s_tmp = sb("s_tmp", [P, 2])
        logits = sb("logits", [P, NTILE, E])
        gw = sb("gw", [P, NTILE, E])
        gt = sb("gt", [P, NTILE, E])
        gsel = sb("gsel", [P, NTILE, E])
        gcol = sb("gcol", [P, 6, NTILE])
        sw3 = sb("sw3", [P, NTILE, P], BF16)
        sw3T = sb("sw3T", [P, NTOK], BF16)
        st6 = sb("st6", [P, TPB, 6])
        mv = sb("mv", [P, TPB, 2])
        var4 = sb("var4", [P, TPB])
        rstdh = sb("rstdh", [P, TPB])
        fmv = sb("fmv", [P, TPB, 2])
        fst6 = sb("fst6", [P, TPB, 6])
        fvar4 = sb("fvar4", [P, TPB])
        frstdh = sb("frstdh", [P, TPB])
        minus_half = sb("minus_half", [P, TPB])
        xn_new = sb("xn_new", [P, TPB, D])
        xT32 = sb("xT32", [P, BLK])

        arena_a = sb("arena_a", [P, 4096])
        arena_b = sb("arena_b", [P, 4096])
        arena_c = sb("arena_c", [P, 6784])

        def carve(arena):
            at = [0]

            def take(n, dt=F32):
                words = n * mybir.dt.size(dt) // 4
                view = arena[:, at[0]:at[0] + words]
                at[0] += words
                assert at[0] <= arena.shape[1], at[0]
                return view if dt == F32 else view.bitcast(dt)
            return take

        take = carve(arena_c)
        h32 = [take(PAIR * BLK) for _ in range(2)]
        h_hi = [take(PAIR * BLK, F16) for _ in range(4)]
        h_lo = [take(PAIR * BLK, F16) for _ in range(4)]
        take = carve(arena_b)
        wb_sb = [take(BLK) for _ in range(2)]
        ytmp = [take(BLK) for _ in range(2)]
        acc = take(BLK)
        zt = take(BLK).rearrange("p (t d) -> p t d", t=TPB)

        take = carve(arena_b)
        q_relu = [take(BLK) for _ in range(2)]
        q_trig = [[take(BLK) for _ in range(2)] for _ in range(2)]
        k_relu = take(BLK)
        take = carve(arena_c)
        probs = [take(BLK) for _ in range(2)]
        k_tok = take(BLK).rearrange("p (c h f) -> p c h f", c=TPB, h=2)
        k_trig = take(TPB * 2 * P).rearrange("p (c h g f) -> p (c h) g f", c=TPB, h=2, g=2)
        v_one = take(TPB * 2 * VZ).rearrange("p (c h f) -> p c h f", c=TPB, h=2)
        o32 = take(BLK).rearrange("p (c h f) -> p c h f", c=TPB, h=2)
        o_hi, o_lo = take(BLK, F16), take(BLK, F16)
        oT = take(2 * BLK, F16)
        s_pref = [take(TPB * 2 * VZ).rearrange("p (c h f) -> p c h f", c=TPB, h=2) for _ in range(2)]
        s_run = take(NHP * 2 * VZ).rearrange("p (n h f) -> p n h f", n=NHP, h=2)
        den = take(2 * TPB).rearrange("p (h c) -> p h c", h=2)
        rden = take(2 * TPB).rearrange("p (h c) -> p h c", h=2)

        bank = [ctx.enter_context(nc.psum_tensor(f"bank{i}", [P, 2, BLK], F32)) for i in range(4)]
        ps_pre = [bank[0], bank[1]]
        ps_y = [bank[2][:, 0, :], bank[2][:, 1, :]]
        ps_wb = bank[3][:, 0, :]
        ps_tr = bank[3][:, 1, :]
        ps_so = bank[0]
        ps_st = bank[1]
        ps_pj = [bank[2][:, 0, :], bank[2][:, 1, :]]
        ps_op = bank[3][:, 0, :]

        in_x, in_up, in_dn, in_const, in_att = (sem(n) for n in ("in_x", "in_up", "in_dn", "in_const", "in_att"))
        out_done = sem("out_done")
        const_ready = sem("const_ready")
        max_part, max_all = sem("max_part"), sem("max_all")
        scale_step = sem("scale_step")
        split_hi = sem("split_hi")
        w_up_ready, w_dn_ready, w_att_ready = sem("w_up_ready"), sem("w_dn_ready"), sem("w_att_ready")
        arena_free = sem("arena_free")
        ln_step, ln_var, ln_rstd, ln_norm = (sem(n) for n in ("ln_step", "ln_var", "ln_rstd", "ln_norm"))
        ln_tr, ln_copied, ln_hi, ln_lo = (sem(n) for n in ("ln_tr", "ln_copied", "ln_hi", "ln_lo"))
        gate_mm, gate_read = sem("gate_mm"), sem("gate_read")
        gate_step, gate_exp, gate_in = sem("gate_step"), sem("gate_exp"), sem("gate_in")
        sw_split, sw_tr, sw_copied = sem("sw_split"), sem("sw_tr"), sem("sw_copied")

        def ffn_sems(k):
            names = ("up_done gelu_done hi_act hi_dve lo_done down_done wb_mm wb_copied y_used "
                     "acc_done acc_tr fin_st fin_ag fin_var fin_rstd fin_z fin_sum fin_x").split()
            return {n: sem(f"{n}{k}") for n in names}

        ffn = [ffn_sems(0), ffn_sems(1)]
        names = ("pq_done pkv_done q_evac kv_evac q_trig_done k_tok_done k_trig_done sc_done "
                 "probs_done st_done st_step s_ready o_done den_step o32_done o_hi_done o_lo_done otr_done "
                 "ot_copied op_done att_sum att_x s_zero").split()
        a = {n: sem(n) for n in names}

        passed = sem("passed")

        def wait_apart(eng, sem, value):
            eng.wait_ge(sem, value)
            eng.sem_inc(passed, 1)

        block = ctx.enter_context(nc.Block())

        def blk_cols(n):
            return bass.ds(n * BLK, BLK)

        def tile_of(t3, n, t):
            return t3[:, bass.ds(n * TPB + t, 1), :].rearrange("p a d -> p (a d)")

        def before(n):
            return nc.s_assert_within(n - 1, 0, NBLK - 2,
                                      skip_runtime_bounds_check_because="stands under If(n > 0)")

        def after(n):
            return nc.s_assert_within(n + 1, 1, NBLK - 1,
                                      skip_runtime_bounds_check_because="stands under If(n < NBLK - 1)")

        def gate_round(r):
            return 0 if r == 0 else NBLK

        def ln_stats(v, r, n):
            k = (r * NBLK + n) * 2
            for t in range(TPB):
                i = nc.vector.bn_stats(st6[:, t, :], tile_of(x_tok, n, t))
            i.then_inc(ln_step, 1)
            wait_apart(v, ln_step, k + 1)
            for t in range(TPB):
                i = nc.vector.bn_aggr(mv[:, t, :], st6[:, t, :])
            i.then_inc(ln_step, 1)
            v.wait_ge(ln_step, k + 2)
            nc.vector.tensor_scalar(var4[:], mv[:, :, 1], LN_EPS, 4.0, ALU.add, ALU.mult).then_inc(ln_var, 1)

        def ln_power(g, r, n):
            g.wait_ge(ln_var, r * NBLK + n + 1)
            nc.gpsimd.tensor_tensor(rstdh[:], var4[:], minus_half[:], ALU.pow).then_inc(ln_rstd, 1)

        def ln_apply(v, r, n):
            v.wait_ge(ln_rstd, r * NBLK + n + 1)
            v.wait_ge(ln_hi, r * NBLK + n)
            for t in range(TPB):
                i = nc.vector.tensor_scalar(xn_new[:, t, :], tile_of(x_tok, n, t), mv[:, t, 0:1], rstdh[:, t:t + 1],
                                            ALU.subtract, ALU.mult)
            i.then_inc(ln_norm, 1)

        def ln_transpose(pe, r, n):
            pe.wait_ge(ln_norm, r * NBLK + n + 1)
            for t in range(TPB):
                i = nc.tensor.transpose(ps_tr[:, t * P:(t + 1) * P], xn_new[:, t, :], ident[:])
            i.then_inc(ln_tr, 1)

        def ln_copy(act, r, n):
            act.wait_ge(ln_lo, r * NBLK + n)
            act.wait_ge(gate_mm, (n, NBLK, NBLK + n)[r])
            act.wait_ge(ln_tr, r * NBLK + n + 1)
            nc.scalar.activation(xT32[:], ps_tr, ACT.Copy).then_inc(ln_copied, 1)
            if r != 1:
                nc.scalar.activation(xnh[:, bass.ds(n * TPB, TPB), :], xn_new[:], ACT.Copy)
            nc.scalar.activation(xT_hi[:, blk_cols(n)], ps_tr, ACT.Copy, scale=XSCALE).then_inc(ln_hi, 1)

        def ln_low(v, r, n):
            v.wait_ge(ln_hi, r * NBLK + n + 1)
            nc.vector.scalar_tensor_tensor(xT_lo[:, blk_cols(n)], xT32[:], XSCALE, xT_hi[:, blk_cols(n)],
                                           ALU.mult, ALU.subtract).then_inc(ln_lo, 1)

        def gate_product(pe, r, n):
            pe.wait_ge(ln_hi, r * NBLK + n + 1)
            for t in range(TPB):
                i = nc.tensor.matmul(ps_tr[:, t * E:(t + 1) * E], xT32[:, t * P:(t + 1) * P], gate_sb[:],
                                     start=True, stop=True)
            i.then_inc(gate_mm, 1)

        def gate_logits(v, r, n):
            v.wait_ge(gate_mm, gate_round(r) + n + 1)
            nc.vector.scalar_tensor_tensor(
                logits[:, bass.ds(n * TPB, TPB), :], ps_tr[:, 0:TPB * E].rearrange("p (t e) -> p t e", t=TPB), 2.0,
                gbias[:].unsqueeze(1).to_broadcast([P, TPB, E]), ALU.mult, ALU.add).then_inc(gate_read, 1)

        def gating(v, k):
            base = k * 20
            step = [base]

            def then(ins):
                ins.then_inc(gate_step, 1)
                step[0] += 1
                v.wait_ge(gate_step, step[0])

            def wide(col):
                return gcol[:, col, :].unsqueeze(2).to_broadcast([P, NTILE, E])

            ranks = rank[:].unsqueeze(1).to_broadcast([P, NTILE, E])
            v.wait_ge(gate_read, NBLK * (k + 1))
            then(nc.vector.tensor_reduce(gcol[:, 0, :], logits[:], AX_X, ALU.max))
            nc.vector.tensor_tensor(gt[:], logits[:], wide(0), ALU.subtract).then_inc(gate_in, 1)
            v.wait_ge(gate_exp, k + 1)
            then(nc.vector.tensor_reduce(gcol[:, 0, :], gw[:], AX_X, ALU.add))
            then(nc.vector.reciprocal(gcol[:, 1, :], gcol[:, 0, :]))
            then(nc.vector.tensor_tensor(gw[:], gw[:], wide(1), ALU.mult))
            then(nc.vector.tensor_reduce(gcol[:, 2, :], gw[:], AX_X, ALU.max))
            then(nc.vector.tensor_tensor(gt[:], gw[:], wide(2), ALU.is_equal))
            then(nc.vector.tensor_tensor(gt[:], gt[:], ranks, ALU.mult))
            then(nc.vector.tensor_reduce(gcol[:, 3, :], gt[:], AX_X, ALU.max))
            then(nc.vector.tensor_tensor(gsel[:], gt[:], wide(3), ALU.is_equal))
            then(nc.vector.scalar_tensor_tensor(gt[:], gsel[:], -2.0, gw[:], ALU.mult, ALU.add))
            then(nc.vector.tensor_reduce(gcol[:, 4, :], gt[:], AX_X, ALU.max))
            then(nc.vector.tensor_tensor(gt[:], gt[:], wide(4), ALU.is_equal))
            then(nc.vector.tensor_tensor(gt[:], gt[:], ranks, ALU.mult))
            then(nc.vector.tensor_reduce(gcol[:, 3, :], gt[:], AX_X, ALU.max))
            then(nc.vector.tensor_tensor(gt[:], gt[:], wide(3), ALU.is_equal))
            then(nc.vector.tensor_tensor(gsel[:], gsel[:], gt[:], ALU.add))
            then(nc.vector.scalar_tensor_tensor(gcol[:, 5, :], gcol[:, 2, :], GATE_EPS, gcol[:, 4, :],
                                                ALU.add, ALU.add))
            then(nc.vector.reciprocal(gcol[:, 5, :], gcol[:, 5, :]))
            then(nc.vector.tensor_tensor(gsel[:], gsel[:], gw[:], ALU.mult))
            then(nc.vector.tensor_tensor(gsel[:], gsel[:], wide(5), ALU.mult))
            assert step[0] == base + 20, step[0] - base
            for part in range(SPLIT3):
                dst = sw3[:, :, part * E:(part + 1) * E]
                nc.vector.tensor_copy(dst, gsel[:]).then_inc(sw_split, 1)
                v.wait_ge(sw_split, k * 2 * SPLIT3 + 2 * part + 1)
                nc.vector.tensor_tensor(gsel[:], gsel[:], dst, ALU.subtract).then_inc(sw_split, 1)
                v.wait_ge(sw_split, k * 2 * SPLIT3 + 2 * part + 2)

        def gating_exp(act, k):
            act.wait_ge(gate_in, k + 1)
            nc.scalar.activation(gw[:], gt[:], ACT.Exp).then_inc(gate_exp, 1)

        def gating_transpose(pe, k):
            pe.wait_ge(sw_split, (k + 1) * 2 * SPLIT3)
            for q in range(NTILE // 8):
                at_least(pe, sw_copied, k * 4 + q)
                if k and not q:
                    pe.wait_ge(a["att_sum"], NBLK)
                for t in range(8):
                    i = nc.tensor.transpose(ps_wb.bitcast(BF16)[:, t * P:(t + 1) * P], sw3[:, q * 8 + t, :], ident_b[:])
                i.then_inc(sw_tr, 1)

        def gating_copy(act, k):
            for q in range(NTILE // 8):
                act.wait_ge(sw_tr, k * 4 + q + 1)
                nc.scalar.activation(sw3T[:, q * 8 * P:(q + 1) * 8 * P], ps_wb.bitcast(BF16), ACT.Copy).then_inc(sw_copied, 1)

        LAG = 3

        def up(pe, S, n, m):
            for c in range(PAIR):
                cols = slice((m * PAIR + c) * P, (m * PAIR + c + 1) * P)
                dst = ps_pre[m % 2][:, c, :]
                nc.tensor.matmul(dst, wup_hi[:, cols], xT_hi[:, blk_cols(n)], start=True, stop=False)
                nc.tensor.matmul(dst, wup_hi[:, cols], xT_lo[:, blk_cols(n)], start=False, stop=False)
                i = nc.tensor.matmul(dst, wup_lo[:, cols], xT_hi[:, blk_cols(n)], start=False, stop=True)
            i.then_inc(S["up_done"], 1)

        def down(pe, S, m):
            e, q = divmod(m, NP)
            for c in range(PAIR):
                w = m * PAIR + c
                hi, lo = (h[m % 4][:, c * BLK:(c + 1) * BLK] for h in (h_hi, h_lo))
                first, last = (q == 0 and c == 0), (q == NP - 1 and c == PAIR - 1)
                nc.tensor.matmul(ps_y[e % 2], wdn_hi[:, w, :], hi, start=first, stop=False)
                nc.tensor.matmul(ps_y[e % 2], wdn_hi[:, w, :], lo, start=False, stop=False)
                i = nc.tensor.matmul(ps_y[e % 2], wdn_lo[:, w, :], hi, start=False, stop=last)
            i.then_inc(S["down_done"], 1)

        def ffn_pe(pe, k):
            S = ffn[k]
            r = 2 * k
            pe.wait_ge(w_up_ready, 1)
            pe.wait_ge(ln_lo, r * NBLK + 1)
            for m in range(LAG):
                if m > 1:
                    pe.wait_ge(S["gelu_done"], m - 1)
                up(pe, S, 0, m)
            gating_transpose(pe, k)
            if k == 0:
                pe.wait_ge(w_dn_ready, 1)

            def finish_transpose(p):
                pe.wait_ge(S["acc_done"], (E - 1) * p + E - 1)
                if k == 0:
                    pe.wait_ge(ln_hi, NBLK + p)
                for t in range(TPB):
                    i = nc.tensor.transpose(ps_tr[:, t * P:(t + 1) * P], acc[:, t * P:(t + 1) * P], ident[:])
                i.then_inc(S["acc_tr"], 1)

            with pe.Fori(0, NBLK) as n:
                for m in range(NPB):
                    e = m // NP
                    if m % NP == 0:
                        pe.wait_ge(S["y_used"], E * n + e)
                    pe.wait_ge(S["lo_done"], NPB * n + m + 1)
                    down(pe, S, m)
                    if m < NPB - LAG:
                        pe.wait_ge(S["gelu_done"], NPB * n + m + LAG - 1)
                        up(pe, S, n, m + LAG)
                    else:
                        with pe.If(n < NBLK - 1):
                            pe.wait_ge(S["gelu_done"], NPB * n + m + LAG - 1)
                            if m == NPB - LAG:
                                pe.wait_ge(ln_lo, r * NBLK + n + 2)
                            up(pe, S, after(n), m + LAG - NPB)
                    if m % NP == 0:
                        pe.wait_ge(S["wb_copied"], E * n + e)
                        pe.wait_ge(sw_copied, 4 * (k + 1))
                        nc.tensor.matmul(ps_wb, pick[:, e, :], sw3T[:, blk_cols(n)], start=True, stop=True
                                         ).then_inc(S["wb_mm"], 1)
                    if m == 1:
                        with pe.If(n > 0):
                            finish_transpose(before(n))
                    if m == 11 and k == 0:
                        with pe.If(n > 0):
                            pe.wait_ge(S["fin_z"], n)
                            ln_transpose(pe, 1, before(n))
            finish_transpose(NBLK - 1)
            if k == 0:
                pe.wait_ge(S["fin_z"], NBLK)
                ln_transpose(pe, 1, NBLK - 1)

        def ffn_act(act, k):
            S = ffn[k]

            def hidden(n, m):
                g = NPB * n + m
                act.wait_ge(S["up_done"], g + 1)
                at_least(act, S["lo_done"], g - 1)
                nc.scalar.activation(h32[m % 2], ps_pre[m % 2][:, :, :].rearrange("p c t -> p (c t)"), ACT.Gelu,
                                     scale=s_pre[:, 0:1]).then_inc(S["gelu_done"], 1)
                if m % 2 == 0:
                    act.wait_ge(S["gelu_done"], g + 1)
                    nc.scalar.activation(h_hi[m % 4], h32[m % 2], ACT.Copy, scale=s_h[:, 0:1]).then_inc(S["hi_act"], 1)

            for m in range(LAG):
                hidden(0, m)
            gating_exp(act, k)
            gating_copy(act, k)
            with act.Fori(0, NBLK) as n:
                for m in range(NPB):
                    if m < NPB - LAG:
                        hidden(n, m + LAG)
                    else:
                        with act.If(n < NBLK - 1):
                            hidden(n + 1, m + LAG - NPB)
                    if m % NP == 0:
                        e = m // NP
                        act.wait_ge(S["y_used"], E * n + e)
                        act.wait_ge(S["wb_mm"], E * n + e + 1)
                        nc.scalar.activation(wb_sb[e % 2], ps_wb, ACT.Copy, scale=s_y[:, 0:1]
                                             ).then_inc(S["wb_copied"], 1)
                    if m == 12 and k == 0:
                        with act.If(n > 0):
                            ln_copy(act, 1, before(n))
            if k == 0:
                ln_copy(act, 1, NBLK - 1)

        def ffn_dve(v, k):
            S = ffn[k]

            def split(n, m, credit=False):
                g = NPB * n + m
                src, hi, lo = h32[m % 2], h_hi[m % 4], h_lo[m % 4]
                if m % 2 == 0:
                    v.wait_ge(S["hi_act"], (NPB // 2) * n + m // 2 + 1)
                else:
                    v.wait_ge(S["gelu_done"], g + 1)
                    nc.vector.tensor_scalar(hi, src, s_h[:, 0:1], None, ALU.mult).then_inc(S["hi_dve"], 1)
                    v.wait_ge(S["hi_dve"], (NPB // 2) * n + m // 2 + 1)
                nc.vector.scalar_tensor_tensor(lo, src, s_h[:, 0:1], hi, ALU.mult, ALU.subtract
                                               ).then_inc(S["lo_done"], 1)

            def combine(n, e):
                v.wait_ge(S["wb_copied"], E * n + e + 1)
                if e == 0:
                    v.wait_ge(S["acc_tr"], n)
                    dst = acc
                else:
                    v.wait_ge(S["acc_done"], (E - 1) * n + max(e - 2, 0))
                    dst = ytmp[e % 2]
                v.wait_ge(S["down_done"], NPB * n + NP * (e + 1))
                nc.vector.tensor_tensor(dst, ps_y[e % 2], wb_sb[e % 2], ALU.mult).then_inc(S["y_used"], 1)

            def finish_stats(p):
                v.wait_ge(S["acc_tr"], p + 1)
                for t in range(TPB):
                    i = nc.vector.bn_stats(fst6[:, t, :], ps_tr[:, t * P:(t + 1) * P])
                i.then_inc(S["fin_st"], 1)
                wait_apart(v, S["fin_st"], p + 1)
                for t in range(TPB):
                    i = nc.vector.bn_aggr(fmv[:, t, :], fst6[:, t, :])
                i.then_inc(S["fin_ag"], 1)
                v.wait_ge(S["fin_ag"], p + 1)
                nc.vector.tensor_scalar(fvar4[:], fmv[:, :, 1], LN_EPS, 4.0, ALU.add, ALU.mult).then_inc(S["fin_var"], 1)

            def finish_apply(p):
                v.wait_ge(S["fin_rstd"], p + 1)
                for t in range(TPB):
                    i = nc.vector.tensor_scalar(zt[:, t, :], ps_tr[:, t * P:(t + 1) * P], fmv[:, t, 0:1],
                                                frstdh[:, t:t + 1], ALU.subtract, ALU.mult)
                i.then_inc(S["fin_z"], 1)

            for m in range(LAG):
                split(0, m)
            v.sem_inc(S["y_used"], 1)
            gating(v, k)
            if k == 0:
                setup_down(v)
            with v.Fori(0, NBLK) as n:
                for m in range(NPB):
                    if m % 2 == 1:
                        combine(n, m // NP)
                    if m < NPB - LAG:
                        split(n, m + LAG)
                    else:
                        with v.If(n < NBLK - 1):
                            split(n + 1, m + LAG - NPB)
                    if m == 2:
                        with v.If(n > 0):
                            finish_stats(before(n))
                    if m == 4:
                        with v.If(n > 0):
                            finish_apply(before(n))
                    if m == 7 and k == 0:
                        with v.If(n > 0):
                            p = before(n)
                            v.wait_ge(S["fin_x"], p + 1)
                            ln_stats(v, 1, p)
                    if m == 9 and k == 0:
                        with v.If(n > 0):
                            ln_apply(v, 1, before(n))
                    if m == 14 and k == 0:
                        with v.If(n > 0):
                            ln_low(v, 1, before(n))
            last = NBLK - 1
            finish_stats(last)
            finish_apply(last)
            if k == 0:
                v.wait_ge(S["fin_x"], NBLK)
                ln_stats(v, 1, last)
                ln_apply(v, 1, last)
                ln_low(v, 1, last)

        def ffn_pool(g, k):
            S = ffn[k]

            def add(n, e):
                g.wait_ge(S["y_used"], E * n + e + 2)
                if e > 1:
                    g.wait_ge(S["acc_done"], (E - 1) * n + e - 1)
                nc.gpsimd.tensor_tensor(acc, acc, ytmp[e % 2], ALU.add).then_inc(S["acc_done"], 1)

            def finish_power(p):
                g.wait_ge(S["fin_var"], p + 1)
                nc.gpsimd.tensor_tensor(frstdh[:], fvar4[:], minus_half[:], ALU.pow).then_inc(S["fin_rstd"], 1)

            def finish_sum(p):
                wait_apart(g, S["fin_z"], p + 1)
                tiles = bass.ds(p * TPB, TPB)
                nc.gpsimd.tensor_tensor(zt, zt, xnh[:, tiles, :], ALU.add).then_inc(S["fin_sum"], 1)
                wait_apart(g, S["fin_sum"], p + 1)
                nc.gpsimd.tensor_tensor(x_tok[:, tiles, :], x_tok[:, tiles, :], zt, ALU.add).then_inc(S["fin_x"], 1)

            with g.Fori(0, NBLK) as n:
                for e in range(E):
                    if e == 4 and k == 0:
                        with g.If(n > 0):
                            ln_power(g, 1, before(n))
                    if e:
                        add(n, e)
                    if e == 1:
                        with g.If(n > 0):
                            finish_power(before(n))
                    if e == 2:
                        with g.If(n > 0):
                            finish_sum(before(n))
            finish_power(NBLK - 1)
            finish_sum(NBLK - 1)
            if k == 0:
                ln_power(g, 1, NBLK - 1)

        def last_step(n):
            return NHP * n + NHP - 1

        def three(dst, lhs, rhs, first, last):
            nc.tensor.matmul(dst, lhs[0], rhs[0], start=first, stop=False, skip_group_check=True)
            nc.tensor.matmul(dst, lhs[0], rhs[1], start=False, stop=False, skip_group_check=True)
            return nc.tensor.matmul(dst, lhs[1], rhs[0], start=False, stop=last, skip_group_check=True)

        def project_q(pe, n, hp, s):
            xs = (xT_hi[:, blk_cols(n)], xT_lo[:, blk_cols(n)])
            for j in range(3):
                if j == 0:
                    at_least(pe, a["kv_evac"], 2 * s - 1)
                elif j == 1:
                    at_least(pe, a["kv_evac"], 2 * s)
                else:
                    pe.wait_ge(a["q_evac"], 3 * s + 1)
                dst = ps_pj[(5 * hp + j) % 2]
                if j < 2:
                    w = tuple(w[:, 2 * hp + j, :, :].rearrange("p g f -> p (g f)") for w in (wq_hi, wq_lo))
                else:
                    w = tuple(w[:, hp * P:(hp + 1) * P] for w in (wk_hi, wk_lo))
                three(dst, w, xs, True, True).then_inc(a["pq_done"], 1)

        def project_kv(pe, n, hp, s):
            for j, (w_hi, w_lo) in enumerate(((wk_hi, wk_lo), (wv_hi, wv_lo))):
                pe.wait_ge(a["q_evac"], 3 * s + 2 + j)
                dst = ps_pj[(5 * hp + 3 + j) % 2]
                w = tuple(w[:, hp * P:(hp + 1) * P] for w in (w_hi, w_lo))
                for c in range(TPB):
                    cols = bass.ds(n * BLK + c * P, P)
                    i = three(dst[:, c * P:(c + 1) * P], (xT_hi[:, cols], xT_lo[:, cols]), w, True, True)
                i.then_inc(a["pkv_done"], 1)

        def attention_pe(pe):
            pe.wait_ge(w_att_ready, 1)
            pe.wait_ge(ln_lo, NBLK + 1)
            pe.wait_ge(ffn[0]["y_used"], E * NBLK + 1)
            project_q(pe, 0, 0, 0)
            project_kv(pe, 0, 0, 0)

            def transpose_out(s):
                pe.wait_ge(a["o_lo_done"], s + 1)
                pe.wait_ge(a["o_hi_done"], s + 1)
                half = ps_tr.bitcast(F16)
                for part, src in enumerate((o_hi, o_lo)):
                    for c in range(TPB):
                        at = part * BLK + c * P
                        i = nc.tensor.transpose(half[:, at:at + P], src[:, c * P:(c + 1) * P], ident_h[:])
                i.then_inc(a["otr_done"], 1)

            def project_out(hp, s):
                pe.wait_ge(a["ot_copied"], s + 1)
                for c in range(TPB):
                    o_t = tuple(oT[:, part * BLK + c * P:part * BLK + (c + 1) * P] for part in range(2))
                    i = three(ps_op[:, c * P:(c + 1) * P], o_t, (wo_hi[:, hp, :], wo_lo[:, hp, :]),
                              hp == 0 and c == 0, hp == NHP - 1 and c == TPB - 1)
                i.then_inc(a["op_done"], 1)

            def step_body(n, hp):
                s = NHP * n + hp
                par = hp % 2
                pe.wait_ge(a["q_evac"], 3 * s + 3)
                pe.wait_ge(a["o32_done"], s)
                for c in range(TPB):
                    cols = slice(c * P, (c + 1) * P)
                    for h in range(2):
                        rows = slice(h * DH, (h + 1) * DH)
                        i = nc.tensor.matmul(ps_so[:, h, cols], k_relu[rows, cols], q_relu[h][rows, cols],
                                             start=True, stop=True)
                i.then_inc(a["sc_done"], 1)
                pe.wait_ge(a["k_trig_done"], s + 1)
                pe.wait_ge(a["kv_evac"], 2 * s + 2)
                pe.wait_ge(a["s_ready"], s)
                for h in range(2):
                    for c in range(TPB):
                        i = nc.tensor.matmul(ps_st[:, h, c * VZ:(c + 1) * VZ],
                                             k_trig[:, 2 * c + h, :, :].rearrange("p g f -> p (g f)"),
                                             v_one[:, c, h, :], start=True, stop=True)
                i.then_inc(a["st_done"], 1)
                if hp < NHP - 1:
                    project_q(pe, n, hp + 1, s + 1)
                else:
                    with pe.If(n < NBLK - 1):
                        pe.wait_ge(ln_lo, NBLK + n + 2)
                        project_q(pe, after(n), 0, s + 1)
                if hp:
                    if hp == 5:
                        pe.wait_ge(ln_hi, 2 * NBLK + n)
                    if hp == 6:
                        pe.wait_ge(gate_read, NBLK + n)
                    transpose_out(s - 1)
                else:
                    with pe.If(n > 0):
                        transpose_out(last_step(before(n)))
                pe.wait_ge(a["probs_done"], s + 1)
                pe.wait_ge(a["q_trig_done"], s + 1)
                pe.wait_ge(a["s_ready"], s + 1)
                for h in range(2):
                    for c in range(TPB):
                        cols = slice(c * P, (c + 1) * P)
                        dst = ps_so[:, h, c * VZ:(c + 1) * VZ]
                        nc.tensor.matmul(dst, probs[h][:, cols], v_one[:, c, h, :], start=True, stop=False)
                        i = nc.tensor.matmul(dst, q_trig[par][h][:, cols], s_pref[par][:, c, h, :],
                                             start=False, stop=True)
                i.then_inc(a["o_done"], 1)
                if hp < NHP - 1:
                    project_kv(pe, n, hp + 1, s + 1)
                else:
                    with pe.If(n < NBLK - 1):
                        project_kv(pe, after(n), 0, s + 1)
                if hp:
                    if hp == 1:
                        pe.wait_ge(a["att_sum"], n)
                    project_out(hp - 1, s - 1)
                else:
                    with pe.If(n > 0):
                        project_out(NHP - 1, last_step(before(n)))
                if hp == 4:
                    with pe.If(n > 0):
                        ln_transpose(pe, 2, before(n))
                if hp == 5:
                    with pe.If(n > 0):
                        gate_product(pe, 2, before(n))

            with pe.Fori(0, B) as b:
                with pe.Fori(0, UPB) as u:
                    n = b * UPB + u
                    for hp in range(NHP):
                        step_body(n, hp)
            transpose_out(last_step(NBLK - 1))
            project_out(NHP - 1, last_step(NBLK - 1))
            ln_transpose(pe, 2, NBLK - 1)
            gate_product(pe, 2, NBLK - 1)
            pe.wait_ge(gate_read, 2 * NBLK)

        def attention_act(act):
            def relu_q(hp, s):
                act.wait_ge(a["q_trig_done"], s)
                for j in range(3):
                    act.wait_ge(a["pq_done"], 3 * s + j + 1)
                    dst = q_relu[j] if j < 2 else k_relu
                    bias = bq_sb[:, 2 * hp + j:2 * hp + j + 1] if j < 2 else bkT_sb[:, hp:hp + 1]
                    nc.scalar.activation(dst, ps_pj[(5 * hp + j) % 2], ACT.Relu, bias=bias, scale=s_qkv[:, 0:1]
                                         ).then_inc(a["q_evac"], 1)

            def copy_out(s):
                act.wait_ge(a["otr_done"], s + 1)
                nc.scalar.activation(oT, ps_tr.bitcast(F16), ACT.Copy).then_inc(a["ot_copied"], 1)

            relu_q(0, 0)
            with act.Fori(0, B) as b:
                with act.Fori(0, UPB) as u:
                    n = b * UPB + u
                    for hp in range(NHP):
                        s = NHP * n + hp
                        if hp < NHP - 1:
                            relu_q(hp + 1, s + 1)
                        else:
                            with act.If(n < NBLK - 1):
                                relu_q(0, s + 1)
                        if hp:
                            copy_out(s - 1)
                        else:
                            with act.If(n > 0):
                                copy_out(last_step(before(n)))
                        act.wait_ge(a["o32_done"], s + 1)
                        nc.scalar.activation(o_hi, o32.rearrange("p c h f -> p (c h f)"), ACT.Copy, scale=s_o[:, 0:1]
                                             ).then_inc(a["o_hi_done"], 1)
                        if hp == 4:
                            with act.If(n > 0):
                                ln_copy(act, 2, before(n))
            copy_out(last_step(NBLK - 1))
            ln_copy(act, 2, NBLK - 1)

        def attention_dve(v):
            def take_kv(u, hp, s):
                cols = slice(hp * P, (hp + 1) * P)

                def row(t):
                    return t[:, cols].rearrange("p (h f) -> p h f", h=2).unsqueeze(1).to_broadcast([P, TPB, 2, DH])

                def out_of(j):
                    return ps_pj[(5 * hp + 3 + j) % 2].rearrange("p (c h f) -> p c h f", c=TPB, h=2)

                v.wait_ge(a["pkv_done"], 2 * s + 1)
                nc.vector.scalar_tensor_tensor(k_tok, out_of(0), s_qkv[:, 0:1], row(bk_row), ALU.mult, ALU.add
                                               ).then_inc(a["kv_evac"], 1)
                wait_apart(v, a["kv_evac"], 2 * s + 1)
                for g in range(2):
                    trig = trig_cols[:, g, bass.ds(u * TPB * 2, TPB * 2)].unsqueeze(2).to_broadcast([P, TPB * 2, DH])
                    i = nc.vector.scalar_tensor_tensor(k_trig[:, :, g, :], k_tok.rearrange("p c h f -> p (c h) f"), 0.0, trig, ALU.max, ALU.mult)
                i.then_inc(a["k_trig_done"], 1)
                v.wait_ge(a["pkv_done"], 2 * s + 2)
                nc.vector.scalar_tensor_tensor(v_one[:, :, :, 0:DH], out_of(1), s_qkv[:, 0:1], row(bv_row),
                                               ALU.mult, ALU.add).then_inc(a["kv_evac"], 1)

            def step_body(n, u, hp):
                s = NHP * n + hp
                par = hp % 2
                v.wait_ge(a["sc_done"], s + 1)
                for h in range(2):
                    i = nc.vector.tensor_tensor(probs[h].rearrange("p (c i) -> p c i", c=TPB),
                                                ps_so[:, h, :].rearrange("p (c i) -> p c i", c=TPB),
                                                decay[:].unsqueeze(1).to_broadcast([P, TPB, P]), ALU.mult)
                i.then_inc(a["probs_done"], 1)
                run, pref = s_run[:, hp, :, :], s_pref[par]
                v.wait_ge(a["st_done"], s + 1)
                nc.vector.tensor_copy(pref[:, 0, :, :], run).then_inc(a["st_step"], 1)
                for c in range(TPB):
                    dst = pref[:, c + 1, :, :] if c < TPB - 1 else run
                    v.wait_ge(a["st_step"], TPB * s + c + 1)
                    nc.vector.tensor_tensor(dst, pref[:, c, :, :], ps_st[:, :, c * VZ:(c + 1) * VZ], ALU.add
                                            ).then_inc(a["st_step"] if c < TPB - 1 else a["s_ready"], 1)
                out = ps_so[:, :, 0:TPB * VZ].rearrange("p h (c z) -> p h c z", c=TPB)
                v.wait_ge(a["o_done"], s + 1)
                nc.vector.tensor_scalar(den, out[:, :, :, DH], DEN_EPS, None, ALU.max).then_inc(a["den_step"], 1)
                v.wait_ge(a["den_step"], 2 * s + 1)
                nc.vector.reciprocal(rden, den).then_inc(a["den_step"], 1)
                v.wait_ge(a["den_step"], 2 * s + 2)
                v.wait_ge(a["o_hi_done"], s)
                nc.vector.tensor_tensor(o32, out[:, :, :, 0:DH].rearrange("p h c f -> p c h f"),
                                        rden.rearrange("p h c -> p c h").unsqueeze(3).to_broadcast([P, TPB, 2, DH]),
                                        ALU.mult).then_inc(a["o32_done"], 1)
                if hp < NHP - 1:
                    take_kv(u, hp + 1, s + 1)
                else:
                    with v.If(n < NBLK - 1):
                        take_kv(1 - u, 0, s + 1)
                v.wait_ge(a["o_hi_done"], s + 1)
                nc.vector.scalar_tensor_tensor(o_lo, o32.rearrange("p c h f -> p (c h f)"), s_o[:, 0:1], o_hi,
                                               ALU.mult, ALU.subtract).then_inc(a["o_lo_done"], 1)

            ones = nc.vector.memset(v_one[:, :, :, DH:VZ], 1.0)
            ones.then_inc(a["s_zero"], 1)
            take_kv(0, 0, 0)
            with v.Fori(0, B) as b:
                nc.vector.memset(s_run, 0.0).then_inc(a["s_zero"], 1)
                wait_apart(v, a["s_zero"], b + 2)
                with v.Fori(0, UPB) as u:
                    n = b * UPB + u
                    for hp in range(NHP):
                        step_body(n, u, hp)
                        if hp == 0:
                            with v.If(n > 0):
                                add_attention(v, before(n))
                        if hp == 1:
                            with v.If(n > 0):
                                p = before(n)
                                v.wait_ge(a["att_x"], n)
                                ln_stats(v, 2, p)
                        if hp == 2:
                            with v.If(n > 0):
                                ln_apply(v, 2, before(n))
                        if hp == 5:
                            with v.If(n > 0):
                                p = before(n)
                                ln_low(v, 2, p)
                                gate_logits(v, 2, p)
            add_attention(v, NBLK - 1)
            v.wait_ge(a["att_x"], NBLK)
            ln_stats(v, 2, NBLK - 1)
            ln_apply(v, 2, NBLK - 1)
            ln_low(v, 2, NBLK - 1)
            gate_logits(v, 2, NBLK - 1)

        def add_attention(v, n):
            x = x_tok[:, bass.ds(n * TPB, TPB), :].rearrange("p t d -> p (t d)")
            v.wait_ge(a["op_done"], NHP * n + NHP)
            nc.vector.scalar_tensor_tensor(x, ps_op, s_att[:, 0:1], x, ALU.mult, ALU.add).then_inc(a["att_sum"], 1)

        def attention_pool(g):
            def trig_q(u, s, par):
                wait_apart(g, a["q_evac"], 3 * s + 2)
                for h in range(2):
                    i = nc.gpsimd.tensor_tensor(q_trig[par][h], q_relu[h], trig_rows[:, bass.ds(u * BLK, BLK)], ALU.mult)
                i.then_inc(a["q_trig_done"], 1)

            def add_bias(p):
                wait_apart(g, a["att_sum"], p + 1)
                x = x_tok[:, bass.ds(p * TPB, TPB), :]
                nc.gpsimd.tensor_tensor(x, x, bo_row[:].unsqueeze(1).to_broadcast([P, TPB, D]), ALU.add
                                        ).then_inc(a["att_x"], 1)

            trig_q(0, 0, 0)
            with g.Fori(0, B) as b:
                with g.Fori(0, UPB) as u:
                    n = b * UPB + u
                    for hp in range(NHP):
                        s = NHP * n + hp
                        if hp < NHP - 1:
                            trig_q(u, s + 1, (hp + 1) % 2)
                        else:
                            with g.If(n < NBLK - 1):
                                trig_q(1 - u, s + 1, 0)
                        if hp == 0:
                            with g.If(n > 0):
                                add_bias(before(n))
                        if hp == 1:
                            with g.If(n > 0):
                                ln_power(g, 2, before(n))
            add_bias(NBLK - 1)
            ln_power(g, 2, NBLK - 1)

        TINY = float(2.0 ** -99)

        def largest_of(v, col, src, last=False):
            i = nc.vector.tensor_reduce(largest[:, col:col + 1], src, AX_X, ALU.max, apply_absolute_value=True)
            if last:
                i.then_inc(max_part, 1)

        def reduce_largest(g, c0, c1, k):
            g.wait_ge(max_part, k + 1)
            nc.gpsimd.partition_all_reduce(largest_all[:, c0:c1], largest[:, c0:c1], P, RMAX).then_inc(max_all, 1)

        chain = [0]

        def link(v, ins):
            ins.then_inc(scale_step, 1)
            chain[0] += 1
            v.wait_ge(scale_step, chain[0])

        def power_of_two(v, col, k):
            at = slice(col, col + 1)
            v.wait_ge(max_all, k + 1)
            if col == W_OUT:
                src = largest_all[:, 4:5]
            else:
                src = largest_all[:, at]
            link(v, nc.vector.tensor_scalar(s_tmp[:, 0:1], src, TINY, None, ALU.max))
            link(v, nc.vector.tensor_scalar(pow2[:, at].bitcast(I32), s_tmp[:, 0:1].bitcast(I32), 0x7F800000, None,
                                            ALU.bitwise_and))
            link(v, nc.vector.reciprocal(rpow2[:, at], pow2[:, at]))
            link(v, nc.vector.tensor_scalar(s_w[:, at], rpow2[:, at], 2.0 ** 14, None, ALU.mult))

        def split_weights(v, pieces, col, ready):
            for raw, hi, lo in pieces:
                link(v, nc.vector.tensor_scalar(hi, raw, s_w[:, col:col + 1], None, ALU.mult))
                i = nc.vector.scalar_tensor_tensor(lo, raw, s_w[:, col:col + 1], hi, ALU.mult, ALU.subtract)
            i.then_inc(ready, 1)

        def setup_up(v):
            v.wait_ge(in_up, 16)
            largest_of(v, W_UP, arena_a[:], last=True)
            power_of_two(v, W_UP, 0)
            link(v, nc.vector.tensor_scalar(s_pre[:], pow2[:, W_UP:W_UP + 1], 2.0 ** -25, None, ALU.mult))
            link(v, nc.vector.tensor_scalar(s_h[:], rpow2[:, W_UP:W_UP + 1], 2.0 ** 7, None, ALU.mult))
            split_weights(v, [(arena_a[:], wup_hi[:], wup_lo[:])], W_UP, w_up_ready)

        def setup_down(v):
            v.wait_ge(in_dn, 16)
            largest_of(v, W_DOWN, arena_b[:], last=True)
            power_of_two(v, W_DOWN, 1)
            link(v, nc.vector.tensor_scalar(s_tmp[:, 1:2], pow2[:, W_DOWN:W_DOWN + 1], 2.0 ** -21, None, ALU.mult))
            link(v, nc.vector.tensor_tensor(s_y[:], s_tmp[:, 1:2], pow2[:, W_UP:W_UP + 1], ALU.mult))
            split_weights(v, [(arena_b[:], wdn_hi[:].rearrange("p c d -> p (c d)"),
                               wdn_lo[:].rearrange("p c d -> p (c d)"))], W_DOWN, w_dn_ready)
            setup_attention(v)

        def setup_attention(v):
            v.wait_ge(in_att, 16 * 4)
            raw = arena_a[:]
            largest_of(v, W_QKV, raw[:, 0:3 * HD])
            largest_of(v, 3, bv_row[:])
            largest_of(v, 4, raw[:, 3 * HD:4 * HD], last=True)
            v.wait_ge(max_all, 3)
            link(v, nc.vector.tensor_tensor(largest_all[:, 2:3], largest_all[:, 2:3], largest_all[:, 3:4], ALU.max))
            power_of_two(v, W_QKV, 2)
            power_of_two(v, W_OUT, 2)
            link(v, nc.vector.tensor_scalar(s_qkv[:], pow2[:, W_QKV:W_QKV + 1], 2.0 ** -25, None, ALU.mult))
            link(v, nc.vector.tensor_scalar(s_o[:], rpow2[:, W_QKV:W_QKV + 1], 2.0 ** 6, None, ALU.mult))
            link(v, nc.vector.tensor_scalar(s_tmp[:, 1:2], pow2[:, W_OUT:W_OUT + 1], 2.0 ** -20, None, ALU.mult))
            link(v, nc.vector.tensor_tensor(s_att[:], s_tmp[:, 1:2], pow2[:, W_QKV:W_QKV + 1], ALU.mult))
            twice = raw[:, 0:HD].rearrange("p (h f) -> p h f", h=H).unsqueeze(2).to_broadcast([P, H, 2, DH])
            for g in range(2):
                link(v, nc.vector.tensor_scalar(wq_hi[:, :, g, :], twice[:, :, g, :], s_w[:, W_QKV:W_QKV + 1], None,
                                                ALU.mult))
                link(v, nc.vector.scalar_tensor_tensor(wq_lo[:, :, g, :], twice[:, :, g, :], s_w[:, W_QKV:W_QKV + 1],
                                                       wq_hi[:, :, g, :], ALU.mult, ALU.subtract))
            for src, hi, lo in ((raw[:, HD:2 * HD], wk_hi[:], wk_lo[:]), (raw[:, 2 * HD:3 * HD], wv_hi[:], wv_lo[:])):
                link(v, nc.vector.tensor_scalar(hi, src, s_w[:, W_QKV:W_QKV + 1], None, ALU.mult))
                link(v, nc.vector.scalar_tensor_tensor(lo, src, s_w[:, W_QKV:W_QKV + 1], hi, ALU.mult, ALU.subtract))
            split_weights(v, [(raw[:, 3 * HD:4 * HD], wo_hi[:].rearrange("p n d -> p (n d)"),
                               wo_lo[:].rearrange("p n d -> p (n d)"))], W_OUT, w_att_ready)

        @block.sync
        def _(sp):
            sp.dma_start(x_tok[:], d["x"].rearrange("(t p) d -> p t d", p=P)).then_inc(in_x, 16)
            sp.dma_start(arena_a[:], d["w_up"]).then_inc(in_up, 16)
            sp.dma_start(arena_b[:], d["w_down"]).then_inc(in_dn, 16)
            sp.wait_ge(w_up_ready, 1)
            for j, name in enumerate(("wq", "wk", "wv", "wo")):
                sp.dma_start(arena_a[:, j * HD:(j + 1) * HD], d[name]).then_inc(in_att, 16)
            with sp.Fori(0, NBLK) as n:
                sp.wait_ge(ffn[1]["fin_x"], n + 1)
                rows = d["out"].rearrange("(t p) d -> p t d", p=P)
                sp.dma_start(rows[:, bass.ds(n * TPB, TPB), :], x_tok[:, bass.ds(n * TPB, TPB), :]).then_inc(out_done, 16)
            sp.wait_ge(out_done, 16 * NBLK)

        @block.scalar
        def _(act):
            small = ((ident, "c_ident"), (gate_sb, "gate_w"), (bq_sb, "bq2"), (bkT_sb, "bkT"), (trig_rows, "c_trig_rows"),
                     (decay, "c_decay"), (rank, "c_rank"))
            for dst, name in small:
                act.dma_start(dst[:], d[name]).then_inc(in_const, 16)
            act.dma_start(trig_cols[:].rearrange("p g t -> p (g t)"), d["c_trig_cols"]).then_inc(in_const, 16)
            act.dma_start(xnh[:, 0:8, :].rearrange("p t d -> p (t d)"), d["c_pick"]).then_inc(in_const, 16)
            for dst, name in ((gbias, "gbias"), (bk_row, "bk"), (bv_row, "bv"), (bo_row, "bo")):
                act.dma_start(dst[:], d[name].partition_broadcast(P)).then_inc(in_const, 16)
            act.wait_ge(const_ready, 1)
            with act.Fori(0, NBLK) as n:
                ln_copy(act, 0, n)
            ffn_act(act, 0)
            attention_act(act)
            ffn_act(act, 1)

        @block.gpsimd
        def _(g):
            g.wait_ge(const_ready, 1)
            with g.Fori(0, NBLK) as n:
                ln_power(g, 0, n)
            reduce_largest(g, 0, 1, 0)
            reduce_largest(g, 1, 2, 1)
            reduce_largest(g, 2, 5, 2)
            ffn_pool(g, 0)
            attention_pool(g)
            ffn_pool(g, 1)

        @block.vector
        def _(v):
            v.wait_ge(in_const, 16 * 13)
            nc.vector.memset(minus_half[:], -0.5)
            nc.vector.memset(sw3[:], 0.0)
            nc.vector.tensor_copy(ident_h[:], ident[:])
            nc.vector.tensor_copy(ident_b[:], ident[:])
            nc.vector.tensor_copy(pick[:].rearrange("p e q -> p (e q)"),
                                  xnh[:, 0:8, :].rearrange("p t d -> p (t d)")).then_inc(const_ready, 1)
            v.wait_ge(const_ready, 1)
            v.wait_ge(in_x, 16)
            with v.Fori(0, NBLK) as n:
                ln_stats(v, 0, n)
                ln_apply(v, 0, n)
                ln_low(v, 0, n)
                gate_logits(v, 0, n)
            setup_up(v)
            ffn_dve(v, 0)
            attention_dve(v)
            ffn_dve(v, 1)

        @block.tensor
        def _(pe):
            pe.wait_ge(const_ready, 1)
            with pe.Fori(0, NBLK) as n:
                pe.wait_ge(gate_read, n)
                ln_transpose(pe, 0, n)
                gate_product(pe, 0, n)
            pe.wait_ge(gate_read, NBLK)
            ffn_pe(pe, 0)
            attention_pe(pe)
            ffn_pe(pe, 1)


_ORDER = ("x", "wq", "wk", "wv", "wo", "bq2", "bkT", "bk", "bv", "bo", "gate_w", "gbias", "w_up", "w_down")


def kernel(L0_attn_x, L0_attn_Wq, L0_attn_bq, L0_attn_Wk, L0_attn_bk, L0_attn_Wv, L0_attn_bv, L0_attn_Wo, L0_attn_bo,
           L0_ffn_gate_w, L0_ffn_expert_bias, L0_ffn_w_up, L0_ffn_w_down):
    import concourse.bacc as bacc
    from concourse.bass_utils import run_bass_kernel_spmd

    bq = np.asarray(L0_attn_bq).reshape(H, DH).T
    arrays = {
        "x": np.asarray(L0_attn_x).reshape(NTOK, D),
        "wq": L0_attn_Wq, "wk": L0_attn_Wk, "wv": L0_attn_Wv,
        "wo": np.asarray(L0_attn_Wo).reshape(NHP, P, D).transpose(1, 0, 2).reshape(P, NHP * D),
        "bq2": np.concatenate([bq, bq], 0),
        "bkT": np.asarray(L0_attn_bk).reshape(NHP, P).T,
        "bk": L0_attn_bk, "bv": L0_attn_bv, "bo": L0_attn_bo,
        "gate_w": np.asarray(L0_ffn_gate_w).T,
        "gbias": L0_ffn_expert_bias,
        "w_up": np.asarray(L0_ffn_w_up).transpose(2, 0, 1).reshape(D, E * I),
        "w_down": np.asarray(L0_ffn_w_down).reshape(E, D, CH, P).transpose(3, 0, 2, 1).reshape(P, E * CH * D),
        **constants(),
    }
    arrays["c_trig_cols"] = arrays["c_trig_cols"].reshape(P, 4 * T // P)
    arrays = {n: np.ascontiguousarray(v) for n, v in arrays.items()}
    nc = bacc.Bacc("TRN2", target_bir_lowering=False, num_devices=1)
    d = {n: nc.dram_tensor(f"in_{n}", v.shape, mybir.dt.from_np(v.dtype), kind="ExternalInput").ap()
         for n, v in arrays.items()}
    d["out"] = nc.dram_tensor("out_x", (NTOK, D), F32, kind="ExternalOutput").ap()
    build(nc, d)
    r = run_bass_kernel_spmd(nc, [{f"in_{n}": v for n, v in arrays.items()}], core_ids=[0])
    return r.results[0]["out_x"].reshape(B, T, D)
```

```python
from contextlib import ExitStack

import numpy as np

import concourse.bass as bass
from concourse import mybir

P = 128
B, T, D = 4, 1024, 128
NTOK = B * T
NTILE = NTOK // P
TPB = 4
BLK = TPB * P
NBLK = NTOK // BLK
E, I, TOPK = 8, 512, 2
CH = I // P
PAIR = 2
NP = CH // PAIR
NPB = E * NP
H, DH = 16, 64
HD = H * DH
NHP = HD // P
VZ = DH + 1
UPB = T // BLK
LN_EPS, GATE_EPS, DEN_EPS = 1e-5, 1e-6, 1e-6
SPLIT3 = 3

F32, F16, BF16 = mybir.dt.float32, mybir.dt.float16, mybir.dt.bfloat16
I32, U32 = mybir.dt.int32, mybir.dt.uint32
ALU = mybir.AluOpType
ACT = mybir.ActivationFunctionType
AX_X = mybir.AxisListType.X
RMAX = bass.bass_isa.ReduceOp.max

CORE = 2.0 ** -23
ONE = 2.0 ** 14
FEATURE = 2.0 ** -19
BIAS_ONE = 2.0 ** 11
XSCALE = 4096.0
W_UP, W_DOWN, W_QKV, W_OUT = range(4)


def constants():
    f = np.float32
    angle = (f(np.pi / (2.0 * T)) * np.arange(T, dtype=f)).astype(f)
    cos, sin = np.cos(angle).astype(f), np.sin(angle).astype(f)
    trig_rows = np.concatenate([np.tile(cos, (DH, 1)), np.tile(sin, (DH, 1))], 0)
    trig_cols = np.stack([cos.reshape(-1, P).T, sin.reshape(-1, P).T], 1).astype(f)
    trig_cols = np.repeat(trig_cols[:, :, :, None], 2, 3)
    i, j = np.arange(P)[None, :], np.arange(P)[:, None]
    decay = np.where(j <= i, np.cos(np.pi / (2.0 * T) * (i - j)), 0.0).astype(f)
    pick = np.zeros((SPLIT3 * E, E, P), f)
    for e in range(E):
        for part in range(SPLIT3):
            pick[part * E + e, e] = 1.0
    return {
        "c_trig_rows": trig_rows,
        "c_trig_cols": trig_cols * f(FEATURE),
        "c_decay": decay * f(CORE),
        "c_ident": np.eye(P, dtype=f),
        "c_pick": pick.reshape(SPLIT3 * E, E * P),
        "c_rank": np.tile(np.arange(E, 0, -1, dtype=f), (P, 1)),
    }


def at_least(eng, sem, value):
    if isinstance(value, int) and value <= 0:
        return
    eng.wait_ge(sem, value)


def build(nc, d):
    with ExitStack() as ctx:
        def sb(name, shape, dt=F32):
            return ctx.enter_context(nc.sbuf_tensor(name, shape, dt))

        def sem(name):
            return ctx.enter_context(nc.semaphore(name))

        x_tok = sb("x_tok", [P, NTILE, D])
        xnh = sb("xnh", [P, NTILE, D])
        xT_hi = sb("xT_hi", [P, NTOK], F16)
        xT_lo = sb("xT_lo", [P, NTOK], F16)
        wup_hi, wup_lo = sb("wup_hi", [P, E * I], F16), sb("wup_lo", [P, E * I], F16)
        wdn_hi, wdn_lo = sb("wdn_hi", [P, E * CH, D], F16), sb("wdn_lo", [P, E * CH, D], F16)
        wq_hi, wq_lo = sb("wq_hi", [P, H, 2, DH], F16), sb("wq_lo", [P, H, 2, DH], F16)
        wk_hi, wk_lo = sb("wk_hi", [P, HD], F16), sb("wk_lo", [P, HD], F16)
        wv_hi, wv_lo = sb("wv_hi", [P, HD], F16), sb("wv_lo", [P, HD], F16)
        wo_hi, wo_lo = sb("wo_hi", [P, NHP, D], F16), sb("wo_lo", [P, NHP, D], F16)
        gate_sb = sb("gate_sb", [P, E])
        gbias = sb("gbias", [P, E])
        bq_sb = sb("bq_sb", [P, H])
        bkT_sb = sb("bkT_sb", [P, NHP])
        bk_row, bv_row, bo_row = sb("bk_row", [P, HD]), sb("bv_row", [P, HD]), sb("bo_row", [P, D])
        trig_rows = sb("trig_rows", [P, T])
        trig_cols = sb("trig_cols", [P, 2, 2 * T // P])
        decay = sb("decay", [P, P])
        ident = sb("ident", [P, P])
        ident_h = sb("ident_h", [P, P], F16)
        ident_b = sb("ident_b", [P, P], BF16)
        pick = sb("pick", [P, E, P], BF16)
        rank = sb("rank", [P, E])
        largest = sb("largest", [P, 9])
        largest_all = sb("largest_all", [P, 9])
        pow2 = sb("pow2", [P, 4])
        rpow2 = sb("rpow2", [P, 4])
        s_w = sb("s_w", [P, 4])
        s_pre = sb("s_pre", [P, 1])
        s_h = sb("s_h", [P, 1])
        s_y = sb("s_y", [P, 1])
        s_feature = sb("s_feature", [P, 1])
        s_eps = sb("s_eps", [P, 1])
        part_row = sb("part_row", [P, 2])
        bq_kept, bkT_kept = sb("bq_kept", [P, H]), sb("bkT_kept", [P, NHP])
        bias_one = sb("bias_one", [P, P], F16)
        s_att = sb("s_att", [P, 1])
        s_tmp = sb("s_tmp", [P, 2])
        logits = sb("logits", [P, NTILE, E])
        gw = sb("gw", [P, NTILE, E])
        gt = sb("gt", [P, NTILE, E])
        gsel = sb("gsel", [P, NTILE, E])
        gcol = sb("gcol", [P, 6, NTILE])
        sw3 = sb("sw3", [P, NTILE, P], BF16)
        sw3T = sb("sw3T", [P, NTOK], BF16)
        st6 = sb("st6", [P, TPB, 6])
        mv = sb("mv", [P, TPB, 2])
        var4 = sb("var4", [P, TPB])
        rstdh = sb("rstdh", [P, TPB])
        fmv = sb("fmv", [P, TPB, 2])
        fst6 = sb("fst6", [P, TPB, 6])
        fvar4 = sb("fvar4", [P, TPB])
        frstdh = sb("frstdh", [P, TPB])
        first_st6 = sb("first_st6", [P, NTILE, 6])
        first_mv = sb("first_mv", [P, NTILE, 2])
        first_var4 = sb("first_var4", [P, NTILE])
        first_rstdh = sb("first_rstdh", [P, NTILE])
        minus_half = sb("minus_half", [P, NTILE])
        xn_new = sb("xn_new", [P, TPB, D])
        xT32 = sb("xT32", [P, BLK])

        arena_a = sb("arena_a", [P, 4096])
        arena_b = sb("arena_b", [P, 4096])
        arena_c = sb("arena_c", [P, 6784])

        def carve(arena):
            at = [0]

            def take(n, dt=F32):
                words = n * mybir.dt.size(dt) // 4
                view = arena[:, at[0]:at[0] + words]
                at[0] += words
                assert at[0] <= arena.shape[1], at[0]
                return view if dt == F32 else view.bitcast(dt)
            return take

        take = carve(arena_c)
        h32 = [take(PAIR * BLK) for _ in range(2)]
        h_hi = [take(PAIR * BLK, F16) for _ in range(4)]
        h_lo = [take(PAIR * BLK, F16) for _ in range(4)]
        take = carve(arena_c)
        first_xT32 = [take(BLK) for _ in range(NBLK)]
        pick32 = take(E * P)[0:SPLIT3 * E, :]
        take = carve(arena_b)
        wb_sb = [take(BLK) for _ in range(2)]
        ytmp = [take(BLK) for _ in range(2)]
        acc = take(BLK)
        zt = take(BLK).rearrange("p (t d) -> p t d", t=TPB)

        bias_part = take(2 * HD, F16)

        take = carve(arena_a)
        q_trig = [take(BLK) for _ in range(2)]
        q_hi, q_lo = take(2 * BLK, F16), take(2 * BLK, F16)
        k_trig = take(TPB * 2 * P)
        bias_rows = take(2 * HD, F16).rearrange("p (j f) -> p j f", j=2)[0:2]
        take = carve(arena_b)
        q_relu = [take(BLK) for _ in range(2)]
        k_relu = take(BLK)
        probs = take(2 * BLK)
        probs_hi, probs_lo = take(2 * BLK, F16), take(2 * BLK, F16)
        take = carve(arena_c)
        k_hi, k_lo = take(TPB * 2 * P, F16), take(TPB * 2 * P, F16)
        v_hi, v_lo = (take(TPB * 2 * VZ, F16).rearrange("p (c h f) -> p (c h) f", c=TPB, h=2) for _ in range(2))
        o32 = take(BLK).rearrange("p (c h f) -> p c h f", c=TPB, h=2)
        o_hi, o_lo = take(BLK, F16), take(BLK, F16)
        oT = take(2 * BLK, F16)
        s_pref = take(TPB * 2 * VZ)
        s_hi, s_lo = take(TPB * 2 * VZ, F16), take(TPB * 2 * VZ, F16)
        s_run = take(NHP * 2 * VZ).rearrange("p (n h f) -> p n h f", n=NHP, h=2)
        den = take(2 * TPB).rearrange("p (h c) -> p h c", h=2)
        rden = take(2 * TPB).rearrange("p (h c) -> p h c", h=2)

        bank = [ctx.enter_context(nc.psum_tensor(f"bank{i}", [P, 2, BLK], F32)) for i in range(4)]
        ps_first = [bank[n // 2][:, n % 2, :] for n in range(NBLK)]
        ps_pre = [bank[0], bank[1]]
        ps_y = [bank[2][:, 0, :], bank[2][:, 1, :]]
        ps_wb = bank[3][:, 0, :]
        ps_tr = bank[3][:, 1, :]
        ps_so = bank[0]
        ps_st = bank[1]
        ps_pj = [bank[2][:, 0, :], bank[2][:, 1, :]]
        ps_op = bank[3][:, 0, :]

        in_x = [sem("in_x0"), sem("in_x1")]
        in_up, in_dn, in_att = sem("in_up"), sem("in_dn"), sem("in_att")
        in_const, in_tab = sem("in_const"), sem("in_tab")
        out_done = sem("out_done")
        zeroed = sem("zeroed")
        const_ready = sem("const_ready")
        first_stats, first_mean, first_var, first_rstd, first_norm, first_tr, first_hi, first_lo = (
            sem(f"first_{n}") for n in "stats mean var rstd norm tr hi lo".split())
        max_part, max_all = sem("max_part"), sem("max_all")
        scale_step = sem("scale_step")
        scale_ready = sem("scale_ready")
        split_hi = sem("split_hi")
        w_up_ready, w_dn_ready, w_att_ready = sem("w_up_ready"), sem("w_dn_ready"), sem("w_att_ready")
        arena_free = sem("arena_free")
        ln_read, ln_mean, ln_var, ln_rstd, ln_norm = (sem(f"ln_{n}") for n in "read mean var rstd norm".split())
        ln_tr, ln_copied, ln_hi, ln_lo = (sem(n) for n in ("ln_tr", "ln_copied", "ln_hi", "ln_lo"))
        gate_mm, gate_read = sem("gate_mm"), sem("gate_read")
        gate_step, gate_exp, gate_in = sem("gate_step"), sem("gate_exp"), sem("gate_in")
        sw_split, sw_tr, sw_copied = sem("sw_split"), sem("sw_tr"), sem("sw_copied")

        def ffn_sems(k):
            names = ("up_done gelu_done hi_act hi_dve lo_done down_done wb_mm wb_copied y_used "
                     "acc_done acc_tr fin_st fin_ag fin_var fin_rstd fin_z fin_sum fin_x").split()
            return {n: sem(f"{n}{k}") for n in names}

        ffn = [ffn_sems(0), ffn_sems(1)]
        names = ("pq_done pk_done pv_done q_evac q_trig_done q_hi_done q_lo_done k_trig_done k_hi_done "
                 "k_lo_done v_hi_done v_lo_done sc_done probs_done probs_hi_done probs_lo_done st_done st_step "
                 "s_ready s_hi_done s_lo_done o_done den_step o32_done o_hi_done o_lo_done otr_done "
                 "ot_copied op_done att_sum att_x s_zero").split()
        a = {n: sem(n) for n in names}

        passed = sem("passed")

        def wait_apart(eng, sem, value):
            eng.wait_ge(sem, value)
            eng.sem_inc(passed, 1)

        block = ctx.enter_context(nc.Block())

        def blk_cols(n):
            return bass.ds(n * BLK, BLK)

        def tile_of(t3, n, t):
            return t3[:, bass.ds(n * TPB + t, 1), :].rearrange("p a d -> p (a d)")

        def before(n):
            return nc.s_assert_within(n - 1, 0, NBLK - 2,
                                      skip_runtime_bounds_check_because="stands under If(n > 0)")

        def after(n):
            return nc.s_assert_within(n + 1, 1, NBLK - 1,
                                      skip_runtime_bounds_check_because="stands under If(n < NBLK - 1)")

        HALF = NTILE // 2
        TPI = 8

        def first_ln_stats(v, half):
            v.wait_ge(in_x[half], 16)
            for t in range(half * HALF, (half + 1) * HALF):
                i = nc.vector.bn_stats(first_st6[:, t, :], x_tok[:, t, :])
            i.then_inc(first_stats, 1)
            v.wait_ge(first_stats, half + 1)
            for t in range(half * HALF, (half + 1) * HALF):
                i = nc.vector.bn_aggr(first_mv[:, t, :], first_st6[:, t, :])
            i.then_inc(first_mean, 1)
            v.wait_ge(first_mean, half + 1)
            tiles = slice(half * HALF, (half + 1) * HALF)
            nc.vector.tensor_scalar(first_var4[:, tiles], first_mv[:, tiles, 1], LN_EPS, 4.0, ALU.add, ALU.mult
                                    ).then_inc(first_var, 1)

        def first_ln_power(g, half):
            g.wait_ge(first_var, half + 1)
            tiles = slice(half * HALF, (half + 1) * HALF)
            nc.gpsimd.tensor_tensor(first_rstdh[:, tiles], first_var4[:, tiles], minus_half[:, tiles], ALU.pow
                                    ).then_inc(first_rstd, 1)

        def first_ln_apply(v, half):
            v.wait_ge(first_rstd, half + 1)
            with v.Fori(half * HALF // TPI, (half + 1) * HALF // TPI) as i:
                for t in range(TPI):
                    tile = bass.ds(i * TPI + t, 1)
                    op = nc.vector.tensor_scalar(
                        xnh[:, tile, :].rearrange("p a d -> p (a d)"), x_tok[:, tile, :].rearrange("p a d -> p (a d)"),
                        first_mv[:, tile, 0:1].rearrange("p a s -> p (a s)"), first_rstdh[:, tile],
                        ALU.subtract, ALU.mult)
                    if t % TPB == TPB - 1:
                        op.then_inc(first_norm, 1)

        def first_transpose(pe):
            for n in range(NBLK):
                pe.wait_ge(first_norm, n + 1)
                for t in range(TPB):
                    i = nc.tensor.transpose(ps_first[n][:, t * P:(t + 1) * P], xnh[:, n * TPB + t, :], ident[:])
                i.then_inc(first_tr, 1)
            for n in range(NBLK):
                pe.wait_ge(first_hi, n + 1)
                for t in range(TPB):
                    i = nc.tensor.matmul(ps_first[n][:, t * E:(t + 1) * E], first_xT32[n][:, t * P:(t + 1) * P],
                                         gate_sb[:], start=True, stop=True)
                i.then_inc(gate_mm, 1)

        def first_copy(act):
            for n in range(NBLK):
                act.wait_ge(first_tr, n + 1)
                nc.scalar.activation(first_xT32[n], ps_first[n], ACT.Copy)
                nc.scalar.activation(xT_hi[:, n * BLK:(n + 1) * BLK], ps_first[n], ACT.Copy, scale=XSCALE
                                     ).then_inc(first_hi, 1)

        def first_low(v):
            for n in range(NBLK):
                v.wait_ge(first_hi, n + 1)
                cols = slice(n * BLK, (n + 1) * BLK)
                nc.vector.scalar_tensor_tensor(xT_lo[:, cols], first_xT32[n], XSCALE, xT_hi[:, cols],
                                               ALU.mult, ALU.subtract).then_inc(first_lo, 1)

        def first_logits(v):
            for n in range(NBLK):
                v.wait_ge(gate_mm, n + 1)
                read_logits(v, n, ps_first[n])

        def read_logits(v, n, ps):
            nc.vector.scalar_tensor_tensor(
                logits[:, bass.ds(n * TPB, TPB), :], ps[:, 0:TPB * E].rearrange("p (t e) -> p t e", t=TPB), 2.0,
                gbias[:].unsqueeze(1).to_broadcast([P, TPB, E]), ALU.mult, ALU.add).then_inc(gate_read, 1)

        def ln_stats(v, r, n):
            for t in range(TPB):
                i = nc.vector.bn_stats(st6[:, t, :], tile_of(x_tok, n, t))
            i.then_inc(ln_read, 1)
            wait_apart(v, ln_read, r * NBLK + n + 1)
            for t in range(TPB):
                i = nc.vector.bn_aggr(mv[:, t, :], st6[:, t, :])
            i.then_inc(ln_mean, 1)
            v.wait_ge(ln_mean, r * NBLK + n + 1)
            nc.vector.tensor_scalar(var4[:], mv[:, :, 1], LN_EPS, 4.0, ALU.add, ALU.mult).then_inc(ln_var, 1)

        def ln_power(g, r, n):
            g.wait_ge(ln_var, r * NBLK + n + 1)
            nc.gpsimd.tensor_tensor(rstdh[:], var4[:], minus_half[:, 0:TPB], ALU.pow).then_inc(ln_rstd, 1)

        def ln_apply(v, r, n):
            v.wait_ge(ln_rstd, r * NBLK + n + 1)
            v.wait_ge(ln_hi, r * NBLK + n + 1)
            for t in range(TPB):
                i = nc.vector.tensor_scalar(xn_new[:, t, :], tile_of(x_tok, n, t), mv[:, t, 0:1], rstdh[:, t:t + 1],
                                            ALU.subtract, ALU.mult)
            i.then_inc(ln_norm, 1)

        def ln_transpose(pe, r, n):
            pe.wait_ge(ln_norm, r * NBLK + n + 1)
            for t in range(TPB):
                i = nc.tensor.transpose(ps_tr[:, t * P:(t + 1) * P], xn_new[:, t, :], ident[:])
            i.then_inc(ln_tr, 1)

        def ln_copy(act, r, n):
            act.wait_ge(ln_lo, r * NBLK + n + 1)
            if r:
                act.wait_ge(gate_mm, NBLK + n)
            act.wait_ge(ln_tr, r * NBLK + n + 1)
            nc.scalar.activation(xT32[:], ps_tr, ACT.Copy).then_inc(ln_copied, 1)
            if r:
                nc.scalar.activation(xnh[:, bass.ds(n * TPB, TPB), :], xn_new[:], ACT.Copy)
            nc.scalar.activation(xT_hi[:, blk_cols(n)], ps_tr, ACT.Copy, scale=XSCALE).then_inc(ln_hi, 1)

        def ln_low(v, r, n):
            v.wait_ge(ln_hi, r * NBLK + n + 2)
            nc.vector.scalar_tensor_tensor(xT_lo[:, blk_cols(n)], xT32[:], XSCALE, xT_hi[:, blk_cols(n)],
                                           ALU.mult, ALU.subtract).then_inc(ln_lo, 1)

        def gate_product(pe, r, n):
            pe.wait_ge(ln_hi, r * NBLK + n + 2)
            for t in range(TPB):
                i = nc.tensor.matmul(ps_tr[:, t * E:(t + 1) * E], xT32[:, t * P:(t + 1) * P], gate_sb[:],
                                     start=True, stop=True)
            i.then_inc(gate_mm, 1)

        def gate_logits(v, r, n):
            v.wait_ge(gate_mm, r * NBLK + n + 1)
            read_logits(v, n, ps_tr)

        def gating(v, k):
            base = k * 20
            step = [base]

            def then(ins):
                ins.then_inc(gate_step, 1)
                step[0] += 1
                v.wait_ge(gate_step, step[0])

            def wide(col):
                return gcol[:, col, :].unsqueeze(2).to_broadcast([P, NTILE, E])

            ranks = rank[:].unsqueeze(1).to_broadcast([P, NTILE, E])
            v.wait_ge(gate_read, NBLK * (k + 1))
            then(nc.vector.tensor_reduce(gcol[:, 0, :], logits[:], AX_X, ALU.max))
            nc.vector.tensor_tensor(gt[:], logits[:], wide(0), ALU.subtract).then_inc(gate_in, 1)
            v.wait_ge(gate_exp, k + 1)
            then(nc.vector.tensor_reduce(gcol[:, 0, :], gw[:], AX_X, ALU.add))
            then(nc.vector.reciprocal(gcol[:, 1, :], gcol[:, 0, :]))
            then(nc.vector.tensor_tensor(gw[:], gw[:], wide(1), ALU.mult))
            then(nc.vector.tensor_reduce(gcol[:, 2, :], gw[:], AX_X, ALU.max))
            then(nc.vector.tensor_tensor(gt[:], gw[:], wide(2), ALU.is_equal))
            then(nc.vector.tensor_tensor(gt[:], gt[:], ranks, ALU.mult))
            then(nc.vector.tensor_reduce(gcol[:, 3, :], gt[:], AX_X, ALU.max))
            then(nc.vector.tensor_tensor(gsel[:], gt[:], wide(3), ALU.is_equal))
            then(nc.vector.scalar_tensor_tensor(gt[:], gsel[:], -2.0, gw[:], ALU.mult, ALU.add))
            then(nc.vector.tensor_reduce(gcol[:, 4, :], gt[:], AX_X, ALU.max))
            then(nc.vector.tensor_tensor(gt[:], gt[:], wide(4), ALU.is_equal))
            then(nc.vector.tensor_tensor(gt[:], gt[:], ranks, ALU.mult))
            then(nc.vector.tensor_reduce(gcol[:, 3, :], gt[:], AX_X, ALU.max))
            then(nc.vector.tensor_tensor(gt[:], gt[:], wide(3), ALU.is_equal))
            then(nc.vector.tensor_tensor(gsel[:], gsel[:], gt[:], ALU.add))
            then(nc.vector.scalar_tensor_tensor(gcol[:, 5, :], gcol[:, 2, :], GATE_EPS, gcol[:, 4, :],
                                                ALU.add, ALU.add))
            then(nc.vector.reciprocal(gcol[:, 5, :], gcol[:, 5, :]))
            then(nc.vector.tensor_tensor(gsel[:], gsel[:], gw[:], ALU.mult))
            then(nc.vector.tensor_tensor(gsel[:], gsel[:], wide(5), ALU.mult))
            assert step[0] == base + 20, step[0] - base
            for part in range(SPLIT3):
                dst = sw3[:, :, part * E:(part + 1) * E]
                nc.vector.tensor_copy(dst, gsel[:]).then_inc(sw_split, 1)
                v.wait_ge(sw_split, k * 2 * SPLIT3 + 2 * part + 1)
                nc.vector.tensor_tensor(gsel[:], gsel[:], dst, ALU.subtract).then_inc(sw_split, 1)
                v.wait_ge(sw_split, k * 2 * SPLIT3 + 2 * part + 2)

        def gating_exp(act, k):
            act.wait_ge(gate_in, k + 1)
            nc.scalar.activation(gw[:], gt[:], ACT.Exp).then_inc(gate_exp, 1)

        def gating_transpose(pe, k):
            pe.wait_ge(sw_split, (k + 1) * 2 * SPLIT3)
            for q in range(NTILE // 8):
                at_least(pe, sw_copied, k * 4 + q)
                if k and not q:
                    pe.wait_ge(a["att_sum"], NBLK)
                for t in range(8):
                    i = nc.tensor.transpose(ps_wb.bitcast(BF16)[:, t * P:(t + 1) * P], sw3[:, q * 8 + t, :], ident_b[:])
                i.then_inc(sw_tr, 1)

        def gating_copy(act, k):
            for q in range(NTILE // 8):
                act.wait_ge(sw_tr, k * 4 + q + 1)
                nc.scalar.activation(sw3T[:, q * 8 * P:(q + 1) * 8 * P], ps_wb.bitcast(BF16), ACT.Copy).then_inc(sw_copied, 1)

        LAG = 3

        def up(pe, S, n, m):
            for c in range(PAIR):
                cols = slice((m * PAIR + c) * P, (m * PAIR + c + 1) * P)
                dst = ps_pre[m % 2][:, c, :]
                nc.tensor.matmul(dst, wup_hi[:, cols], xT_hi[:, blk_cols(n)], start=True, stop=False)
                nc.tensor.matmul(dst, wup_hi[:, cols], xT_lo[:, blk_cols(n)], start=False, stop=False)
                i = nc.tensor.matmul(dst, wup_lo[:, cols], xT_hi[:, blk_cols(n)], start=False, stop=True)
            i.then_inc(S["up_done"], 1)

        def down(pe, S, m):
            e, q = divmod(m, NP)
            for c in range(PAIR):
                w = m * PAIR + c
                hi, lo = (h[m % 4][:, c * BLK:(c + 1) * BLK] for h in (h_hi, h_lo))
                first, last = (q == 0 and c == 0), (q == NP - 1 and c == PAIR - 1)
                nc.tensor.matmul(ps_y[e % 2], wdn_hi[:, w, :], hi, start=first, stop=False)
                nc.tensor.matmul(ps_y[e % 2], wdn_hi[:, w, :], lo, start=False, stop=False)
                i = nc.tensor.matmul(ps_y[e % 2], wdn_lo[:, w, :], hi, start=False, stop=last)
            i.then_inc(S["down_done"], 1)

        def ffn_pe(pe, k):
            S = ffn[k]
            if k == 0:
                pe.wait_ge(w_up_ready, 1)
                pe.wait_ge(first_lo, NBLK)
            else:
                pe.wait_ge(ln_lo, NBLK + 2)
            for m in range(LAG):
                if m > 1:
                    pe.wait_ge(S["gelu_done"], m - 1)
                up(pe, S, 0, m)
            gating_transpose(pe, k)
            if k == 0:
                pe.wait_ge(w_dn_ready, 1)

            def finish_transpose(p):
                pe.wait_ge(S["acc_done"], (E - 1) * p + E - 1)
                if k == 0:
                    pe.wait_ge(ln_hi, p + 1)
                for t in range(TPB):
                    i = nc.tensor.transpose(ps_tr[:, t * P:(t + 1) * P], acc[:, t * P:(t + 1) * P], ident[:])
                i.then_inc(S["acc_tr"], 1)

            with pe.Fori(0, NBLK) as n:
                for m in range(NPB):
                    e = m // NP
                    if m % NP == 0:
                        pe.wait_ge(S["y_used"], E * n + e)
                    pe.wait_ge(S["lo_done"], NPB * n + m + 1)
                    down(pe, S, m)
                    if m < NPB - LAG:
                        pe.wait_ge(S["gelu_done"], NPB * n + m + LAG - 1)
                        up(pe, S, n, m + LAG)
                    else:
                        with pe.If(n < NBLK - 1):
                            pe.wait_ge(S["gelu_done"], NPB * n + m + LAG - 1)
                            if m == NPB - LAG and k:
                                pe.wait_ge(ln_lo, NBLK + n + 3)
                            up(pe, S, after(n), m + LAG - NPB)
                    if m % NP == 0:
                        pe.wait_ge(S["wb_copied"], E * n + e)
                        pe.wait_ge(sw_copied, 4 * (k + 1))
                        nc.tensor.matmul(ps_wb, pick[:, e, :], sw3T[:, blk_cols(n)], start=True, stop=True
                                         ).then_inc(S["wb_mm"], 1)
                    if m == 1:
                        with pe.If(n > 0):
                            finish_transpose(before(n))
                    if m == 11 and k == 0:
                        with pe.If(n > 0):
                            pe.wait_ge(S["fin_z"], n)
                            ln_transpose(pe, 0, before(n))
            finish_transpose(NBLK - 1)
            if k == 0:
                pe.wait_ge(S["fin_z"], NBLK)
                ln_transpose(pe, 0, NBLK - 1)

        def ffn_act(act, k):
            S = ffn[k]

            def hidden(n, m):
                g = NPB * n + m
                act.wait_ge(S["up_done"], g + 1)
                at_least(act, S["lo_done"], g - 1)
                nc.scalar.activation(h32[m % 2], ps_pre[m % 2][:, :, :].rearrange("p c t -> p (c t)"), ACT.Gelu,
                                     scale=s_pre[:, 0:1]).then_inc(S["gelu_done"], 1)
                if m % 2 == 0:
                    act.wait_ge(S["gelu_done"], g + 1)
                    nc.scalar.activation(h_hi[m % 4], h32[m % 2], ACT.Copy, scale=s_h[:, 0:1]).then_inc(S["hi_act"], 1)

            for m in range(LAG):
                hidden(0, m)
            gating_exp(act, k)
            gating_copy(act, k)
            with act.Fori(0, NBLK) as n:
                for m in range(NPB):
                    if m < NPB - LAG:
                        hidden(n, m + LAG)
                    else:
                        with act.If(n < NBLK - 1):
                            hidden(n + 1, m + LAG - NPB)
                    if m % NP == 0:
                        e = m // NP
                        act.wait_ge(S["y_used"], E * n + e)
                        act.wait_ge(S["wb_mm"], E * n + e + 1)
                        nc.scalar.activation(wb_sb[e % 2], ps_wb, ACT.Copy, scale=s_y[:, 0:1]
                                             ).then_inc(S["wb_copied"], 1)
                    if m == 12 and k == 0:
                        with act.If(n > 0):
                            ln_copy(act, 0, before(n))
            if k == 0:
                ln_copy(act, 0, NBLK - 1)

        def ffn_dve(v, k):
            S = ffn[k]

            def split(n, m, credit=False):
                g = NPB * n + m
                src, hi, lo = h32[m % 2], h_hi[m % 4], h_lo[m % 4]
                if m % 2 == 0:
                    v.wait_ge(S["hi_act"], (NPB // 2) * n + m // 2 + 1)
                else:
                    v.wait_ge(S["gelu_done"], g + 1)
                    nc.vector.tensor_scalar(hi, src, s_h[:, 0:1], None, ALU.mult).then_inc(S["hi_dve"], 1)
                    v.wait_ge(S["hi_dve"], (NPB // 2) * n + m // 2 + 1)
                nc.vector.scalar_tensor_tensor(lo, src, s_h[:, 0:1], hi, ALU.mult, ALU.subtract
                                               ).then_inc(S["lo_done"], 1)

            def combine(n, e):
                v.wait_ge(S["wb_copied"], E * n + e + 1)
                if e == 0:
                    v.wait_ge(S["acc_tr"], n)
                    dst = acc
                else:
                    v.wait_ge(S["acc_done"], (E - 1) * n + max(e - 2, 0))
                    dst = ytmp[e % 2]
                v.wait_ge(S["down_done"], NPB * n + NP * (e + 1))
                nc.vector.tensor_tensor(dst, ps_y[e % 2], wb_sb[e % 2], ALU.mult).then_inc(S["y_used"], 1)

            def finish_stats(p):
                v.wait_ge(S["acc_tr"], p + 1)
                for t in range(TPB):
                    i = nc.vector.bn_stats(fst6[:, t, :], ps_tr[:, t * P:(t + 1) * P])
                i.then_inc(S["fin_st"], 1)
                wait_apart(v, S["fin_st"], p + 1)
                for t in range(TPB):
                    i = nc.vector.bn_aggr(fmv[:, t, :], fst6[:, t, :])
                i.then_inc(S["fin_ag"], 1)
                v.wait_ge(S["fin_ag"], p + 1)
                nc.vector.tensor_scalar(fvar4[:], fmv[:, :, 1], LN_EPS, 4.0, ALU.add, ALU.mult).then_inc(S["fin_var"], 1)

            def finish_apply(p):
                v.wait_ge(S["fin_rstd"], p + 1)
                for t in range(TPB):
                    i = nc.vector.tensor_scalar(zt[:, t, :], ps_tr[:, t * P:(t + 1) * P], fmv[:, t, 0:1],
                                                frstdh[:, t:t + 1], ALU.subtract, ALU.mult)
                i.then_inc(S["fin_z"], 1)

            for m in range(LAG):
                split(0, m)
            v.sem_inc(S["y_used"], 1)
            gating(v, k)
            with v.Fori(0, NBLK) as n:
                for m in range(NPB):
                    if m in ATT_SETUP_SLOTS and k == 0:
                        with v.If(n < 1):
                            attention_weights(v, ATT_SETUP_SLOTS.index(m))
                    if m % 2 == 1:
                        combine(n, m // NP)
                    if m < NPB - LAG:
                        split(n, m + LAG)
                    else:
                        with v.If(n < NBLK - 1):
                            split(n + 1, m + LAG - NPB)
                    if m == 2:
                        with v.If(n > 0):
                            finish_stats(before(n))
                    if m == 4:
                        with v.If(n > 0):
                            finish_apply(before(n))
                    if m == 7 and k == 0:
                        with v.If(n > 0):
                            p = before(n)
                            v.wait_ge(S["fin_x"], p + 1)
                            ln_stats(v, 0, p)
                    if m == 9 and k == 0:
                        with v.If(n > 0):
                            ln_apply(v, 0, before(n))
                    if m == 14 and k == 0:
                        with v.If(n > 0):
                            ln_low(v, 0, before(n))
            last = NBLK - 1
            finish_stats(last)
            finish_apply(last)
            if k == 0:
                v.wait_ge(S["fin_x"], NBLK)
                ln_stats(v, 0, last)
                ln_apply(v, 0, last)
                ln_low(v, 0, last)

        def ffn_pool(g, k):
            S = ffn[k]

            def add(n, e):
                g.wait_ge(S["y_used"], E * n + e + 2)
                if e > 1:
                    g.wait_ge(S["acc_done"], (E - 1) * n + e - 1)
                nc.gpsimd.tensor_tensor(acc, acc, ytmp[e % 2], ALU.add).then_inc(S["acc_done"], 1)

            def finish_power(p):
                g.wait_ge(S["fin_var"], p + 1)
                nc.gpsimd.tensor_tensor(frstdh[:], fvar4[:], minus_half[:, 0:TPB], ALU.pow).then_inc(S["fin_rstd"], 1)

            def finish_sum(p):
                wait_apart(g, S["fin_z"], p + 1)
                tiles = bass.ds(p * TPB, TPB)
                nc.gpsimd.tensor_tensor(zt, zt, xnh[:, tiles, :], ALU.add).then_inc(S["fin_sum"], 1)
                wait_apart(g, S["fin_sum"], p + 1)
                nc.gpsimd.tensor_tensor(x_tok[:, tiles, :], x_tok[:, tiles, :], zt, ALU.add).then_inc(S["fin_x"], 1)

            with g.Fori(0, NBLK) as n:
                for e in range(E):
                    if e == 4 and k == 0:
                        with g.If(n > 0):
                            ln_power(g, 0, before(n))
                    if e:
                        add(n, e)
                    if e == 3 and k == 0:
                        with g.If(n < 1):
                            reduce_largest(g, 2, 9, 2)
                    if e == 1:
                        with g.If(n > 0):
                            finish_power(before(n))
                    if e == 2:
                        with g.If(n > 0):
                            finish_sum(before(n))
            finish_power(NBLK - 1)
            finish_sum(NBLK - 1)
            if k == 0:
                ln_power(g, 0, NBLK - 1)

        def last_step(n):
            return NHP * n + NHP - 1

        def three(dst, lhs, rhs, first, last):
            nc.tensor.matmul(dst, lhs[0], rhs[0], start=first, stop=False, skip_group_check=True)
            nc.tensor.matmul(dst, lhs[0], rhs[1], start=False, stop=False, skip_group_check=True)
            return nc.tensor.matmul(dst, lhs[1], rhs[0], start=False, stop=last, skip_group_check=True)

        def project_q(pe, n, hp, s):
            xs = (xT_hi[:, blk_cols(n)], xT_lo[:, blk_cols(n)])
            for j in range(3):
                if j == 0:
                    at_least(pe, a["k_trig_done"], s)
                elif j == 1:
                    at_least(pe, a["v_lo_done"], s)
                else:
                    pe.wait_ge(a["q_evac"], 3 * s + 1)
                dst = ps_pj[(5 * hp + j) % 2]
                if j < 2:
                    w = tuple(w[:, 2 * hp + j, :, :].rearrange("p g f -> p (g f)") for w in (wq_hi, wq_lo))
                else:
                    w = tuple(w[:, hp * P:(hp + 1) * P] for w in (wk_hi, wk_lo))
                three(dst, w, xs, True, True).then_inc(a["pq_done"], 1)

        def project_tok(pe, n, hp, s, j):
            pe.wait_ge(a["q_evac"], 3 * s + 2 + j)
            dst = ps_pj[(5 * hp + 3 + j) % 2]
            feats = slice(hp * P, (hp + 1) * P)
            w = tuple(w[:, feats] for w in ((wk_hi, wk_lo), (wv_hi, wv_lo))[j])
            for c in range(TPB):
                cols = bass.ds(n * BLK + c * P, P)
                to = dst[:, c * P:(c + 1) * P]
                nc.tensor.matmul(to, bias_one[0:2, :], bias_rows[:, j, feats], start=True, stop=False,
                                 skip_group_check=True)
                i = three(to, (xT_hi[:, cols], xT_lo[:, cols]), w, False, True)
            i.then_inc(a[("pk_done", "pv_done")[j]], 1)

        def attention_pe(pe):
            pe.wait_ge(w_att_ready, 1)
            pe.wait_ge(ln_lo, 2)
            pe.wait_ge(ffn[0]["y_used"], E * NBLK + 1)
            project_q(pe, 0, 0, 0)
            project_tok(pe, 0, 0, 0, 0)
            project_tok(pe, 0, 0, 0, 1)

            def transpose_out(s):
                pe.wait_ge(a["o_lo_done"], s + 1)
                pe.wait_ge(a["o_hi_done"], s + 1)
                half = ps_tr.bitcast(F16)
                for part, src in enumerate((o_hi, o_lo)):
                    for c in range(TPB):
                        at = part * BLK + c * P
                        i = nc.tensor.transpose(half[:, at:at + P], src[:, c * P:(c + 1) * P], ident_h[:])
                i.then_inc(a["otr_done"], 1)

            def project_out(hp, s):
                pe.wait_ge(a["ot_copied"], s + 1)
                for c in range(TPB):
                    o_t = tuple(oT[:, part * BLK + c * P:part * BLK + (c + 1) * P] for part in range(2))
                    i = three(ps_op[:, c * P:(c + 1) * P], o_t, (wo_hi[:, hp, :], wo_lo[:, hp, :]),
                              hp == 0 and c == 0, hp == NHP - 1 and c == TPB - 1)
                i.then_inc(a["op_done"], 1)

            def step_body(n, hp):
                s = NHP * n + hp
                pe.wait_ge(a["q_evac"], 3 * s + 3)
                pe.wait_ge(a["o32_done"], s)
                for c in range(TPB):
                    cols = slice(c * P, (c + 1) * P)
                    for h in range(2):
                        rows = slice(h * DH, (h + 1) * DH)
                        i = nc.tensor.matmul(ps_so[:, h, cols], k_relu[rows, cols], q_relu[h][rows, cols],
                                             start=True, stop=True)
                i.then_inc(a["sc_done"], 1)
                pe.wait_ge(a["v_lo_done"], s + 1)
                pe.wait_ge(a["k_lo_done"], s + 1)
                pe.wait_ge(a["s_ready"], s)
                for h in range(2):
                    for c in range(TPB):
                        at = 2 * c + h
                        i = three(ps_st[:, h, c * VZ:(c + 1) * VZ], tuple(k[:, at * P:(at + 1) * P] for k in (k_hi, k_lo)),
                                  (v_hi[:, at, :], v_lo[:, at, :]), True, True)
                i.then_inc(a["st_done"], 1)
                if hp < NHP - 1:
                    project_q(pe, n, hp + 1, s + 1)
                else:
                    with pe.If(n < NBLK - 1):
                        pe.wait_ge(ln_lo, n + 3)
                        project_q(pe, after(n), 0, s + 1)
                if hp:
                    if hp == 5:
                        pe.wait_ge(ln_hi, NBLK + n + 1)
                    if hp == 6:
                        pe.wait_ge(gate_read, NBLK + n)
                    transpose_out(s - 1)
                else:
                    with pe.If(n > 0):
                        transpose_out(last_step(before(n)))
                if hp < NHP - 1:
                    project_tok(pe, n, hp + 1, s + 1, 0)
                else:
                    with pe.If(n < NBLK - 1):
                        project_tok(pe, after(n), 0, s + 1, 0)
                pe.wait_ge(a["probs_lo_done"], s + 1)
                for h in range(2):
                    for c in range(TPB):
                        at = h * BLK + c * P
                        v_c = (v_hi[:, 2 * c + h, :], v_lo[:, 2 * c + h, :])
                        three(ps_so[:, h, c * VZ:(c + 1) * VZ], tuple(p[:, at:at + P] for p in (probs_hi, probs_lo)),
                              v_c, c == 0, False)
                pe.wait_ge(a["q_lo_done"], s + 1)
                pe.wait_ge(a["s_lo_done"], s + 1)
                for h in range(2):
                    for c in range(TPB):
                        at, z = h * BLK + c * P, (2 * c + h) * VZ
                        i = three(ps_so[:, h, c * VZ:(c + 1) * VZ], tuple(q[:, at:at + P] for q in (q_hi, q_lo)),
                                  tuple(s_[:, z:z + VZ] for s_ in (s_hi, s_lo)), False, c == TPB - 1)
                i.then_inc(a["o_done"], 1)
                if hp < NHP - 1:
                    project_tok(pe, n, hp + 1, s + 1, 1)
                else:
                    with pe.If(n < NBLK - 1):
                        project_tok(pe, after(n), 0, s + 1, 1)
                if hp:
                    if hp == 1:
                        pe.wait_ge(a["att_sum"], n)
                    project_out(hp - 1, s - 1)
                else:
                    with pe.If(n > 0):
                        project_out(NHP - 1, last_step(before(n)))
                if hp == 4:
                    with pe.If(n > 0):
                        ln_transpose(pe, 1, before(n))
                if hp == 5:
                    with pe.If(n > 0):
                        gate_product(pe, 1, before(n))

            with pe.Fori(0, B) as b:
                with pe.Fori(0, UPB) as u:
                    n = b * UPB + u
                    for hp in range(NHP):
                        step_body(n, hp)
            transpose_out(last_step(NBLK - 1))
            project_out(NHP - 1, last_step(NBLK - 1))
            ln_transpose(pe, 1, NBLK - 1)
            gate_product(pe, 1, NBLK - 1)
            pe.wait_ge(gate_read, 2 * NBLK)

        def attention_act(act):
            def relu_q(hp, s, js):
                act.wait_ge(a["q_trig_done"], s)
                for j in js:
                    act.wait_ge(a["pq_done"], 3 * s + j + 1)
                    dst = q_relu[j] if j < 2 else k_relu
                    bias = bq_kept[:, 2 * hp + j:2 * hp + j + 1] if j < 2 else bkT_kept[:, hp:hp + 1]
                    nc.scalar.activation(dst, ps_pj[(5 * hp + j) % 2], ACT.Relu, bias=bias, scale=FEATURE
                                         ).then_inc(a["q_evac"], 1)

            def high(dst, src, ready, value, done, scale=1.0):
                act.wait_ge(ready, value)
                nc.scalar.activation(dst, src, ACT.Copy, scale=scale).then_inc(done, 1)

            def k_high(s):
                high(k_hi, k_trig, a["k_trig_done"], s + 1, a["k_hi_done"])

            def v_high(hp, s):
                high(v_hi[:, :, 0:DH], ps_pj[(5 * hp + 4) % 2].rearrange("p (c f) -> p c f", f=DH),
                     a["pv_done"], s + 1, a["v_hi_done"], FEATURE)

            def q_high(s):
                high(q_hi, arena_a[:, 0:2 * BLK], a["q_trig_done"], s + 1, a["q_hi_done"])

            def copy_out(s):
                act.wait_ge(a["otr_done"], s + 1)
                nc.scalar.activation(oT, ps_tr.bitcast(F16), ACT.Copy).then_inc(a["ot_copied"], 1)

            def ahead(n, hp, do):
                if hp < NHP - 1:
                    do(hp + 1)
                else:
                    with act.If(n < NBLK - 1):
                        do(0)

            relu_q(0, 0, range(3))
            k_high(0)
            act.wait_ge(a["s_zero"], 1)
            v_high(0, 0)
            q_high(0)
            with act.Fori(0, B) as b:
                with act.Fori(0, UPB) as u:
                    n = b * UPB + u
                    for hp in range(NHP):
                        s = NHP * n + hp
                        ahead(n, hp, lambda to: relu_q(to, s + 1, (0,)))
                        high(probs_hi, probs, a["probs_done"], s + 1, a["probs_hi_done"])
                        ahead(n, hp, lambda to: relu_q(to, s + 1, (1,)))
                        high(s_hi, s_pref, a["s_ready"], s + 1, a["s_hi_done"])
                        ahead(n, hp, lambda to: relu_q(to, s + 1, (2,)))
                        if hp:
                            copy_out(s - 1)
                        else:
                            with act.If(n > 0):
                                copy_out(last_step(before(n)))
                        ahead(n, hp, lambda to: k_high(s + 1))
                        ahead(n, hp, lambda to: v_high(to, s + 1))
                        high(o_hi, o32.rearrange("p c h f -> p (c h f)"), a["o32_done"], s + 1, a["o_hi_done"])
                        ahead(n, hp, lambda to: q_high(s + 1))
                        if hp == 4:
                            with act.If(n > 0):
                                ln_copy(act, 1, before(n))
            copy_out(last_step(NBLK - 1))
            ln_copy(act, 1, NBLK - 1)

        def attention_dve(v):
            def k_features(u, hp, s):
                keys = ps_pj[(5 * hp + 3) % 2].rearrange("p (c f) -> p c f", f=DH)
                to = k_trig.rearrange("p (c g f) -> p c g f", g=2, f=DH)
                wait_apart(v, a["pk_done"], s + 1)
                for g in range(2):
                    trig = trig_cols[:, g, bass.ds(u * TPB * 2, TPB * 2)].unsqueeze(2).to_broadcast([P, TPB * 2, DH])
                    i = nc.vector.scalar_tensor_tensor(to[:, :, g, :], keys, 0.0, trig, ALU.max, ALU.mult)
                i.then_inc(a["k_trig_done"], 1)

            def k_low(s):
                v.wait_ge(a["k_hi_done"], s + 1)
                nc.vector.tensor_tensor(k_lo, k_trig, k_hi, ALU.subtract).then_inc(a["k_lo_done"], 1)

            def v_low(hp, s):
                v.wait_ge(a["v_hi_done"], s + 1)
                nc.vector.scalar_tensor_tensor(
                    v_lo[:, :, 0:DH], ps_pj[(5 * hp + 4) % 2].rearrange("p (c f) -> p c f", f=DH), FEATURE,
                    v_hi[:, :, 0:DH], ALU.mult, ALU.subtract).then_inc(a["v_lo_done"], 1)

            def ahead(n, u, hp, do):
                if hp < NHP - 1:
                    do(u, hp + 1)
                else:
                    with v.If(n < NBLK - 1):
                        do(1 - u, 0)

            def step_body(n, u, hp):
                s = NHP * n + hp
                v.wait_ge(a["sc_done"], s + 1)
                for h in range(2):
                    i = nc.vector.tensor_tensor(probs[:, h * BLK:(h + 1) * BLK].rearrange("p (c i) -> p c i", c=TPB),
                                                ps_so[:, h, :].rearrange("p (c i) -> p c i", c=TPB),
                                                decay[:].unsqueeze(1).to_broadcast([P, TPB, P]), ALU.mult)
                i.then_inc(a["probs_done"], 1)
                run, pref = s_run[:, hp, :, :], s_pref.rearrange("p (c h f) -> p c h f", c=TPB, h=2)
                v.wait_ge(a["st_done"], s + 1)
                v.wait_ge(a["s_lo_done"], s)
                nc.vector.tensor_copy(pref[:, 0, :, :], run).then_inc(a["st_step"], 1)
                for c in range(TPB):
                    dst = pref[:, c + 1, :, :] if c < TPB - 1 else run
                    v.wait_ge(a["st_step"], TPB * s + c + 1)
                    nc.vector.scalar_tensor_tensor(dst, ps_st[:, :, c * VZ:(c + 1) * VZ], CORE, pref[:, c, :, :],
                                                   ALU.mult, ALU.add
                                                   ).then_inc(a["st_step"] if c < TPB - 1 else a["s_ready"], 1)
                v.wait_ge(a["probs_hi_done"], s + 1)
                nc.vector.tensor_tensor(probs_lo, probs, probs_hi, ALU.subtract).then_inc(a["probs_lo_done"], 1)
                ahead(n, u, hp, lambda u_, to: k_features(u_, to, s + 1))
                out = ps_so[:, :, 0:TPB * VZ].rearrange("p h (c z) -> p h c z", c=TPB)
                v.wait_ge(a["o_done"], s + 1)
                nc.vector.tensor_scalar(den, out[:, :, :, DH], 1.0 / ONE, s_eps[:, 0:1], ALU.mult, ALU.max
                                        ).then_inc(a["den_step"], 1)
                v.wait_ge(a["den_step"], 2 * s + 1)
                nc.vector.reciprocal(rden, den).then_inc(a["den_step"], 1)
                v.wait_ge(a["den_step"], 2 * s + 2)
                v.wait_ge(a["o_hi_done"], s)
                nc.vector.tensor_tensor(o32, out[:, :, :, 0:DH].rearrange("p h c f -> p c h f"),
                                        rden.rearrange("p h c -> p c h").unsqueeze(3).to_broadcast([P, TPB, 2, DH]),
                                        ALU.mult).then_inc(a["o32_done"], 1)
                ahead(n, u, hp, lambda u_, to: k_low(s + 1))
                ahead(n, u, hp, lambda u_, to: v_low(to, s + 1))
                v.wait_ge(a["o_hi_done"], s + 1)
                nc.vector.tensor_tensor(o_lo, o32.rearrange("p c h f -> p (c h f)"), o_hi, ALU.subtract
                                        ).then_inc(a["o_lo_done"], 1)

            nc.vector.memset(v_hi[:, :, DH:VZ], ONE)
            nc.vector.memset(v_lo[:, :, DH:VZ], 0.0).then_inc(a["s_zero"], 1)
            k_features(0, 0, 0)
            k_low(0)
            v_low(0, 0)
            with v.Fori(0, B) as b:
                nc.vector.memset(s_run, 0.0).then_inc(a["s_zero"], 1)
                wait_apart(v, a["s_zero"], b + 2)
                with v.Fori(0, UPB) as u:
                    n = b * UPB + u
                    for hp in range(NHP):
                        step_body(n, u, hp)
                        if hp == 0:
                            with v.If(n > 0):
                                add_attention(v, before(n))
                        if hp == 1:
                            with v.If(n > 0):
                                p = before(n)
                                v.wait_ge(a["att_x"], n)
                                ln_stats(v, 1, p)
                        if hp == 2:
                            with v.If(n > 0):
                                ln_apply(v, 1, before(n))
                        if hp == 5:
                            with v.If(n > 0):
                                p = before(n)
                                ln_low(v, 1, p)
                                gate_logits(v, 1, p)
            add_attention(v, NBLK - 1)
            v.wait_ge(a["att_x"], NBLK)
            ln_stats(v, 1, NBLK - 1)
            ln_apply(v, 1, NBLK - 1)
            ln_low(v, 1, NBLK - 1)
            gate_logits(v, 1, NBLK - 1)

        def add_attention(v, n):
            x = x_tok[:, bass.ds(n * TPB, TPB), :].rearrange("p t d -> p (t d)")
            v.wait_ge(a["op_done"], NHP * n + NHP)
            nc.vector.scalar_tensor_tensor(x, ps_op, s_att[:, 0:1], x, ALU.mult, ALU.add).then_inc(a["att_sum"], 1)

        def attention_pool(g):
            def trig_q(u, s):
                at_least(g, a["q_lo_done"], s)
                wait_apart(g, a["q_evac"], 3 * s + 2)
                for h in range(2):
                    i = nc.gpsimd.tensor_tensor(q_trig[h], q_relu[h], trig_rows[:, bass.ds(u * BLK, BLK)], ALU.mult)
                i.then_inc(a["q_trig_done"], 1)

            def add_bias(p):
                wait_apart(g, a["att_sum"], p + 1)
                x = x_tok[:, bass.ds(p * TPB, TPB), :]
                nc.gpsimd.tensor_tensor(x, x, bo_row[:].unsqueeze(1).to_broadcast([P, TPB, D]), ALU.add
                                        ).then_inc(a["att_x"], 1)

            g.wait_ge(in_tab, 16 * TABLES)
            trig_q(0, 0)
            with g.Fori(0, B) as b:
                with g.Fori(0, UPB) as u:
                    n = b * UPB + u
                    for hp in range(NHP):
                        s = NHP * n + hp
                        g.wait_ge(a["q_hi_done"], s + 1)
                        nc.gpsimd.tensor_tensor(q_lo, arena_a[:, 0:2 * BLK], q_hi, ALU.subtract
                                                ).then_inc(a["q_lo_done"], 1)
                        g.wait_ge(a["s_hi_done"], s + 1)
                        nc.gpsimd.tensor_tensor(s_lo, s_pref, s_hi, ALU.subtract).then_inc(a["s_lo_done"], 1)
                        if hp < NHP - 1:
                            trig_q(u, s + 1)
                        else:
                            with g.If(n < NBLK - 1):
                                trig_q(1 - u, s + 1)
                        if hp == 0:
                            with g.If(n > 0):
                                add_bias(before(n))
                        if hp == 1:
                            with g.If(n > 0):
                                ln_power(g, 1, before(n))
            add_bias(NBLK - 1)
            ln_power(g, 1, NBLK - 1)

        TINY = float(2.0 ** -99)

        def largest_of(v, col, src, last=False):
            i = nc.vector.tensor_reduce(largest[:, col:col + 1], src, AX_X, ALU.max, apply_absolute_value=True)
            if last:
                i.then_inc(max_part, 1)

        def reduce_largest(g, c0, c1, k):
            g.wait_ge(max_part, k + 1)
            nc.gpsimd.partition_all_reduce(largest_all[:, c0:c1], largest[:, c0:c1], P, RMAX).then_inc(max_all, 1)

        chain = [0]

        def link(v, ins):
            ins.then_inc(scale_step, 1)
            chain[0] += 1
            v.wait_ge(scale_step, chain[0])

        def power_of_two(v, col, src):
            at = slice(col, col + 1)
            link(v, nc.vector.tensor_scalar(s_tmp[:, 0:1], src, TINY, None, ALU.max))
            link(v, nc.vector.tensor_scalar(pow2[:, at].bitcast(I32), s_tmp[:, 0:1].bitcast(I32), 0x7F800000, None,
                                            ALU.bitwise_and))
            link(v, nc.vector.reciprocal(rpow2[:, at], pow2[:, at]))
            link(v, nc.vector.tensor_scalar(s_w[:, at], rpow2[:, at], 2.0 ** 14, None, ALU.mult))

        flat_dn_hi, flat_dn_lo = (w[:].rearrange("p c d -> p (c d)") for w in (wdn_hi, wdn_lo))

        def scale_up(v):
            v.wait_ge(max_all, 1)
            power_of_two(v, W_UP, largest_all[:, 0:1])
            link(v, nc.vector.tensor_scalar(s_pre[:], pow2[:, W_UP:W_UP + 1], 2.0 ** -25, None, ALU.mult))
            nc.vector.tensor_scalar(s_h[:], rpow2[:, W_UP:W_UP + 1], 2.0 ** 7, None, ALU.mult).then_inc(scale_ready, 1)

        def scale_down(v):
            v.wait_ge(max_all, 2)
            power_of_two(v, W_DOWN, largest_all[:, 1:2])
            link(v, nc.vector.tensor_scalar(s_tmp[:, 1:2], pow2[:, W_DOWN:W_DOWN + 1], 2.0 ** -21, None, ALU.mult))
            nc.vector.tensor_tensor(s_y[:], s_tmp[:, 1:2], pow2[:, W_UP:W_UP + 1], ALU.mult).then_inc(scale_ready, 1)

        def expert_weights_high(act):
            for k, (hi, raw, col) in enumerate(((wup_hi[:], arena_a[:], W_UP), (flat_dn_hi, arena_b[:], W_DOWN))):
                act.wait_ge(scale_ready, k + 1)
                nc.scalar.activation(hi, raw, ACT.Copy, scale=s_w[:, col:col + 1]).then_inc(split_hi, 1)

        def expert_weights_low(v, col):
            hi, lo, raw, ready = ((wup_hi[:], wup_lo[:], arena_a[:], w_up_ready),
                                  (flat_dn_hi, flat_dn_lo, arena_b[:], w_dn_ready))[col]
            v.wait_ge(split_hi, col + 1)
            nc.vector.scalar_tensor_tensor(lo, raw, s_w[:, col:col + 1], hi, ALU.mult, ALU.subtract).then_inc(ready, 1)

        ATT_SETUP_SLOTS = (1, 2, 3, 4, 9, 10, 11, 12, 13, 14, 15)

        def attention_weights(v, j):
            raw = [arena_a[:, i * HD:(i + 1) * HD] for i in range(4)]
            s_qkvw, s_outw = s_w[:, W_QKV:W_QKV + 1], s_w[:, W_OUT:W_OUT + 1]

            def both(hi, lo, src, scale):
                link(v, nc.vector.tensor_scalar(hi, src, scale, None, ALU.mult))
                return nc.vector.scalar_tensor_tensor(lo, src, scale, hi, ALU.mult, ALU.subtract)

            if j < 4:
                if j == 0:
                    v.wait_ge(in_att, 16 * 4)
                    v.wait_ge(in_tab, 16 * TABLES)
                    for col, bias in enumerate((bv_row, bk_row, bq_sb), 5):
                        largest_of(v, col, bias[:])
                largest_of(v, (2, 3, 4, 8)[j], raw[j], last=(j == 3))
            elif j == 4:
                v.wait_ge(max_all, 3)
                link(v, nc.vector.tensor_reduce(s_tmp[:, 1:2], largest_all[:, 2:8], AX_X, ALU.max))
                power_of_two(v, W_QKV, s_tmp[:, 1:2])
                power_of_two(v, W_OUT, largest_all[:, 8:9])
                link(v, nc.vector.tensor_scalar(s_feature[:], rpow2[:, W_QKV:W_QKV + 1], 2.0 ** 6, None, ALU.mult))
                link(v, nc.vector.tensor_scalar(bq_kept[:], bq_sb[:], s_feature[:, 0:1], None, ALU.mult))
                link(v, nc.vector.tensor_scalar(bkT_kept[:], bkT_sb[:], s_feature[:, 0:1], None, ALU.mult))
                link(v, nc.vector.tensor_tensor(s_eps[:], s_feature[:], s_feature[:], ALU.mult))
                link(v, nc.vector.tensor_scalar(s_eps[:], s_eps[:], DEN_EPS * CORE, 2.0 ** -100, ALU.mult, ALU.max))
                link(v, nc.vector.tensor_scalar(s_tmp[:, 1:2], pow2[:, W_OUT:W_OUT + 1], 2.0 ** -20, None, ALU.mult))
                link(v, nc.vector.tensor_tensor(s_att[:], s_tmp[:, 1:2], pow2[:, W_QKV:W_QKV + 1], ALU.mult))
            elif j < 7:
                g = j - 5
                both(wq_hi[:, :, g, :], wq_lo[:, :, g, :], raw[0].rearrange("p (h f) -> p h f", h=H), s_qkvw)
            elif j < 9:
                hi, lo = ((wk_hi, wk_lo), (wv_hi, wv_lo))[j - 7]
                both(hi[:], lo[:], raw[j - 6], s_qkvw)
            elif j == 9:
                link(v, both(wo_hi[:].rearrange("p n d -> p (n d)"), wo_lo[:].rearrange("p n d -> p (n d)"), raw[3], s_outw))
            else:
                link(v, nc.vector.tensor_tensor(part_row[:, 0:1], s_qkvw, ident[:, 1:2], ALU.mult))
                link(v, nc.vector.tensor_tensor(part_row[:, 1:2], ident[:, 0:1], ident[:, 1:2], ALU.subtract))
                for i, bias in enumerate((bk_row, bv_row)):
                    part = bias_part[:, i * HD:(i + 1) * HD]
                    link(v, nc.vector.tensor_scalar(part, bias[:], s_qkvw, None, ALU.mult))
                    link(v, nc.vector.tensor_scalar(bias[:], bias[:], part_row[:, 0:1], None, ALU.mult))
                    i = nc.vector.scalar_tensor_tensor(bias_rows[:, i, :], part[0:2, :], part_row[0:2, 1:2],
                                                       bias[0:2, :], ALU.mult, ALU.add)
                i.then_inc(w_att_ready, 1)

        small = ((ident[:], d["c_ident"]), (gate_sb[:], d["gate_w"]), (pick32, d["c_pick"]), (rank[:], d["c_rank"]),
                 (gbias[:], d["gbias"].partition_broadcast(P)))
        tables = ((bk_row[:], d["bk"].partition_broadcast(P)), (bv_row[:], d["bv"].partition_broadcast(P)),
                  (bo_row[:], d["bo"].partition_broadcast(P)), (bq_sb[:], d["bq2"]), (bkT_sb[:], d["bkT"]),
                  (trig_rows[:], d["c_trig_rows"]), (trig_cols[:].rearrange("p g t -> p (g t)"), d["c_trig_cols"]),
                  (decay[:], d["c_decay"]))
        TABLES = len(tables)

        @block.sync
        def _(sp):
            x = d["x"].rearrange("(t p) d -> p t d", p=P)
            for half in range(2):
                tiles = slice(half * HALF, (half + 1) * HALF)
                sp.dma_start(x_tok[:, tiles, :], x[:, tiles, :]).then_inc(in_x[half], 16)
            sp.dma_start(arena_a[:], d["w_up"]).then_inc(in_up, 16)
            sp.dma_start(arena_b[:], d["w_down"]).then_inc(in_dn, 16)
            for dst, src in tables:
                sp.dma_start(dst, src).then_inc(in_tab, 16)
            sp.wait_ge(w_up_ready, 1)
            for j, name in enumerate(("wq", "wk", "wv", "wo")):
                sp.dma_start(arena_a[:, j * HD:(j + 1) * HD], d[name]).then_inc(in_att, 16)
            with sp.Fori(0, NBLK) as n:
                sp.wait_ge(ffn[1]["fin_x"], n + 1)
                rows = d["out"].rearrange("(t p) d -> p t d", p=P)
                sp.dma_start(rows[:, bass.ds(n * TPB, TPB), :], x_tok[:, bass.ds(n * TPB, TPB), :]).then_inc(out_done, 16)
            sp.wait_ge(out_done, 16 * NBLK)

        @block.scalar
        def _(act):
            for dst, src in small:
                act.dma_start(dst, src).then_inc(in_const, 16)
            act.sem_inc(ln_hi, 1)
            first_copy(act)
            expert_weights_high(act)
            ffn_act(act, 0)
            attention_act(act)
            ffn_act(act, 1)

        @block.gpsimd
        def _(g):
            nc.gpsimd.memset(minus_half[:], -0.5)
            nc.gpsimd.memset(bias_one[:], BIAS_ONE)
            nc.gpsimd.memset(pick[:], 0.0)
            nc.gpsimd.memset(sw3[:], 0.0).then_inc(zeroed, 1)
            g.wait_ge(zeroed, 1)
            first_ln_power(g, 0)
            first_ln_power(g, 1)
            reduce_largest(g, 0, 1, 0)
            reduce_largest(g, 1, 2, 1)
            ffn_pool(g, 0)
            attention_pool(g)
            ffn_pool(g, 1)

        @block.vector
        def _(v):
            v.sem_inc(ln_lo, 1)
            first_ln_stats(v, 0)
            first_ln_stats(v, 1)
            v.wait_ge(in_const, 16 * len(small))
            v.wait_ge(zeroed, 1)
            nc.vector.tensor_copy(ident_h[:], ident[:])
            nc.vector.tensor_copy(ident_b[:], ident[:])
            nc.vector.tensor_copy(pick[0:SPLIT3 * E].rearrange("p e q -> p (e q)"), pick32).then_inc(const_ready, 1)
            v.wait_ge(in_up, 16)
            largest_of(v, 0, arena_a[:], last=True)
            first_ln_apply(v, 0)
            first_ln_apply(v, 1)
            scale_up(v)
            v.wait_ge(in_dn, 16)
            largest_of(v, 1, arena_b[:], last=True)
            first_low(v)
            first_logits(v)
            expert_weights_low(v, W_UP)
            scale_down(v)
            expert_weights_low(v, W_DOWN)
            ffn_dve(v, 0)
            attention_dve(v)
            ffn_dve(v, 1)

        @block.tensor
        def _(pe):
            pe.wait_ge(const_ready, 1)
            first_transpose(pe)
            pe.wait_ge(gate_read, NBLK)
            ffn_pe(pe, 0)
            attention_pe(pe)
            ffn_pe(pe, 1)


_ORDER = ("x", "wq", "wk", "wv", "wo", "bq2", "bkT", "bk", "bv", "bo", "gate_w", "gbias", "w_up", "w_down")


def kernel(L0_attn_x, L0_attn_Wq, L0_attn_bq, L0_attn_Wk, L0_attn_bk, L0_attn_Wv, L0_attn_bv, L0_attn_Wo, L0_attn_bo,
           L0_ffn_gate_w, L0_ffn_expert_bias, L0_ffn_w_up, L0_ffn_w_down):
    import concourse.bacc as bacc
    from concourse.bass_utils import run_bass_kernel_spmd

    bq = np.asarray(L0_attn_bq).reshape(H, DH).T
    arrays = {
        "x": np.asarray(L0_attn_x).reshape(NTOK, D),
        "wq": L0_attn_Wq, "wk": L0_attn_Wk, "wv": L0_attn_Wv,
        "wo": np.asarray(L0_attn_Wo).reshape(NHP, P, D).transpose(1, 0, 2).reshape(P, NHP * D),
        "bq2": np.concatenate([bq, bq], 0),
        "bkT": np.asarray(L0_attn_bk).reshape(NHP, P).T,
        "bk": L0_attn_bk, "bv": L0_attn_bv, "bo": L0_attn_bo,
        "gate_w": np.asarray(L0_ffn_gate_w).T,
        "gbias": L0_ffn_expert_bias,
        "w_up": np.asarray(L0_ffn_w_up).transpose(2, 0, 1).reshape(D, E * I),
        "w_down": np.asarray(L0_ffn_w_down).reshape(E, D, CH, P).transpose(3, 0, 2, 1).reshape(P, E * CH * D),
        **constants(),
    }
    arrays["c_trig_cols"] = arrays["c_trig_cols"].reshape(P, 4 * T // P)
    arrays = {n: np.ascontiguousarray(v) for n, v in arrays.items()}
    nc = bacc.Bacc("TRN2", target_bir_lowering=False, num_devices=1)
    d = {n: nc.dram_tensor(f"in_{n}", v.shape, mybir.dt.from_np(v.dtype), kind="ExternalInput").ap()
         for n, v in arrays.items()}
    d["out"] = nc.dram_tensor("out_x", (NTOK, D), F32, kind="ExternalOutput").ap()
    build(nc, d)
    r = run_bass_kernel_spmd(nc, [{f"in_{n}": v for n, v in arrays.items()}], core_ids=[0])
    return r.results[0]["out_x"].reshape(B, T, D)
```

```python
from contextlib import ExitStack

import numpy as np

import concourse.bass as bass
from concourse import mybir

P = 128
B, T, D = 4, 1024, 128
NTOK = B * T
NTILE = NTOK // P
TPB = 4
BLK = TPB * P
NBLK = NTOK // BLK
E, I = 8, 512
CH = I // P
PAIR = 2
NP = CH // PAIR
NPB = E * NP
H, DH = 16, 64
HD = H * DH
NHP = HD // P
VZ = DH + 1
UPB = T // BLK
LN_EPS, GATE_EPS, DEN_EPS = 1e-5, 1e-6, 1e-6
SPLIT3 = 3

F32, F16, BF16 = mybir.dt.float32, mybir.dt.float16, mybir.dt.bfloat16
I32 = mybir.dt.int32
ALU = mybir.AluOpType
ACT = mybir.ActivationFunctionType
AX_X = mybir.AxisListType.X
RMAX = bass.bass_isa.ReduceOp.max

CORE = 2.0 ** -23
ONE = 2.0 ** 14
FEATURE = 2.0 ** -19
BIAS_ONE = 2.0 ** 11
XSCALE = 4096.0
W_UP, W_DOWN, W_QKV, W_OUT = range(4)


def constants():
    f = np.float32
    angle = (f(np.pi / (2.0 * T)) * np.arange(T, dtype=f)).astype(f)
    cos, sin = np.cos(angle).astype(f), np.sin(angle).astype(f)
    trig_rows = np.concatenate([np.tile(cos, (DH, 1)), np.tile(sin, (DH, 1))], 0)
    trig_cols = np.stack([cos.reshape(-1, P).T, sin.reshape(-1, P).T], 1).astype(f)
    trig_cols = np.repeat(trig_cols[:, :, :, None], 2, 3)
    i, j = np.arange(P)[None, :], np.arange(P)[:, None]
    decay = np.where(j <= i, np.cos(np.pi / (2.0 * T) * (i - j)), 0.0).astype(f)
    pick = np.zeros((SPLIT3 * E, E, P), f)
    for e in range(E):
        for part in range(SPLIT3):
            pick[part * E + e, e] = 1.0
    return {
        "c_trig_rows": trig_rows,
        "c_trig_cols": trig_cols * f(FEATURE),
        "c_decay": decay * f(CORE),
        "c_ident": np.eye(P, dtype=f),
        "c_pick": pick.reshape(SPLIT3 * E, E * P),
        "c_rank": np.tile(np.arange(E, 0, -1, dtype=f), (P, 1)),
    }


def at_least(eng, sem, value):
    if isinstance(value, int) and value <= 0:
        return
    eng.wait_ge(sem, value)


def build(nc, d):
    with ExitStack() as ctx:
        def sb(name, shape, dt=F32):
            return ctx.enter_context(nc.sbuf_tensor(name, shape, dt))

        def sem(name):
            return ctx.enter_context(nc.semaphore(name))

        x_tok = sb("x_tok", [P, NTILE, D])
        xnh = sb("xnh", [P, NTILE, D])
        xT_hi = sb("xT_hi", [P, NTOK], F16)
        xT_lo = sb("xT_lo", [P, NTOK], F16)
        wup_hi, wup_lo = sb("wup_hi", [P, E * I], F16), sb("wup_lo", [P, E * I], F16)
        wdn_hi, wdn_lo = sb("wdn_hi", [P, E * CH, D], F16), sb("wdn_lo", [P, E * CH, D], F16)
        wq_hi, wq_lo = sb("wq_hi", [P, H, 2, DH], F16), sb("wq_lo", [P, H, 2, DH], F16)
        wk_hi, wk_lo = sb("wk_hi", [P, HD], F16), sb("wk_lo", [P, HD], F16)
        wv_hi, wv_lo = sb("wv_hi", [P, HD], F16), sb("wv_lo", [P, HD], F16)
        wo_hi, wo_lo = sb("wo_hi", [P, NHP, D], F16), sb("wo_lo", [P, NHP, D], F16)
        gate_sb = sb("gate_sb", [P, E])
        gbias = sb("gbias", [P, E])
        bq_sb = sb("bq_sb", [P, H])
        bkT_sb = sb("bkT_sb", [P, NHP])
        bk_row, bv_row, bo_row = sb("bk_row", [P, HD]), sb("bv_row", [P, HD]), sb("bo_row", [P, D])
        trig_rows = sb("trig_rows", [P, T])
        trig_cols = sb("trig_cols", [P, 2, 2 * T // P])
        decay = sb("decay", [P, P])
        ident = sb("ident", [P, P])
        ident_h = sb("ident_h", [P, P], F16)
        ident_b = sb("ident_b", [P, P], BF16)
        pick = sb("pick", [P, E, P], BF16)
        rank = sb("rank", [P, E])
        largest = sb("largest", [P, 9])
        largest_all = sb("largest_all", [P, 9])
        pow2 = sb("pow2", [P, 4])
        rpow2 = sb("rpow2", [P, 4])
        s_w = sb("s_w", [P, 4])
        s_pre = sb("s_pre", [P, 1])
        s_h = sb("s_h", [P, 1])
        s_y = sb("s_y", [P, 1])
        s_feature = sb("s_feature", [P, 1])
        s_eps = sb("s_eps", [P, 1])
        part_row = sb("part_row", [P, 2])
        bq_kept, bkT_kept = sb("bq_kept", [P, H]), sb("bkT_kept", [P, NHP])
        bias_one = sb("bias_one", [P, P], F16)
        s_att = sb("s_att", [P, 1])
        s_tmp = sb("s_tmp", [P, 2])
        logits = sb("logits", [P, NTILE, E])
        gw = sb("gw", [P, NTILE, E])
        gt = sb("gt", [P, NTILE, E])
        gsel = sb("gsel", [P, NTILE, E])
        gcol = sb("gcol", [P, 6, NTILE])
        sw3 = sb("sw3", [P, NTILE, P], BF16)
        sw3T = sb("sw3T", [P, NTOK], BF16)
        st6 = sb("st6", [P, TPB, 6])
        mv = sb("mv", [P, TPB, 2])
        var4 = sb("var4", [P, TPB])
        rstdh = sb("rstdh", [P, TPB])
        fmv = sb("fmv", [P, TPB, 2])
        fst6 = sb("fst6", [P, TPB, 6])
        fvar4 = sb("fvar4", [P, TPB])
        frstdh = sb("frstdh", [P, TPB])
        first_st6 = sb("first_st6", [P, NTILE, 6])
        first_mv = sb("first_mv", [P, NTILE, 2])
        first_var4 = sb("first_var4", [P, NTILE])
        first_rstdh = sb("first_rstdh", [P, NTILE])
        minus_half = sb("minus_half", [P, NTILE])
        xn_new = sb("xn_new", [P, TPB, D])
        xT32 = sb("xT32", [P, BLK])

        arena_a = sb("arena_a", [P, 4096])
        arena_b = sb("arena_b", [P, 4096])
        arena_c = sb("arena_c", [P, 6784])

        def carve(arena):
            at = [0]

            def take(n, dt=F32):
                words = n * mybir.dt.size(dt) // 4
                view = arena[:, at[0]:at[0] + words]
                at[0] += words
                assert at[0] <= arena.shape[1], at[0]
                return view if dt == F32 else view.bitcast(dt)
            return take

        take = carve(arena_c)
        h32 = [take(PAIR * BLK) for _ in range(2)]
        h_hi = [take(PAIR * BLK, F16) for _ in range(4)]
        h_lo = [take(PAIR * BLK, F16) for _ in range(4)]
        take = carve(arena_c)
        first_xT32 = [take(BLK) for _ in range(NBLK)]
        pick32 = take(E * P)[0:SPLIT3 * E, :]
        take = carve(arena_b)
        wb_sb = [take(BLK) for _ in range(2)]
        ytmp = [take(BLK) for _ in range(2)]
        acc = take(BLK)
        bias_part = take(HD, F16)
        zt = arena_b[:, 4096 - BLK:].rearrange("p (t d) -> p t d", t=TPB)

        take = carve(arena_a)
        q_trig = [take(BLK) for _ in range(2)]
        q_hi, q_lo = take(2 * BLK, F16), take(2 * BLK, F16)
        k_trig = take(TPB * 2 * P)
        bias_rows = take(2 * HD, F16).rearrange("p (j f) -> p j f", j=2)[0:2]
        take = carve(arena_b)
        q_relu = [take(BLK) for _ in range(2)]
        k_relu = take(BLK)
        probs = take(2 * BLK)
        probs_hi, probs_lo = take(2 * BLK, F16), take(2 * BLK, F16)
        take = carve(arena_c)
        k_hi, k_lo = take(TPB * 2 * P, F16), take(TPB * 2 * P, F16)
        v_hi, v_lo = (take(TPB * 2 * VZ, F16).rearrange("p (c h f) -> p (c h) f", c=TPB, h=2) for _ in range(2))
        o32 = take(BLK).rearrange("p (c h f) -> p c h f", c=TPB, h=2)
        o_hi, o_lo = take(BLK, F16), take(BLK, F16)
        oT = take(2 * BLK, F16)
        s_pref = take(TPB * 2 * VZ)
        s_hi, s_lo = take(TPB * 2 * VZ, F16), take(TPB * 2 * VZ, F16)
        s_run = take(NHP * 2 * VZ).rearrange("p (n h f) -> p n h f", n=NHP, h=2)
        den = take(2 * TPB).rearrange("p (h c) -> p h c", h=2)
        rden = take(2 * TPB).rearrange("p (h c) -> p h c", h=2)

        bank = [ctx.enter_context(nc.psum_tensor(f"bank{i}", [P, 2, BLK], F32)) for i in range(4)]
        ps_first = [bank[n // 2][:, n % 2, :] for n in range(NBLK)]
        ps_pre = [bank[0], bank[1]]
        ps_y = [bank[2][:, 0, :], bank[2][:, 1, :]]
        ps_wb = bank[3][:, 0, :]
        ps_tr = bank[3][:, 1, :]
        ps_so = bank[0]
        ps_st = bank[1]
        ps_pj = [bank[2][:, 0, :], bank[2][:, 1, :]]
        ps_op = bank[3][:, 0, :]

        in_x = [sem("in_x0"), sem("in_x1")]
        in_up, in_dn, in_att = sem("in_up"), sem("in_dn"), sem("in_att")
        in_const, in_tab = sem("in_const"), sem("in_tab")
        out_done = sem("out_done")
        zeroed = sem("zeroed")
        const_ready = sem("const_ready")
        first_stats, first_mean, first_var, first_rstd, first_norm, first_tr, first_hi, first_lo = (
            sem(f"first_{n}") for n in "stats mean var rstd norm tr hi lo".split())
        max_part, max_all = sem("max_part"), sem("max_all")
        scale_step = sem("scale_step")
        scale_ready = sem("scale_ready")
        split_hi = sem("split_hi")
        w_up_ready, w_dn_ready, w_att_ready = sem("w_up_ready"), sem("w_dn_ready"), sem("w_att_ready")
        ln_read, ln_mean, ln_var, ln_rstd, ln_norm = (sem(f"ln_{n}") for n in "read mean var rstd norm".split())
        ln_tr, ln_hi, ln_lo = (sem(n) for n in ("ln_tr", "ln_hi", "ln_lo"))
        gate_mm, gate_read = sem("gate_mm"), sem("gate_read")
        gate_step, gate_exp, gate_in = sem("gate_step"), sem("gate_exp"), sem("gate_in")
        sw_split, sw_tr, sw_copied = sem("sw_split"), sem("sw_tr"), sem("sw_copied")

        def ffn_sems(k):
            names = ("up_done gelu_done hi_act hi_dve lo_done down_done wb_mm wb_copied y_used "
                     "acc_done acc_tr fin_st fin_ag fin_var fin_rstd fin_z fin_sum fin_x").split()
            return {n: sem(f"{n}{k}") for n in names}

        ffn = [ffn_sems(0), ffn_sems(1)]
        names = ("pq_done pk_done pv_done q_evac q_trig_done q_hi_done q_lo_done k_trig_done k_hi_done "
                 "k_lo_done v_hi_done v_lo_done sc_done probs_done probs_hi_done probs_lo_done st_done st_step "
                 "s_ready s_hi_done s_lo_done o_done den_step o32_done o_hi_done o_lo_done otr_done "
                 "ot_copied op_done att_sum att_x s_zero").split()
        a = {n: sem(n) for n in names}

        passed = sem("passed")

        def give(eng, *sems):
            for s in sems:
                eng.sem_inc(s, 1)

        def wait_apart(eng, sem, value):
            eng.wait_ge(sem, value)
            eng.sem_inc(passed, 1)

        block = ctx.enter_context(nc.Block())

        def blk_cols(n):
            return bass.ds(n * BLK, BLK)

        def tile_of(t3, n, t):
            return t3[:, bass.ds(n * TPB + t, 1), :].rearrange("p a d -> p (a d)")

        def before(n):
            return nc.s_assert_within(n - 1, 0, NBLK - 2,
                                      skip_runtime_bounds_check_because="stands under If(n > 0)")

        def after(n):
            return nc.s_assert_within(n + 1, 1, NBLK - 1,
                                      skip_runtime_bounds_check_because="stands under If(n < NBLK - 1)")

        HALF = NTILE // 2
        TPI = 8

        def first_ln_stats(v, half):
            v.wait_ge(in_x[half], 16)
            for t in range(half * HALF, (half + 1) * HALF):
                i = nc.vector.bn_stats(first_st6[:, t, :], x_tok[:, t, :])
            i.then_inc(first_stats, 1)
            v.wait_ge(first_stats, half + 1)
            for t in range(half * HALF, (half + 1) * HALF):
                i = nc.vector.bn_aggr(first_mv[:, t, :], first_st6[:, t, :])
            i.then_inc(first_mean, 1)
            v.wait_ge(first_mean, half + 1)
            tiles = slice(half * HALF, (half + 1) * HALF)
            nc.vector.tensor_scalar(first_var4[:, tiles], first_mv[:, tiles, 1], LN_EPS, 4.0, ALU.add, ALU.mult
                                    ).then_inc(first_var, 1)

        def first_ln_power(g, half):
            g.wait_ge(first_var, half + 1)
            tiles = slice(half * HALF, (half + 1) * HALF)
            nc.gpsimd.tensor_tensor(first_rstdh[:, tiles], first_var4[:, tiles], minus_half[:, tiles], ALU.pow
                                    ).then_inc(first_rstd, 1)

        def first_ln_apply(v, half):
            v.wait_ge(first_rstd, half + 1)
            with v.Fori(half * HALF // TPI, (half + 1) * HALF // TPI) as i:
                for t in range(TPI):
                    tile = bass.ds(i * TPI + t, 1)
                    op = nc.vector.tensor_scalar(
                        xnh[:, tile, :].rearrange("p a d -> p (a d)"), x_tok[:, tile, :].rearrange("p a d -> p (a d)"),
                        first_mv[:, tile, 0:1].rearrange("p a s -> p (a s)"), first_rstdh[:, tile],
                        ALU.subtract, ALU.mult)
                    if t % TPB == TPB - 1:
                        op.then_inc(first_norm, 1)

        def first_transpose(pe):
            pe.wait_ge(in_const, 16 * len(small))
            for n in range(NBLK):
                pe.wait_ge(first_norm, n + 1)
                for t in range(TPB):
                    i = nc.tensor.transpose(ps_first[n][:, t * P:(t + 1) * P], xnh[:, n * TPB + t, :], ident[:])
                i.then_inc(first_tr, 1)
            for n in range(NBLK):
                pe.wait_ge(first_hi, n + 1)
                for t in range(TPB):
                    i = nc.tensor.matmul(ps_first[n][:, t * E:(t + 1) * E], first_xT32[n][:, t * P:(t + 1) * P],
                                         gate_sb[:], start=True, stop=True)
                i.then_inc(gate_mm, 1)

        def first_copy(act):
            for n in range(NBLK):
                act.wait_ge(first_tr, n + 1)
                nc.scalar.activation(first_xT32[n], ps_first[n], ACT.Copy, scale=XSCALE)
                nc.scalar.activation(xT_hi[:, n * BLK:(n + 1) * BLK], ps_first[n], ACT.Copy, scale=XSCALE
                                     ).then_inc(first_hi, 1)

        def first_low(g):
            for n in range(NBLK):
                g.wait_ge(first_hi, n + 1)
                cols = slice(n * BLK, (n + 1) * BLK)
                nc.gpsimd.tensor_tensor(xT_lo[:, cols], first_xT32[n], xT_hi[:, cols], ALU.subtract
                                        ).then_inc(first_lo, 1)

        def first_logits(v):
            for n in range(NBLK):
                v.wait_ge(gate_mm, n + 1)
                read_logits(v, n, ps_first[n], 2.0 / XSCALE)

        def read_logits(v, n, ps, scale=2.0):
            nc.vector.scalar_tensor_tensor(
                logits[:, bass.ds(n * TPB, TPB), :], ps[:, 0:TPB * E].rearrange("p (t e) -> p t e", t=TPB), scale,
                gbias[:].unsqueeze(1).to_broadcast([P, TPB, E]), ALU.mult, ALU.add).then_inc(gate_read, 1)

        def ln_stats(v, r, n):
            for t in range(TPB):
                i = nc.vector.bn_stats(st6[:, t, :], tile_of(x_tok, n, t))
            i.then_inc(ln_read, 1)
            wait_apart(v, ln_read, r * NBLK + n + 1)
            for t in range(TPB):
                i = nc.vector.bn_aggr(mv[:, t, :], st6[:, t, :])
            i.then_inc(ln_mean, 1)
            v.wait_ge(ln_mean, r * NBLK + n + 1)
            nc.vector.tensor_scalar(var4[:], mv[:, :, 1], LN_EPS, 4.0, ALU.add, ALU.mult).then_inc(ln_var, 1)

        def ln_power(g, r, n):
            g.wait_ge(ln_var, r * NBLK + n + 1)
            nc.gpsimd.tensor_tensor(rstdh[:], var4[:], minus_half[:, 0:TPB], ALU.pow).then_inc(ln_rstd, 1)

        def ln_apply(v, r, n):
            v.wait_ge(ln_rstd, r * NBLK + n + 1)
            v.wait_ge(ln_hi, r * NBLK + n + 1)
            for t in range(TPB):
                i = nc.vector.tensor_scalar(xn_new[:, t, :], tile_of(x_tok, n, t), mv[:, t, 0:1], rstdh[:, t:t + 1],
                                            ALU.subtract, ALU.mult)
            i.then_inc(ln_norm, 1)

        def ln_transpose(pe, r, n):
            pe.wait_ge(ln_norm, r * NBLK + n + 1)
            for t in range(TPB):
                i = nc.tensor.transpose(ps_tr[:, t * P:(t + 1) * P], xn_new[:, t, :], ident[:])
            i.then_inc(ln_tr, 1)

        def ln_copy(act, r, n):
            act.wait_ge(ln_lo, r * NBLK + n + 1)
            if r:
                act.wait_ge(gate_mm, NBLK + n)
            act.wait_ge(ln_tr, r * NBLK + n + 1)
            nc.scalar.activation(xT32[:], ps_tr, ACT.Copy)
            if r:
                nc.scalar.activation(xnh[:, bass.ds(n * TPB, TPB), :], xn_new[:], ACT.Copy)
            nc.scalar.activation(xT_hi[:, blk_cols(n)], ps_tr, ACT.Copy, scale=XSCALE).then_inc(ln_hi, 1)

        def ln_low(v, r, n):
            v.wait_ge(ln_hi, r * NBLK + n + 2)
            nc.vector.scalar_tensor_tensor(xT_lo[:, blk_cols(n)], xT32[:], XSCALE, xT_hi[:, blk_cols(n)],
                                           ALU.mult, ALU.subtract).then_inc(ln_lo, 1)

        def gate_product(pe, r, n):
            pe.wait_ge(ln_hi, r * NBLK + n + 2)
            for t in range(TPB):
                i = nc.tensor.matmul(ps_tr[:, t * E:(t + 1) * E], xT32[:, t * P:(t + 1) * P], gate_sb[:],
                                     start=True, stop=True)
            i.then_inc(gate_mm, 1)

        def gate_logits(v, r, n):
            v.wait_ge(gate_mm, r * NBLK + n + 1)
            read_logits(v, n, ps_tr)

        GATE_BLOCKS, GATE_UNITS = (2, 3), (5, 6)
        GATE_SLOTS = (0, 3, 6, 8, 10, 12)
        GATE_STEPS_OF_UNIT = (0, 2, 3, 4, 6, 7)
        assert GATE_BLOCKS[1] < NBLK // 2 <= GATE_UNITS[0]
        GATE_BEFORE = (0, 1, 3, 5, 7, 9, 11, 13, 15, 18, 20, 22)
        GATE_STEPS = 25

        def gating(v, i, j):
            tiles = slice((i % 2) * HALF, (i % 2 + 1) * HALF)
            lg, gw_, gt_, gs = logits[:, tiles, :], gw[:, tiles, :], gt[:, tiles, :], gsel[:, tiles, :]
            ranks = rank[:].unsqueeze(1).to_broadcast([P, HALF, E])

            step = [GATE_STEPS * i + GATE_BEFORE[j]]

            def then(ins):
                ins.then_inc(gate_step, 1)
                step[0] += 1
                v.wait_ge(gate_step, step[0])

            def col(c):
                return gcol[:, c, tiles]

            def wide(c):
                return col(c).unsqueeze(2).to_broadcast([P, HALF, E])

            if j == 0:
                v.wait_ge(gate_read, NBLK // 2 * (i + 1))
                then(nc.vector.tensor_reduce(col(0), lg, AX_X, ALU.max))
                nc.vector.tensor_tensor(gt_, lg, wide(0), ALU.subtract).then_inc(gate_in, 1)
            elif j == 1:
                v.wait_ge(gate_exp, i + 1)
                then(nc.vector.tensor_reduce(col(0), gw_, AX_X, ALU.add))
                then(nc.vector.reciprocal(col(1), col(0)))
            elif j == 2:
                then(nc.vector.tensor_tensor(gw_, gw_, wide(1), ALU.mult))
                then(nc.vector.tensor_reduce(col(2), gw_, AX_X, ALU.max))
            elif j == 3:
                then(nc.vector.tensor_tensor(gt_, gw_, wide(2), ALU.is_equal))
                then(nc.vector.tensor_tensor(gt_, gt_, ranks, ALU.mult))
            elif j == 4:
                then(nc.vector.tensor_reduce(col(3), gt_, AX_X, ALU.max))
                then(nc.vector.tensor_tensor(gs, gt_, wide(3), ALU.is_equal))
            elif j == 5:
                then(nc.vector.scalar_tensor_tensor(gt_, gs, -2.0, gw_, ALU.mult, ALU.add))
                then(nc.vector.tensor_reduce(col(4), gt_, AX_X, ALU.max))
            elif j == 6:
                then(nc.vector.tensor_tensor(gt_, gt_, wide(4), ALU.is_equal))
                then(nc.vector.tensor_tensor(gt_, gt_, ranks, ALU.mult))
            elif j == 7:
                then(nc.vector.tensor_reduce(col(3), gt_, AX_X, ALU.max))
                then(nc.vector.tensor_tensor(gt_, gt_, wide(3), ALU.is_equal))
            elif j == 8:
                then(nc.vector.tensor_tensor(gs, gs, gt_, ALU.add))
                then(nc.vector.scalar_tensor_tensor(col(5), col(2), GATE_EPS, col(4), ALU.add, ALU.add))
                then(nc.vector.reciprocal(col(5), col(5)))
            elif j == 9:
                then(nc.vector.tensor_tensor(gs, gs, gw_, ALU.mult))
                then(nc.vector.tensor_tensor(gs, gs, wide(5), ALU.mult))
            else:
                for part in ((0,), (1, 2))[j - 10]:
                    dst = sw3[:, tiles, part * E:(part + 1) * E]
                    then(nc.vector.tensor_copy(dst, gs))
                    last = nc.vector.tensor_tensor(gs, gs, dst, ALU.subtract)
                    if part < SPLIT3 - 1:
                        then(last)
                if j == GATE_PIECES - 1:
                    last.then_inc(sw_split, 1)
            assert step[0] == GATE_STEPS * i + (GATE_BEFORE + (GATE_STEPS,))[j + 1], (j, step[0])

        GATE_PIECES = 12

        def gating_exp(act, i):
            tiles = slice((i % 2) * HALF, (i % 2 + 1) * HALF)
            act.wait_ge(gate_in, i + 1)
            nc.scalar.activation(gw[:, tiles, :], gt[:, tiles, :], ACT.Exp).then_inc(gate_exp, 1)

        def gating_transpose(pe, i, q, ps):
            pe.wait_ge(sw_split, i + 1)
            at_least(pe, sw_copied, 2 * i + q)
            for t in range(8):
                tile = (i % 2) * HALF + q * 8 + t
                op = nc.tensor.transpose(ps.bitcast(BF16)[:, t * P:(t + 1) * P], sw3[:, tile, :], ident_b[:])
            op.then_inc(sw_tr, 1)

        def gating_copy(act, i, q, ps):
            at = ((i % 2) * HALF + q * 8) * P
            act.wait_ge(sw_tr, 2 * i + q + 1)
            nc.scalar.activation(sw3T[:, at:at + 8 * P], ps.bitcast(BF16), ACT.Copy).then_inc(sw_copied, 1)

        def only(eng, n, turn):
            return eng.If(n == turn)

        LAG = 3

        def up(pe, S, n, m):
            for c in range(PAIR):
                cols = slice((m * PAIR + c) * P, (m * PAIR + c + 1) * P)
                dst = ps_pre[m % 2][:, c, :]
                nc.tensor.matmul(dst, wup_hi[:, cols], xT_hi[:, blk_cols(n)], start=True, stop=False)
                nc.tensor.matmul(dst, wup_hi[:, cols], xT_lo[:, blk_cols(n)], start=False, stop=False)
                i = nc.tensor.matmul(dst, wup_lo[:, cols], xT_hi[:, blk_cols(n)], start=False, stop=True)
            i.then_inc(S["up_done"], 1)

        def down(pe, S, m):
            e, q = divmod(m, NP)
            for c in range(PAIR):
                w = m * PAIR + c
                hi, lo = (h[m % 4][:, c * BLK:(c + 1) * BLK] for h in (h_hi, h_lo))
                first, last = (q == 0 and c == 0), (q == NP - 1 and c == PAIR - 1)
                nc.tensor.matmul(ps_y[e % 2], wdn_hi[:, w, :], hi, start=first, stop=False)
                nc.tensor.matmul(ps_y[e % 2], wdn_hi[:, w, :], lo, start=False, stop=False)
                i = nc.tensor.matmul(ps_y[e % 2], wdn_lo[:, w, :], hi, start=False, stop=last)
            i.then_inc(S["down_done"], 1)

        def finish_transpose(pe, k, p):
            S = ffn[k]
            pe.wait_ge(S["acc_done"], (E - 1) * p + E)
            if k == 0:
                pe.wait_ge(ln_hi, p + 1)
            for t in range(TPB):
                i = nc.tensor.transpose(ps_tr[:, t * P:(t + 1) * P], acc[:, t * P:(t + 1) * P], ident[:])
            i.then_inc(S["acc_tr"], 1)

        def finish_stats(v, k, p):
            S = ffn[k]
            v.wait_ge(S["acc_tr"], p + 2)
            for t in range(TPB):
                i = nc.vector.bn_stats(fst6[:, t, :], ps_tr[:, t * P:(t + 1) * P])
            i.then_inc(S["fin_st"], 1)
            wait_apart(v, S["fin_st"], p + 1)
            for t in range(TPB):
                i = nc.vector.bn_aggr(fmv[:, t, :], fst6[:, t, :])
            i.then_inc(S["fin_ag"], 1)
            v.wait_ge(S["fin_ag"], p + 1)
            nc.vector.tensor_scalar(fvar4[:], fmv[:, :, 1], LN_EPS, 4.0, ALU.add, ALU.mult).then_inc(S["fin_var"], 1)

        def finish_apply(v, k, p):
            S = ffn[k]
            v.wait_ge(S["fin_rstd"], p + 1)
            for t in range(TPB):
                i = nc.vector.tensor_scalar(zt[:, t, :], ps_tr[:, t * P:(t + 1) * P], fmv[:, t, 0:1],
                                            frstdh[:, t:t + 1], ALU.subtract, ALU.mult)
            i.then_inc(S["fin_z"], 1)

        def finish_power(g, k, p):
            S = ffn[k]
            g.wait_ge(S["fin_var"], p + 1)
            nc.gpsimd.tensor_tensor(frstdh[:], fvar4[:], minus_half[:, 0:TPB], ALU.pow).then_inc(S["fin_rstd"], 1)

        def finish_sum(g, k, p):
            S = ffn[k]
            wait_apart(g, S["fin_z"], p + 1)
            tiles = bass.ds(p * TPB, TPB)
            nc.gpsimd.tensor_tensor(zt, zt, xnh[:, tiles, :], ALU.add).then_inc(S["fin_sum"], 1)
            wait_apart(g, S["fin_sum"], p + 1)
            nc.gpsimd.tensor_tensor(x_tok[:, tiles, :], x_tok[:, tiles, :], zt, ALU.add).then_inc(S["fin_x"], 1)

        def ffn_pe(pe, k):
            S = ffn[k]
            if k == 0:
                pe.wait_ge(w_up_ready, 1)
                pe.wait_ge(first_lo, NBLK)
            else:
                pe.wait_ge(ln_lo, NBLK + 2)
            for m in range(LAG):
                if m > 1:
                    pe.wait_ge(S["gelu_done"], m - 1)
                up(pe, S, 0, m)
            if k == 0:
                for q in range(2):
                    gating_transpose(pe, 0, q, ps_wb)
                pe.wait_ge(w_dn_ready, 1)
            else:
                pe.wait_ge(a["att_sum"], NBLK + 1)
            pe.wait_ge(sw_copied, 4 * k + 2)

            with pe.Fori(0, NBLK) as n:
                for m in range(NPB):
                    e = m // NP
                    if m % NP == 0:
                        pe.wait_ge(S["y_used"], E * n + e + 1)
                    pe.wait_ge(S["lo_done"], NPB * n + m + 1)
                    down(pe, S, m)
                    if m < NPB - LAG:
                        pe.wait_ge(S["gelu_done"], NPB * n + m + LAG - 1)
                        up(pe, S, n, m + LAG)
                    else:
                        with pe.If(n < NBLK - 1):
                            pe.wait_ge(S["gelu_done"], NPB * n + m + LAG - 1)
                            if m == NPB - LAG and k:
                                pe.wait_ge(ln_lo, NBLK + n + 3)
                            up(pe, S, after(n), m + LAG - NPB)
                    if m == 0:
                        with only(pe, n, GATE_BLOCKS[1] + 1):
                            pe.wait_ge(sw_copied, 4 * k + 4)
                    if m % NP == 0:
                        pe.wait_ge(S["wb_copied"], E * n + e + 1)
                        nc.tensor.matmul(ps_wb, pick[:, e, :], sw3T[:, blk_cols(n)], start=True, stop=True
                                         ).then_inc(S["wb_mm"], 1)
                    if m == 1:
                        with pe.If(n > 0):
                            finish_transpose(pe, k, before(n))
                    if m == 12 and k == 0:
                        with pe.If(n > 0):
                            pe.wait_ge(S["fin_z"], n)
                            ln_transpose(pe, 0, before(n))
                    if m == 12 and k:
                        with pe.If(n < 1):
                            ln_transpose(pe, 1, NBLK - 1)
                    if m == 14 and k:
                        with pe.If(n < 1):
                            gate_product(pe, 1, NBLK - 1)
                    if m in (14, 15):
                        with only(pe, n, GATE_BLOCKS[1]):
                            if k:
                                pe.wait_ge(S["fin_z"], GATE_BLOCKS[1])
                            else:
                                pe.wait_ge(ln_hi, GATE_BLOCKS[1] + 1)
                            gating_transpose(pe, 2 * k + 1, m - 14, ps_tr)
            if k:
                finish_transpose(pe, k, NBLK - 1)

        def ffn_act(act, k):
            S = ffn[k]

            def hidden(n, m):
                g = NPB * n + m
                act.wait_ge(S["up_done"], g + 1)
                at_least(act, S["lo_done"], g - 1)
                nc.scalar.activation(h32[m % 2], ps_pre[m % 2][:, :, :].rearrange("p c t -> p (c t)"), ACT.Gelu,
                                     scale=s_pre[:, 0:1]).then_inc(S["gelu_done"], 1)
                if m % 2 == 0:
                    act.wait_ge(S["gelu_done"], g + 1)
                    nc.scalar.activation(h_hi[m % 4], h32[m % 2], ACT.Copy, scale=s_h[:, 0:1]).then_inc(S["hi_act"], 1)

            for m in range(LAG):
                if m == LAG - 1 and k == 0:
                    for q in range(2):
                        gating_copy(act, 0, q, ps_wb)
                hidden(0, m)
            with act.Fori(0, NBLK) as n:
                for m in range(NPB):
                    if m < NPB - LAG:
                        hidden(n, m + LAG)
                    else:
                        with act.If(n < NBLK - 1):
                            hidden(n + 1, m + LAG - NPB)
                    if m == GATE_SLOTS[0] + 1:
                        with only(act, n, GATE_BLOCKS[0]):
                            gating_exp(act, 2 * k + 1)
                    if m in (14, 15):
                        with only(act, n, GATE_BLOCKS[1]):
                            gating_copy(act, 2 * k + 1, m - 14, ps_tr)
                    if m % NP == 0:
                        e = m // NP
                        act.wait_ge(S["y_used"], E * n + e + 1)
                        act.wait_ge(S["wb_mm"], E * n + e + 1)
                        nc.scalar.activation(wb_sb[e % 2], ps_wb, ACT.Copy, scale=s_y[:, 0:1]
                                             ).then_inc(S["wb_copied"], 1)
                    if m == 13 and k == 0:
                        with act.If(n > 0):
                            ln_copy(act, 0, before(n))
                    if m == 13 and k:
                        with act.If(n < 1):
                            ln_copy(act, 1, NBLK - 1)

        def ffn_dve(v, k):
            S = ffn[k]

            def split(n, m):
                g = NPB * n + m
                src, hi, lo = h32[m % 2], h_hi[m % 4], h_lo[m % 4]
                if m % 2 == 0:
                    v.wait_ge(S["hi_act"], (NPB // 2) * n + m // 2 + 1)
                else:
                    v.wait_ge(S["gelu_done"], g + 1)
                    nc.vector.tensor_scalar(hi, src, s_h[:, 0:1], None, ALU.mult).then_inc(S["hi_dve"], 1)
                    v.wait_ge(S["hi_dve"], (NPB // 2) * n + m // 2 + 1)
                nc.vector.scalar_tensor_tensor(lo, src, s_h[:, 0:1], hi, ALU.mult, ALU.subtract
                                               ).then_inc(S["lo_done"], 1)

            def combine(n, e):
                v.wait_ge(S["wb_copied"], E * n + e + 2)
                if e == 0:
                    v.wait_ge(S["acc_tr"], n + 1)
                    dst = acc
                else:
                    v.wait_ge(S["acc_done"], (E - 1) * n + max(e - 2, 0) + 1)
                    dst = ytmp[e % 2]
                v.wait_ge(S["down_done"], NPB * n + NP * (e + 1))
                nc.vector.tensor_tensor(dst, ps_y[e % 2], wb_sb[e % 2], ALU.mult).then_inc(S["y_used"], 1)

            for m in range(LAG):
                split(0, m)
            with v.Fori(0, NBLK) as n:
                for m in range(NPB):
                    for turn in range(2):
                        if (turn, m) in ATT_SETUP_SLOTS and k == 0:
                            with only(v, n, turn):
                                attention_weights(v, ATT_SETUP_SLOTS.index((turn, m)))
                    if m == 15 and k:
                        with v.If(n < 1):
                            gate_logits(v, 1, NBLK - 1)
                    if m % 2 == 1:
                        combine(n, m // NP)
                    if m < NPB - LAG:
                        split(n, m + LAG)
                    else:
                        with v.If(n < NBLK - 1):
                            split(n + 1, m + LAG - NPB)
                    if m == 2:
                        with v.If(n > 0):
                            finish_stats(v, k, before(n))
                    if m == 4:
                        with v.If(n > 0):
                            finish_apply(v, k, before(n))
                    if m == 7 and k == 0:
                        with v.If(n > 0):
                            p = before(n)
                            v.wait_ge(S["fin_x"], p + 1)
                            ln_stats(v, 0, p)
                    if m == 9 and k == 0:
                        with v.If(n > 0):
                            ln_apply(v, 0, before(n))
                    if m == 15 and k == 0:
                        with v.If(n > 0):
                            ln_low(v, 0, before(n))
                    if m in (7, 9, 14) and k:
                        with v.If(n < 1):
                            if m == 7:
                                v.wait_ge(a["att_x"], NBLK)
                            {7: ln_stats, 9: ln_apply, 14: ln_low}[m](v, 1, NBLK - 1)
                    if m in GATE_SLOTS:
                        for part, turn in enumerate(GATE_BLOCKS):
                            with only(v, n, turn):
                                gating(v, 2 * k + 1, part * len(GATE_SLOTS) + GATE_SLOTS.index(m))
            if k:
                finish_stats(v, k, NBLK - 1)
                finish_apply(v, k, NBLK - 1)

        def ffn_pool(g, k):
            S = ffn[k]

            def add(n, e):
                g.wait_ge(S["y_used"], E * n + e + 3)
                if e > 1:
                    g.wait_ge(S["acc_done"], (E - 1) * n + e)
                nc.gpsimd.tensor_tensor(acc, acc, ytmp[e % 2], ALU.add).then_inc(S["acc_done"], 1)

            with g.Fori(0, NBLK) as n:
                for e in range(E):
                    if e == 4 and k == 0:
                        with g.If(n > 0):
                            ln_power(g, 0, before(n))
                    if e == 4 and k:
                        with g.If(n < 1):
                            ln_power(g, 1, NBLK - 1)
                    if e:
                        add(n, e)
                    if e == 3 and k == 0:
                        with g.If(n < 1):
                            reduce_largest(g, 2, 9, 2)
                    if e == 1:
                        with g.If(n > 0):
                            finish_power(g, k, before(n))
                    if e == 2:
                        with g.If(n > 0):
                            finish_sum(g, k, before(n))
            finish_power(g, k, NBLK - 1)
            if k:
                finish_sum(g, k, NBLK - 1)

        def last_step(n):
            return NHP * n + NHP - 1

        def three(dst, lhs, rhs, first, last):
            nc.tensor.matmul(dst, lhs[0], rhs[0], start=first, stop=False, skip_group_check=True)
            nc.tensor.matmul(dst, lhs[0], rhs[1], start=False, stop=False, skip_group_check=True)
            return nc.tensor.matmul(dst, lhs[1], rhs[0], start=False, stop=last, skip_group_check=True)

        def project_q(pe, n, hp, s, js=range(3)):
            xs = (xT_hi[:, blk_cols(n)], xT_lo[:, blk_cols(n)])
            for j in js:
                if j == 0:
                    at_least(pe, a["k_trig_done"], s)
                elif j == 1:
                    at_least(pe, a["v_lo_done"], s)
                else:
                    pe.wait_ge(a["q_evac"], 3 * s + 1)
                dst = ps_pj[(5 * hp + j) % 2]
                if j < 2:
                    w = tuple(w[:, 2 * hp + j, :, :].rearrange("p g f -> p (g f)") for w in (wq_hi, wq_lo))
                else:
                    w = tuple(w[:, hp * P:(hp + 1) * P] for w in (wk_hi, wk_lo))
                three(dst, w, xs, True, True).then_inc(a["pq_done"], 1)

        def project_tok(pe, n, hp, s, j):
            pe.wait_ge(a["q_evac"], 3 * s + 2 + j)
            dst = ps_pj[(5 * hp + 3 + j) % 2]
            feats = slice(hp * P, (hp + 1) * P)
            w = tuple(w[:, feats] for w in ((wk_hi, wk_lo), (wv_hi, wv_lo))[j])
            for c in range(TPB):
                cols = bass.ds(n * BLK + c * P, P)
                to = dst[:, c * P:(c + 1) * P]
                nc.tensor.matmul(to, bias_one[0:2, :], bias_rows[:, j, feats], start=True, stop=False,
                                 skip_group_check=True)
                i = three(to, (xT_hi[:, cols], xT_lo[:, cols]), w, False, True)
            i.then_inc(a[("pk_done", "pv_done")[j]], 1)

        def attention_pe(pe):
            pe.wait_ge(w_att_ready, 1)
            pe.wait_ge(ln_lo, 2)
            pe.wait_ge(ffn[0]["y_used"], E * NBLK + 2)
            project_q(pe, 0, 0, 0)
            finish_transpose(pe, 0, NBLK - 1)
            project_tok(pe, 0, 0, 0, 0)
            project_tok(pe, 0, 0, 0, 1)

            def transpose_out(s):
                pe.wait_ge(a["o_lo_done"], s + 2)
                pe.wait_ge(a["o_hi_done"], s + 1)
                half = ps_tr.bitcast(F16)
                for part, src in enumerate((o_hi, o_lo)):
                    for c in range(TPB):
                        at = part * BLK + c * P
                        i = nc.tensor.transpose(half[:, at:at + P], src[:, c * P:(c + 1) * P], ident_h[:])
                i.then_inc(a["otr_done"], 1)

            def project_out(hp, s):
                pe.wait_ge(a["ot_copied"], s + 1)
                for c in range(TPB):
                    o_t = tuple(oT[:, part * BLK + c * P:part * BLK + (c + 1) * P] for part in range(2))
                    i = three(ps_op[:, c * P:(c + 1) * P], o_t, (wo_hi[:, hp, :], wo_lo[:, hp, :]),
                              hp == 0 and c == 0, hp == NHP - 1 and c == TPB - 1)
                i.then_inc(a["op_done"], 1)

            def step_body(n, hp):
                s = NHP * n + hp
                pe.wait_ge(a["q_evac"], 3 * s + 3)
                pe.wait_ge(a["o32_done"], s + 1)
                for c in range(TPB):
                    cols = slice(c * P, (c + 1) * P)
                    for h in range(2):
                        rows = slice(h * DH, (h + 1) * DH)
                        i = nc.tensor.matmul(ps_so[:, h, cols], k_relu[rows, cols], q_relu[h][rows, cols],
                                             start=True, stop=True)
                i.then_inc(a["sc_done"], 1)
                pe.wait_ge(a["v_lo_done"], s + 1)
                pe.wait_ge(a["k_lo_done"], s + 1)
                pe.wait_ge(a["s_ready"], s + 1)
                for h in range(2):
                    for c in range(TPB):
                        at = 2 * c + h
                        i = three(ps_st[:, h, c * VZ:(c + 1) * VZ], tuple(k[:, at * P:(at + 1) * P] for k in (k_hi, k_lo)),
                                  (v_hi[:, at, :], v_lo[:, at, :]), True, True)
                i.then_inc(a["st_done"], 1)
                if hp < NHP - 1:
                    project_q(pe, n, hp + 1, s + 1, (0, 1))
                else:
                    with pe.If(n < NBLK - 1):
                        pe.wait_ge(ln_lo, n + 3)
                        project_q(pe, after(n), 0, s + 1, (0, 1))
                if hp:
                    if hp == 1:
                        pe.wait_ge(ffn[0]["fin_z"], NBLK)
                    if hp == 5:
                        pe.wait_ge(ln_hi, NBLK + n + 1)
                    if hp == 6:
                        pe.wait_ge(gate_read, NBLK + n)
                    transpose_out(s - 1)
                else:
                    with pe.If(n > 0):
                        transpose_out(last_step(before(n)))
                if hp < NHP - 1:
                    project_q(pe, n, hp + 1, s + 1, (2,))
                    project_tok(pe, n, hp + 1, s + 1, 0)
                else:
                    with pe.If(n < NBLK - 1):
                        project_q(pe, after(n), 0, s + 1, (2,))
                        project_tok(pe, after(n), 0, s + 1, 0)
                pe.wait_ge(a["probs_lo_done"], s + 1)
                for h in range(2):
                    for c in range(TPB):
                        at = h * BLK + c * P
                        v_c = (v_hi[:, 2 * c + h, :], v_lo[:, 2 * c + h, :])
                        three(ps_so[:, h, c * VZ:(c + 1) * VZ], tuple(p[:, at:at + P] for p in (probs_hi, probs_lo)),
                              v_c, c == 0, False)
                pe.wait_ge(a["q_lo_done"], s + 1)
                pe.wait_ge(a["s_lo_done"], s + 2)
                for h in range(2):
                    for c in range(TPB):
                        at, z = h * BLK + c * P, (2 * c + h) * VZ
                        i = three(ps_so[:, h, c * VZ:(c + 1) * VZ], tuple(q[:, at:at + P] for q in (q_hi, q_lo)),
                                  tuple(s_[:, z:z + VZ] for s_ in (s_hi, s_lo)), False, c == TPB - 1)
                i.then_inc(a["o_done"], 1)
                if hp < NHP - 1:
                    project_tok(pe, n, hp + 1, s + 1, 1)
                else:
                    with pe.If(n < NBLK - 1):
                        project_tok(pe, after(n), 0, s + 1, 1)
                if hp:
                    if hp == 1:
                        pe.wait_ge(a["att_sum"], n + 1)
                    project_out(hp - 1, s - 1)
                else:
                    with pe.If(n > 0):
                        project_out(NHP - 1, last_step(before(n)))
                if hp == 4:
                    with pe.If(n > 0):
                        ln_transpose(pe, 1, before(n))
                    with pe.If(n < 1):
                        ln_transpose(pe, 0, NBLK - 1)
                if hp == 5:
                    with pe.If(n > 0):
                        gate_product(pe, 1, before(n))
                if hp in (6, 7):
                    with only(pe, n, GATE_UNITS[1] + 1):
                        gating_transpose(pe, 2, hp - 6, ps_tr)

            with pe.Fori(0, B) as b:
                with pe.Fori(0, UPB) as u:
                    n = b * UPB + u
                    for hp in range(NHP):
                        step_body(n, hp)
            transpose_out(last_step(NBLK - 1))
            project_out(NHP - 1, last_step(NBLK - 1))

        def attention_act(act):
            def relu_q(hp, s, js):
                act.wait_ge(a["q_trig_done"], s)
                for j in js:
                    act.wait_ge(a["pq_done"], 3 * s + j + 1)
                    dst = q_relu[j] if j < 2 else k_relu
                    bias = bq_kept[:, 2 * hp + j:2 * hp + j + 1] if j < 2 else bkT_kept[:, hp:hp + 1]
                    nc.scalar.activation(dst, ps_pj[(5 * hp + j) % 2], ACT.Relu, bias=bias, scale=FEATURE
                                         ).then_inc(a["q_evac"], 1)

            def high(dst, src, ready, value, done, scale=1.0):
                act.wait_ge(ready, value)
                nc.scalar.activation(dst, src, ACT.Copy, scale=scale).then_inc(done, 1)

            def k_high(s):
                high(k_hi, k_trig, a["k_trig_done"], s + 1, a["k_hi_done"])

            def v_high(hp, s):
                high(v_hi[:, :, 0:DH], ps_pj[(5 * hp + 4) % 2].rearrange("p (c f) -> p c f", f=DH),
                     a["pv_done"], s + 1, a["v_hi_done"], FEATURE)

            def q_high(s):
                high(q_hi, arena_a[:, 0:2 * BLK], a["q_trig_done"], s + 1, a["q_hi_done"])

            def copy_out(s):
                act.wait_ge(a["otr_done"], s + 1)
                nc.scalar.activation(oT, ps_tr.bitcast(F16), ACT.Copy).then_inc(a["ot_copied"], 1)

            def ahead(n, hp, do):
                if hp < NHP - 1:
                    do(hp + 1)
                else:
                    with act.If(n < NBLK - 1):
                        do(0)

            act.wait_ge(ffn[0]["acc_done"], (E - 1) * NBLK)
            relu_q(0, 0, range(3))
            k_high(0)
            act.wait_ge(a["s_zero"], 1)
            v_high(0, 0)
            q_high(0)
            with act.Fori(0, B) as b:
                with act.Fori(0, UPB) as u:
                    n = b * UPB + u
                    for hp in range(NHP):
                        s = NHP * n + hp
                        for h in range(2):
                            of = slice(h * BLK, (h + 1) * BLK)
                            high(probs_hi[:, of], probs[:, of], a["probs_done"], 2 * s + h + 1, a["probs_hi_done"])
                            ahead(n, hp, lambda to: relu_q(to, s + 1, (h,)))
                        high(s_hi, s_pref, a["s_ready"], s + 2, a["s_hi_done"])
                        ahead(n, hp, lambda to: relu_q(to, s + 1, (2,)))
                        if hp:
                            copy_out(s - 1)
                        else:
                            with act.If(n > 0):
                                copy_out(last_step(before(n)))
                        ahead(n, hp, lambda to: k_high(s + 1))
                        ahead(n, hp, lambda to: v_high(to, s + 1))
                        if hp in (6, 7):
                            with only(act, n, GATE_UNITS[1] + 1):
                                gating_copy(act, 2, hp - 6, ps_tr)
                        high(o_hi, o32.rearrange("p c h f -> p (c h f)"), a["o32_done"], s + 2, a["o_hi_done"])
                        ahead(n, hp, lambda to: q_high(s + 1))
                        if hp == 0:
                            with only(act, n, GATE_UNITS[0]):
                                gating_exp(act, 2)
                        if hp == 4:
                            with act.If(n > 0):
                                ln_copy(act, 1, before(n))
                            with act.If(n < 1):
                                ln_copy(act, 0, NBLK - 1)
            copy_out(last_step(NBLK - 1))

        def attention_dve(v):
            def k_features(u, hp, s):
                keys = ps_pj[(5 * hp + 3) % 2].rearrange("p (c f) -> p c f", f=DH)
                to = k_trig.rearrange("p (c g f) -> p c g f", g=2, f=DH)
                wait_apart(v, a["pk_done"], s + 1)
                for g in range(2):
                    trig = trig_cols[:, g, bass.ds(u * TPB * 2, TPB * 2)].unsqueeze(2).to_broadcast([P, TPB * 2, DH])
                    i = nc.vector.scalar_tensor_tensor(to[:, :, g, :], keys, 0.0, trig, ALU.max, ALU.mult)
                i.then_inc(a["k_trig_done"], 1)

            def k_low(s):
                v.wait_ge(a["k_hi_done"], s + 1)
                nc.vector.tensor_tensor(k_lo, k_trig, k_hi, ALU.subtract).then_inc(a["k_lo_done"], 1)

            def v_low(hp, s):
                v.wait_ge(a["v_hi_done"], s + 1)
                nc.vector.scalar_tensor_tensor(
                    v_lo[:, :, 0:DH], ps_pj[(5 * hp + 4) % 2].rearrange("p (c f) -> p c f", f=DH), FEATURE,
                    v_hi[:, :, 0:DH], ALU.mult, ALU.subtract).then_inc(a["v_lo_done"], 1)

            def ahead(n, u, hp, do):
                if hp < NHP - 1:
                    do(u, hp + 1)
                else:
                    with v.If(n < NBLK - 1):
                        do(1 - u, 0)

            def step_body(n, u, hp):
                s = NHP * n + hp
                v.wait_ge(a["sc_done"], s + 1)
                for h in range(2):
                    i = nc.vector.tensor_tensor(probs[:, h * BLK:(h + 1) * BLK].rearrange("p (c i) -> p c i", c=TPB),
                                                ps_so[:, h, :].rearrange("p (c i) -> p c i", c=TPB),
                                                decay[:].unsqueeze(1).to_broadcast([P, TPB, P]), ALU.mult)
                    i.then_inc(a["probs_done"], 1)
                run, pref = s_run[:, hp, :, :], s_pref.rearrange("p (c h f) -> p c h f", c=TPB, h=2)
                v.wait_ge(a["st_done"], s + 1)
                v.wait_ge(a["s_lo_done"], s + 1)
                nc.vector.tensor_copy(pref[:, 0, :, :], run).then_inc(a["st_step"], 1)
                for c in range(TPB):
                    dst = pref[:, c + 1, :, :] if c < TPB - 1 else run
                    v.wait_ge(a["st_step"], TPB * s + c + 1)
                    nc.vector.scalar_tensor_tensor(dst, ps_st[:, :, c * VZ:(c + 1) * VZ], CORE, pref[:, c, :, :],
                                                   ALU.mult, ALU.add
                                                   ).then_inc(a["st_step"] if c < TPB - 1 else a["s_ready"], 1)
                v.wait_ge(a["probs_hi_done"], 2 * s + 2)
                nc.vector.tensor_tensor(probs_lo, probs, probs_hi, ALU.subtract).then_inc(a["probs_lo_done"], 1)
                beside(n, hp)
                ahead(n, u, hp, lambda u_, to: k_features(u_, to, s + 1))
                out = ps_so[:, :, 0:TPB * VZ].rearrange("p h (c z) -> p h c z", c=TPB)
                v.wait_ge(a["o_done"], s + 1)
                nc.vector.tensor_scalar(den, out[:, :, :, DH], 1.0 / ONE, s_eps[:, 0:1], ALU.mult, ALU.max
                                        ).then_inc(a["den_step"], 1)
                v.wait_ge(a["den_step"], 2 * s + 1)
                nc.vector.reciprocal(rden, den).then_inc(a["den_step"], 1)
                v.wait_ge(a["den_step"], 2 * s + 2)
                v.wait_ge(a["o_lo_done"], s + 1)
                nc.vector.tensor_tensor(o32, out[:, :, :, 0:DH].rearrange("p h c f -> p c h f"),
                                        rden.rearrange("p h c -> p c h").unsqueeze(3).to_broadcast([P, TPB, 2, DH]),
                                        ALU.mult).then_inc(a["o32_done"], 1)
                ahead(n, u, hp, lambda u_, to: k_low(s + 1))
                ahead(n, u, hp, lambda u_, to: v_low(to, s + 1))

            def beside(n, hp):
                if hp == 1:
                    with v.If(n > 0):
                        v.wait_ge(a["att_x"], n)
                        ln_stats(v, 1, before(n))
                    with v.If(n < 1):
                        v.wait_ge(ffn[0]["fin_x"], NBLK)
                        ln_stats(v, 0, NBLK - 1)
                if hp in (2, 5):
                    do = ln_apply if hp == 2 else ln_low
                    with v.If(n > 0):
                        do(v, 1, before(n))
                    with v.If(n < 1):
                        do(v, 0, NBLK - 1)
                if hp in GATE_STEPS_OF_UNIT:
                    for part, unit in enumerate(GATE_UNITS):
                        with only(v, n, unit):
                            gating(v, 2, part * len(GATE_STEPS_OF_UNIT) + GATE_STEPS_OF_UNIT.index(hp))

            nc.vector.memset(v_hi[:, :, DH:VZ], ONE)
            nc.vector.memset(v_lo[:, :, DH:VZ], 0.0).then_inc(a["s_zero"], 1)
            finish_stats(v, 0, NBLK - 1)
            k_features(0, 0, 0)
            k_low(0)
            v_low(0, 0)
            finish_apply(v, 0, NBLK - 1)
            with v.Fori(0, B) as b:
                nc.vector.memset(s_run, 0.0).then_inc(a["s_zero"], 1)
                wait_apart(v, a["s_zero"], b + 2)
                with v.Fori(0, UPB) as u:
                    n = b * UPB + u
                    for hp in range(NHP):
                        step_body(n, u, hp)
                        if hp == 0:
                            with v.If(n > 0):
                                add_attention(v, before(n))
                        if hp == 5:
                            with v.If(n > 0):
                                gate_logits(v, 1, before(n))
            add_attention(v, NBLK - 1)

        def add_attention(v, n):
            x = x_tok[:, bass.ds(n * TPB, TPB), :].rearrange("p t d -> p (t d)")
            v.wait_ge(a["op_done"], NHP * n + NHP)
            nc.vector.scalar_tensor_tensor(x, ps_op, s_att[:, 0:1], x, ALU.mult, ALU.add).then_inc(a["att_sum"], 1)

        def attention_pool(g):
            def trig_q(u, s):
                at_least(g, a["q_lo_done"], s)
                wait_apart(g, a["q_evac"], 3 * s + 2)
                for h in range(2):
                    i = nc.gpsimd.tensor_tensor(q_trig[h], q_relu[h], trig_rows[:, bass.ds(u * BLK, BLK)], ALU.mult)
                i.then_inc(a["q_trig_done"], 1)

            def add_bias(p):
                wait_apart(g, a["att_sum"], p + 2)
                x = x_tok[:, bass.ds(p * TPB, TPB), :]
                nc.gpsimd.tensor_tensor(x, x, bo_row[:].unsqueeze(1).to_broadcast([P, TPB, D]), ALU.add
                                        ).then_inc(a["att_x"], 1)

            g.wait_ge(in_tab, 16 * TABLES)
            trig_q(0, 0)
            finish_sum(g, 0, NBLK - 1)
            with g.Fori(0, B) as b:
                with g.Fori(0, UPB) as u:
                    n = b * UPB + u
                    for hp in range(NHP):
                        s = NHP * n + hp
                        g.wait_ge(a["q_hi_done"], s + 1)
                        nc.gpsimd.tensor_tensor(q_lo, arena_a[:, 0:2 * BLK], q_hi, ALU.subtract
                                                ).then_inc(a["q_lo_done"], 1)
                        g.wait_ge(a["s_hi_done"], s + 1)
                        nc.gpsimd.tensor_tensor(s_lo, s_pref, s_hi, ALU.subtract).then_inc(a["s_lo_done"], 1)
                        if hp < NHP - 1:
                            trig_q(u, s + 1)
                        else:
                            with g.If(n < NBLK - 1):
                                trig_q(1 - u, s + 1)
                        g.wait_ge(a["o_hi_done"], s + 1)
                        nc.gpsimd.tensor_tensor(o_lo, o32.rearrange("p c h f -> p (c h f)"), o_hi, ALU.subtract
                                                ).then_inc(a["o_lo_done"], 1)
                        if hp == 0:
                            with g.If(n > 0):
                                add_bias(before(n))
                        if hp == 1:
                            with g.If(n > 0):
                                ln_power(g, 1, before(n))
                            with g.If(n < 1):
                                ln_power(g, 0, NBLK - 1)
            add_bias(NBLK - 1)

        TINY = float(2.0 ** -99)

        def largest_of(v, col, src, last=False):
            i = nc.vector.tensor_reduce(largest[:, col:col + 1], src, AX_X, ALU.max, apply_absolute_value=True)
            if last:
                i.then_inc(max_part, 1)

        def reduce_largest(g, c0, c1, k):
            g.wait_ge(max_part, k + 1)
            nc.gpsimd.partition_all_reduce(largest_all[:, c0:c1], largest[:, c0:c1], P, RMAX).then_inc(max_all, 1)

        chain = [0]

        def link(v, ins):
            ins.then_inc(scale_step, 1)
            chain[0] += 1
            v.wait_ge(scale_step, chain[0])

        def power_of_two(v, col, src):
            at = slice(col, col + 1)
            link(v, nc.vector.tensor_scalar(s_tmp[:, 0:1], src, TINY, None, ALU.max))
            link(v, nc.vector.tensor_scalar(pow2[:, at].bitcast(I32), s_tmp[:, 0:1].bitcast(I32), 0x7F800000, None,
                                            ALU.bitwise_and))
            link(v, nc.vector.reciprocal(rpow2[:, at], pow2[:, at]))
            link(v, nc.vector.tensor_scalar(s_w[:, at], rpow2[:, at], 2.0 ** 14, None, ALU.mult))

        flat_dn_hi, flat_dn_lo = (w[:].rearrange("p c d -> p (c d)") for w in (wdn_hi, wdn_lo))

        def scale_up(v):
            v.wait_ge(max_all, 1)
            power_of_two(v, W_UP, largest_all[:, 0:1])
            link(v, nc.vector.tensor_scalar(s_pre[:], pow2[:, W_UP:W_UP + 1], 2.0 ** -25, None, ALU.mult))
            nc.vector.tensor_scalar(s_h[:], rpow2[:, W_UP:W_UP + 1], 2.0 ** 7, None, ALU.mult).then_inc(scale_ready, 1)

        def scale_down(v):
            v.wait_ge(max_all, 2)
            power_of_two(v, W_DOWN, largest_all[:, 1:2])
            link(v, nc.vector.tensor_scalar(s_tmp[:, 1:2], pow2[:, W_DOWN:W_DOWN + 1], 2.0 ** -21, None, ALU.mult))
            nc.vector.tensor_tensor(s_y[:], s_tmp[:, 1:2], pow2[:, W_UP:W_UP + 1], ALU.mult).then_inc(scale_ready, 1)

        def expert_weights_high(act):
            for k, (hi, raw, col) in enumerate(((wup_hi[:], arena_a[:], W_UP), (flat_dn_hi, arena_b[:], W_DOWN))):
                act.wait_ge(scale_ready, k + 1)
                nc.scalar.activation(hi, raw, ACT.Copy, scale=s_w[:, col:col + 1]).then_inc(split_hi, 1)

        def expert_weights_low(v, col):
            hi, lo, raw, ready = ((wup_hi[:], wup_lo[:], arena_a[:], w_up_ready),
                                  (flat_dn_hi, flat_dn_lo, arena_b[:], w_dn_ready))[col]
            v.wait_ge(split_hi, col + 1)
            nc.vector.scalar_tensor_tensor(lo, raw, s_w[:, col:col + 1], hi, ALU.mult, ALU.subtract).then_inc(ready, 1)

        ATT_SETUP_SLOTS = ((0, 0), (0, 2), (0, 4), (0, 6), (0, 10), (0, 12), (0, 14),
                           (1, 0), (1, 6), (1, 8), (1, 10), (1, 12))

        LINKS, LINKS_BEFORE = 10, (0, 0, 0, 0, 0, 16, 17, 18, 19, 20, 22, 27, 31)

        def attention_weights(v, j):
            chain[0] = LINKS + LINKS_BEFORE[j]
            raw = [arena_a[:, i * HD:(i + 1) * HD] for i in range(4)]
            s_qkvw, s_outw = s_w[:, W_QKV:W_QKV + 1], s_w[:, W_OUT:W_OUT + 1]

            def both(hi, lo, src, scale):
                link(v, nc.vector.tensor_scalar(hi, src, scale, None, ALU.mult))
                return nc.vector.scalar_tensor_tensor(lo, src, scale, hi, ALU.mult, ALU.subtract)

            if j < 4:
                if j == 0:
                    v.wait_ge(in_att, 16 * 4)
                    v.wait_ge(in_tab, 16 * TABLES)
                    for col, bias in enumerate((bv_row, bk_row, bq_sb), 5):
                        largest_of(v, col, bias[:])
                largest_of(v, (2, 3, 4, 8)[j], raw[j], last=(j == 3))
            elif j == 4:
                v.wait_ge(max_all, 3)
                link(v, nc.vector.tensor_reduce(s_tmp[:, 1:2], largest_all[:, 2:8], AX_X, ALU.max))
                power_of_two(v, W_QKV, s_tmp[:, 1:2])
                power_of_two(v, W_OUT, largest_all[:, 8:9])
                link(v, nc.vector.tensor_scalar(s_feature[:], rpow2[:, W_QKV:W_QKV + 1], 2.0 ** 6, None, ALU.mult))
                link(v, nc.vector.tensor_scalar(bq_kept[:], bq_sb[:], s_feature[:, 0:1], None, ALU.mult))
                link(v, nc.vector.tensor_scalar(bkT_kept[:], bkT_sb[:], s_feature[:, 0:1], None, ALU.mult))
                link(v, nc.vector.tensor_tensor(s_eps[:], s_feature[:], s_feature[:], ALU.mult))
                link(v, nc.vector.tensor_scalar(s_eps[:], s_eps[:], DEN_EPS * CORE, 2.0 ** -100, ALU.mult, ALU.max))
                link(v, nc.vector.tensor_scalar(s_tmp[:, 1:2], pow2[:, W_OUT:W_OUT + 1], 2.0 ** -20, None, ALU.mult))
                link(v, nc.vector.tensor_tensor(s_att[:], s_tmp[:, 1:2], pow2[:, W_QKV:W_QKV + 1], ALU.mult))
            elif j < 7:
                g = j - 5
                both(wq_hi[:, :, g, :], wq_lo[:, :, g, :], raw[0].rearrange("p (h f) -> p h f", h=H), s_qkvw)
            elif j < 9:
                hi, lo = ((wk_hi, wk_lo), (wv_hi, wv_lo))[j - 7]
                both(hi[:], lo[:], raw[j - 6], s_qkvw)
            elif j == 9:
                link(v, both(wo_hi[:].rearrange("p n d -> p (n d)"), wo_lo[:].rearrange("p n d -> p (n d)"), raw[3], s_outw))
            else:
                link(v, nc.vector.tensor_tensor(part_row[:, 0:1], s_qkvw, ident[:, 1:2], ALU.mult))
                link(v, nc.vector.tensor_tensor(part_row[:, 1:2], ident[:, 0:1], ident[:, 1:2], ALU.subtract))
                i = j - 10
                bias = (bk_row, bv_row)[i]
                link(v, nc.vector.tensor_scalar(bias_part, bias[:], s_qkvw, None, ALU.mult))
                link(v, nc.vector.tensor_scalar(bias[:], bias[:], part_row[:, 0:1], None, ALU.mult))
                rows = nc.vector.scalar_tensor_tensor(bias_rows[:, i, :], bias_part[0:2, :], part_row[0:2, 1:2],
                                                      bias[0:2, :], ALU.mult, ALU.add)
                if i:
                    rows.then_inc(w_att_ready, 1)
                else:
                    link(v, rows)
            assert chain[0] == LINKS + LINKS_BEFORE[j + 1], (j, chain[0])

        small = ((ident[:], d["c_ident"]), (gate_sb[:], d["gate_w"]), (pick32, d["c_pick"]), (rank[:], d["c_rank"]),
                 (gbias[:], d["gbias"].partition_broadcast(P)))
        tables = ((bk_row[:], d["bk"].partition_broadcast(P)), (bv_row[:], d["bv"].partition_broadcast(P)),
                  (bo_row[:], d["bo"].partition_broadcast(P)), (bq_sb[:], d["bq2"]), (bkT_sb[:], d["bkT"]),
                  (trig_rows[:], d["c_trig_rows"]), (trig_cols[:].rearrange("p g t -> p (g t)"), d["c_trig_cols"]),
                  (decay[:], d["c_decay"]))
        TABLES = len(tables)

        @block.sync
        def _(sp):
            x = d["x"].rearrange("(t p) d -> p t d", p=P)
            for half in range(2):
                tiles = slice(half * HALF, (half + 1) * HALF)
                sp.dma_start(x_tok[:, tiles, :], x[:, tiles, :]).then_inc(in_x[half], 16)
            sp.dma_start(arena_a[:], d["w_up"]).then_inc(in_up, 16)
            sp.dma_start(arena_b[:], d["w_down"]).then_inc(in_dn, 16)
            for dst, src in tables:
                sp.dma_start(dst, src).then_inc(in_tab, 16)
            sp.wait_ge(w_up_ready, 1)
            for j, name in enumerate(("wq", "wk", "wv", "wo")):
                sp.dma_start(arena_a[:, j * HD:(j + 1) * HD], d[name]).then_inc(in_att, 16)
            with sp.Fori(0, NBLK) as n:
                sp.wait_ge(ffn[1]["fin_x"], n + 1)
                rows = d["out"].rearrange("(t p) d -> p t d", p=P)
                sp.dma_start(rows[:, bass.ds(n * TPB, TPB), :], x_tok[:, bass.ds(n * TPB, TPB), :]).then_inc(out_done, 16)
            sp.wait_ge(out_done, 16 * NBLK)

        @block.scalar
        def _(act):
            for dst, src in small:
                act.dma_start(dst, src).then_inc(in_const, 16)
            give(act, ln_hi, *(S["wb_copied"] for S in ffn))
            first_copy(act)
            expert_weights_high(act)
            gating_exp(act, 0)
            ffn_act(act, 0)
            attention_act(act)
            ffn_act(act, 1)

        @block.gpsimd
        def _(g):
            give(g, a["s_lo_done"], a["o_lo_done"], *(S["acc_done"] for S in ffn))
            nc.gpsimd.memset(minus_half[:], -0.5)
            nc.gpsimd.memset(bias_one[:], BIAS_ONE)
            nc.gpsimd.memset(pick[:], 0.0)
            nc.gpsimd.memset(sw3[:], 0.0).then_inc(zeroed, 1)
            g.wait_ge(zeroed, 1)
            first_ln_power(g, 0)
            first_ln_power(g, 1)
            reduce_largest(g, 0, 1, 0)
            first_low(g)
            reduce_largest(g, 1, 2, 1)
            ffn_pool(g, 0)
            attention_pool(g)
            ffn_pool(g, 1)

        @block.vector
        def _(v):
            give(v, ln_lo, *(S["y_used"] for S in ffn * 2), a["s_ready"], a["o32_done"], a["att_sum"])
            first_ln_stats(v, 0)
            first_ln_stats(v, 1)
            first_ln_apply(v, 0)
            first_ln_apply(v, 1)
            v.wait_ge(in_up, 16)
            largest_of(v, 0, arena_a[:], last=True)
            scale_up(v)
            v.wait_ge(in_dn, 16)
            largest_of(v, 1, arena_b[:], last=True)
            v.wait_ge(in_const, 16 * len(small))
            v.wait_ge(zeroed, 1)
            nc.vector.tensor_copy(ident_h[:], ident[:])
            nc.vector.tensor_copy(ident_b[:], ident[:])
            nc.vector.tensor_copy(pick[0:SPLIT3 * E].rearrange("p e q -> p (e q)"), pick32).then_inc(const_ready, 1)
            first_logits(v)
            scale_down(v)
            expert_weights_low(v, W_UP)
            for j in range(GATE_PIECES):
                gating(v, 0, j)
            expert_weights_low(v, W_DOWN)
            assert chain[0] == LINKS
            ffn_dve(v, 0)
            attention_dve(v)
            ffn_dve(v, 1)

        @block.tensor
        def _(pe):
            give(pe, *(S["acc_tr"] for S in ffn))
            first_transpose(pe)
            pe.wait_ge(const_ready, 1)
            pe.wait_ge(gate_read, NBLK)
            ffn_pe(pe, 0)
            attention_pe(pe)
            ffn_pe(pe, 1)


_ORDER = ("x", "wq", "wk", "wv", "wo", "bq2", "bkT", "bk", "bv", "bo", "gate_w", "gbias", "w_up", "w_down")


def kernel(L0_attn_x, L0_attn_Wq, L0_attn_bq, L0_attn_Wk, L0_attn_bk, L0_attn_Wv, L0_attn_bv, L0_attn_Wo, L0_attn_bo,
           L0_ffn_gate_w, L0_ffn_expert_bias, L0_ffn_w_up, L0_ffn_w_down):
    import concourse.bacc as bacc
    from concourse.bass_utils import run_bass_kernel_spmd

    bq = np.asarray(L0_attn_bq).reshape(H, DH).T
    arrays = {
        "x": np.asarray(L0_attn_x).reshape(NTOK, D),
        "wq": L0_attn_Wq, "wk": L0_attn_Wk, "wv": L0_attn_Wv,
        "wo": np.asarray(L0_attn_Wo).reshape(NHP, P, D).transpose(1, 0, 2).reshape(P, NHP * D),
        "bq2": np.concatenate([bq, bq], 0),
        "bkT": np.asarray(L0_attn_bk).reshape(NHP, P).T,
        "bk": L0_attn_bk, "bv": L0_attn_bv, "bo": L0_attn_bo,
        "gate_w": np.asarray(L0_ffn_gate_w).T,
        "gbias": L0_ffn_expert_bias,
        "w_up": np.asarray(L0_ffn_w_up).transpose(2, 0, 1).reshape(D, E * I),
        "w_down": np.asarray(L0_ffn_w_down).reshape(E, D, CH, P).transpose(3, 0, 2, 1).reshape(P, E * CH * D),
        **constants(),
    }
    arrays["c_trig_cols"] = arrays["c_trig_cols"].reshape(P, 4 * T // P)
    arrays = {n: np.ascontiguousarray(v) for n, v in arrays.items()}
    nc = bacc.Bacc("TRN2", target_bir_lowering=False, num_devices=1)
    d = {n: nc.dram_tensor(f"in_{n}", v.shape, mybir.dt.from_np(v.dtype), kind="ExternalInput").ap()
         for n, v in arrays.items()}
    d["out"] = nc.dram_tensor("out_x", (NTOK, D), F32, kind="ExternalOutput").ap()
    build(nc, d)
    r = run_bass_kernel_spmd(nc, [{f"in_{n}": v for n, v in arrays.items()}], core_ids=[0])
    return r.results[0]["out_x"].reshape(B, T, D)
```
